# Optimizing a Trainium2 kernel written in Bass

```python
import numpy as np
import jax
import jax.numpy as jnp

def _softmax(x, axis=-1):
    return jax.nn.softmax(x, axis=axis)

def _gelu(x):
    return jax.nn.gelu(x, approximate=True)

def _silu(x):
    return jax.nn.silu(x)

def _sigmoid(x):
    return jax.nn.sigmoid(x)

def _layernorm(x, axis=-1, eps=1e-05):
    m = jnp.mean(x, axis=axis, keepdims=True)
    v = jnp.var(x, axis=axis, keepdims=True)
    return (x - m) / jnp.sqrt(v + eps)

def _scatter_add(tgt, idx, src, axis=0):
    return tgt.at[idx].add(src)

def _segment_sum(src, seg, n):
    return jax.ops.segment_sum(src, seg, n)
kernel_name = 'mk_gnn_ffn_d1_gnn_r8_7acff1'

def setup_inputs(seed: int=0):
    np.random.seed(seed)
    _w = jnp.asarray

    def _rec_inputs():
        import jax
        import jax.numpy as jnp
        _gk = jax.random.key(seed)
        x = -0.0002949 + 1 * jax.random.normal(jax.random.fold_in(_gk, 1), (1250, 512), jnp.float32)
        src = jax.random.randint(jax.random.fold_in(_gk, 2), (20000,), 0, 1250, jnp.int32)
        dst = jnp.minimum((1250 * jax.random.uniform(jax.random.fold_in(_gk, 3), (20000,)) ** 2.0).astype(jnp.int32), 9999)
        _o = jnp.argsort(dst, stable=True)
        src = src[_o]
        dst = dst[_o]
        node_vec1 = jax.random.uniform(jax.random.fold_in(_gk, 12), (1250, 1), jnp.float32, 0.0, 0.999957)
        return (x, src, dst, node_vec1)
    x, src, dst, node_vec1 = _rec_inputs()

    def _L0_gnn_setup():
        import jax, jax.numpy as jnp
        import numpy as np
        N_NODES = 40962
        LATENT_DIM = 512
        N_EDGES = 81924
        NUM_BLOCKS = 4
        NUM_HEADS = 4
        NUM_FREQ = 32
        BASE_PERIOD = 16
        NOISE_EMB_DIM = 16
        EPS = 1e-05

        def _cond_layer_norm(x, cond, sw, sb, bw, bb):
            mu = jnp.mean(x, axis=-1, keepdims=True)
            var = jnp.var(x, axis=-1, keepdims=True)
            xn = (x - mu) * jax.lax.rsqrt(var + EPS)
            scale = cond @ sw + sb
            bias = cond @ bw + bb
            return xn * (1.0 + scale) + bias

        def _sparse_attention(x, src, dst, wq, bq, wk, bk, wv, bv, wo, bo):
            N, D = x.shape
            H, Dh = (NUM_HEADS, D // NUM_HEADS)
            q = (x @ wq + bq).reshape(N, H, Dh) * Dh ** (-0.5)
            k = (x @ wk + bk).reshape(N, H, Dh)
            v = (x @ wv + bv).reshape(N, H, Dh)
            scores = jnp.einsum('ehd,ehd->eh', q[src], k[dst])
            smax = jax.ops.segment_max(scores, src, num_segments=N)
            ex = jnp.exp(scores - smax[src])
            denom = jax.ops.segment_sum(ex, src, num_segments=N)
            attn = ex / denom[src]
            out = jax.ops.segment_sum(attn[:, :, None] * v[dst], src, num_segments=N)
            return out.reshape(N, D) @ wo + bo

        def _forward(x, edge_index, noise_levels, f_w1, f_b1, f_w2, f_b2, s1_w, s1_b, b1_w, b1_b, wq, bq, wk, bk, wv, bv, wo, bo, s2_w, s2_b, b2_w, b2_b, m_w1, m_b1, m_w2, m_b2):
            src, dst = (edge_index[0], edge_index[1])
            freqs = jnp.arange(1, NUM_FREQ + 1, dtype=x.dtype) * (2.0 * np.pi / BASE_PERIOD)
            ph = noise_levels * freqs
            emb = jnp.concatenate([jnp.sin(ph), jnp.cos(ph)], axis=-1)
            cond = jax.nn.silu(emb @ f_w1 + f_b1) @ f_w2 + f_b2
            for i in range(NUM_BLOCKS):
                y = _cond_layer_norm(x, cond, s1_w[i], s1_b[i], b1_w[i], b1_b[i])
                y = _sparse_attention(y, src, dst, wq[i], bq[i], wk[i], bk[i], wv[i], bv[i], wo[i], bo[i])
                x = x + y
                y = _cond_layer_norm(x, cond, s2_w[i], s2_b[i], b2_w[i], b2_b[i])
                y = jax.nn.relu(y @ m_w1[i] + m_b1[i]) @ m_w2[i] + m_b2[i]
                x = x + y
            return x
        key = jax.random.key(seed)
        ks = jax.random.split(key, 20)

        def w(k, shape, s=0.02):
            return jax.random.normal(k, shape, dtype=jnp.float32) * s
        D, B, C = (LATENT_DIM, NUM_BLOCKS, NOISE_EMB_DIM)
        z = lambda *s: jnp.zeros(s, jnp.float32)
        return {'latent_mesh_nodes': jax.random.normal(ks[0], (N_NODES, D), dtype=jnp.float32), 'edge_index': jax.random.randint(ks[1], (2, N_EDGES), 0, N_NODES, dtype=jnp.int32), 'noise_levels': jax.random.uniform(ks[2], (N_NODES, 1), dtype=jnp.float32), 'f_w1': w(ks[3], (2 * NUM_FREQ, C)), 'f_b1': z(C), 'f_w2': w(ks[4], (C, C)), 'f_b2': z(C), 's1_w': w(ks[5], (B, C, D)), 's1_b': z(B, D), 'b1_w': w(ks[6], (B, C, D)), 'b1_b': z(B, D), 'wq': w(ks[7], (B, D, D)), 'bq': z(B, D), 'wk': w(ks[8], (B, D, D)), 'bk': z(B, D), 'wv': w(ks[9], (B, D, D)), 'bv': z(B, D), 'wo': w(ks[10], (B, D, D)), 'bo': z(B, D), 's2_w': w(ks[11], (B, C, D)), 's2_b': z(B, D), 'b2_w': w(ks[12], (B, C, D)), 'b2_b': z(B, D), 'm_w1': w(ks[13], (B, D, D)), 'm_b1': z(B, D), 'm_w2': w(ks[14], (B, D, D)), 'm_b2': z(B, D)}
    _L0_gnn_all = _L0_gnn_setup()
    _L0_gnn_in = {k: v for k, v in _L0_gnn_all.items() if k in ('f_w1', 'f_b1', 'f_w2', 'f_b2', 's1_w', 's1_b', 'b1_w', 'b1_b', 'wq', 'bq', 'wk', 'bk', 'wv', 'bv', 'wo', 'bo', 's2_w', 's2_b', 'b2_w', 'b2_b', 'm_w1', 'm_b1', 'm_w2', 'm_b2')}
    del _L0_gnn_all

    def _L0_ffn_setup():
        import jax, jax.numpy as jnp
        import numpy as np
        TOP_K = 2

        def quick_gelu(x):
            return x * jax.nn.sigmoid(1.702 * x)
        key = jax.random.key(seed)
        ks = jax.random.split(key, 6)
        B, S, H, I, E = (8, 512, 512, 1024, 8)
        s_h = 1.0 / np.sqrt(H).astype(np.float32)
        s_i = 1.0 / np.sqrt(I).astype(np.float32)
        return {'hidden_states': jax.random.normal(ks[0], (B, S, H), jnp.float32), 'router_w': jax.random.normal(ks[1], (H, E), jnp.float32) * s_h, 'router_b': jnp.zeros((E,), jnp.float32), 'gate_up_proj': jax.random.normal(ks[2], (E, H, 2 * I), jnp.float32) * s_h, 'gate_up_proj_bias': jnp.zeros((E, 2 * I), jnp.float32), 'down_proj': jax.random.normal(ks[3], (E, I, H), jnp.float32) * s_i, 'down_proj_bias': jnp.zeros((E, H), jnp.float32)}
    _L0_ffn_all = _L0_ffn_setup()
    _L0_ffn_in = {k: v for k, v in _L0_ffn_all.items() if k in ('router_w', 'router_b', 'gate_up_proj', 'gate_up_proj_bias', 'down_proj', 'down_proj_bias')}
    del _L0_ffn_all
    return {'x': x, 'src': src, 'dst': dst, 'node_vec1': node_vec1, 'L0_gnn_f_w1': _L0_gnn_in['f_w1'], 'L0_gnn_f_b1': _L0_gnn_in['f_b1'], 'L0_gnn_f_w2': _L0_gnn_in['f_w2'], 'L0_gnn_f_b2': _L0_gnn_in['f_b2'], 'L0_gnn_s1_w': _L0_gnn_in['s1_w'], 'L0_gnn_s1_b': _L0_gnn_in['s1_b'], 'L0_gnn_b1_w': _L0_gnn_in['b1_w'], 'L0_gnn_b1_b': _L0_gnn_in['b1_b'], 'L0_gnn_wq': _L0_gnn_in['wq'], 'L0_gnn_bq': _L0_gnn_in['bq'], 'L0_gnn_wk': _L0_gnn_in['wk'], 'L0_gnn_bk': _L0_gnn_in['bk'], 'L0_gnn_wv': _L0_gnn_in['wv'], 'L0_gnn_bv': _L0_gnn_in['bv'], 'L0_gnn_wo': _L0_gnn_in['wo'], 'L0_gnn_bo': _L0_gnn_in['bo'], 'L0_gnn_s2_w': _L0_gnn_in['s2_w'], 'L0_gnn_s2_b': _L0_gnn_in['s2_b'], 'L0_gnn_b2_w': _L0_gnn_in['b2_w'], 'L0_gnn_b2_b': _L0_gnn_in['b2_b'], 'L0_gnn_m_w1': _L0_gnn_in['m_w1'], 'L0_gnn_m_b1': _L0_gnn_in['m_b1'], 'L0_gnn_m_w2': _L0_gnn_in['m_w2'], 'L0_gnn_m_b2': _L0_gnn_in['m_b2'], 'L0_ffn_router_w': _L0_ffn_in['router_w'], 'L0_ffn_router_b': _L0_ffn_in['router_b'], 'L0_ffn_gate_up_proj': _L0_ffn_in['gate_up_proj'], 'L0_ffn_gate_up_proj_bias': _L0_ffn_in['gate_up_proj_bias'], 'L0_ffn_down_proj': _L0_ffn_in['down_proj'], 'L0_ffn_down_proj_bias': _L0_ffn_in['down_proj_bias']}

def reference(x, src, dst, node_vec1, L0_gnn_f_w1, L0_gnn_f_b1, L0_gnn_f_w2, L0_gnn_f_b2, L0_gnn_s1_w, L0_gnn_s1_b, L0_gnn_b1_w, L0_gnn_b1_b, L0_gnn_wq, L0_gnn_bq, L0_gnn_wk, L0_gnn_bk, L0_gnn_wv, L0_gnn_bv, L0_gnn_wo, L0_gnn_bo, L0_gnn_s2_w, L0_gnn_s2_b, L0_gnn_b2_w, L0_gnn_b2_b, L0_gnn_m_w1, L0_gnn_m_b1, L0_gnn_m_w2, L0_gnn_m_b2, L0_ffn_router_w, L0_ffn_router_b, L0_ffn_gate_up_proj, L0_ffn_gate_up_proj_bias, L0_ffn_down_proj, L0_ffn_down_proj_bias):
    import jax
    import jax.numpy as jnp

    def _L0_gnn_ref(latent_mesh_nodes, edge_index, noise_levels, f_w1, f_b1, f_w2, f_b2, s1_w, s1_b, b1_w, b1_b, wq, bq, wk, bk, wv, bv, wo, bo, s2_w, s2_b, b2_w, b2_b, m_w1, m_b1, m_w2, m_b2):
        import jax, jax.numpy as jnp
        import numpy as np
        N_NODES = 40962
        LATENT_DIM = 512
        N_EDGES = 81924
        NUM_BLOCKS = 4
        NUM_HEADS = 4
        NUM_FREQ = 32
        BASE_PERIOD = 16
        NOISE_EMB_DIM = 16
        EPS = 1e-05

        def _cond_layer_norm(x, cond, sw, sb, bw, bb):
            mu = jnp.mean(x, axis=-1, keepdims=True)
            var = jnp.var(x, axis=-1, keepdims=True)
            xn = (x - mu) * jax.lax.rsqrt(var + EPS)
            scale = cond @ sw + sb
            bias = cond @ bw + bb
            return xn * (1.0 + scale) + bias

        def _sparse_attention(x, src, dst, wq, bq, wk, bk, wv, bv, wo, bo):
            N, D = x.shape
            H, Dh = (NUM_HEADS, D // NUM_HEADS)
            q = (x @ wq + bq).reshape(N, H, Dh) * Dh ** (-0.5)
            k = (x @ wk + bk).reshape(N, H, Dh)
            v = (x @ wv + bv).reshape(N, H, Dh)
            scores = jnp.einsum('ehd,ehd->eh', q[src], k[dst])
            smax = jax.ops.segment_max(scores, src, num_segments=N)
            ex = jnp.exp(scores - smax[src])
            denom = jax.ops.segment_sum(ex, src, num_segments=N)
            attn = ex / denom[src]
            out = jax.ops.segment_sum(attn[:, :, None] * v[dst], src, num_segments=N)
            return out.reshape(N, D) @ wo + bo

        def _forward(x, edge_index, noise_levels, f_w1, f_b1, f_w2, f_b2, s1_w, s1_b, b1_w, b1_b, wq, bq, wk, bk, wv, bv, wo, bo, s2_w, s2_b, b2_w, b2_b, m_w1, m_b1, m_w2, m_b2):
            src, dst = (edge_index[0], edge_index[1])
            freqs = jnp.arange(1, NUM_FREQ + 1, dtype=x.dtype) * (2.0 * np.pi / BASE_PERIOD)
            ph = noise_levels * freqs
            emb = jnp.concatenate([jnp.sin(ph), jnp.cos(ph)], axis=-1)
            cond = jax.nn.silu(emb @ f_w1 + f_b1) @ f_w2 + f_b2
            for i in range(NUM_BLOCKS):
                y = _cond_layer_norm(x, cond, s1_w[i], s1_b[i], b1_w[i], b1_b[i])
                y = _sparse_attention(y, src, dst, wq[i], bq[i], wk[i], bk[i], wv[i], bv[i], wo[i], bo[i])
                x = x + y
                y = _cond_layer_norm(x, cond, s2_w[i], s2_b[i], b2_w[i], b2_b[i])
                y = jax.nn.relu(y @ m_w1[i] + m_b1[i]) @ m_w2[i] + m_b2[i]
                x = x + y
            return x
        return _forward(latent_mesh_nodes, edge_index, noise_levels, f_w1, f_b1, f_w2, f_b2, s1_w, s1_b, b1_w, b1_b, wq, bq, wk, bk, wv, bv, wo, bo, s2_w, s2_b, b2_w, b2_b, m_w1, m_b1, m_w2, m_b2)

    def _L0_ffn_ref(hidden_states, router_w, router_b, gate_up_proj, gate_up_proj_bias, down_proj, down_proj_bias):
        import jax, jax.numpy as jnp
        import numpy as np
        TOP_K = 2

        def quick_gelu(x):
            return x * jax.nn.sigmoid(1.702 * x)
        B, S, H = hidden_states.shape
        E = router_b.shape[0]
        x = hidden_states.reshape(-1, H)
        T = x.shape[0]
        logits = x @ router_w + router_b
        top_w, sel = jax.lax.top_k(logits, TOP_K)
        top_w = jax.nn.softmax(top_w, axis=-1)
        tok_w = jnp.zeros((T, E), x.dtype).at[jnp.arange(T)[:, None], sel].add(top_w)

        def body(acc, params):
            Wgu, bgu, Wd, bd, w_e = params
            gu = x @ Wgu + bgu
            gate, up = jnp.split(gu, 2, axis=-1)
            act = (up + 1.0) * quick_gelu(gate)
            out = act @ Wd + bd
            return (acc + out * w_e[:, None], None)
        acc0 = jnp.zeros((T, H), x.dtype)
        acc, _ = jax.lax.scan(body, acc0, (gate_up_proj, gate_up_proj_bias, down_proj, down_proj_bias, tok_w.T))
        return acc.reshape(B, S, H)
    edge_index = jnp.stack([src, dst])
    x = x + _L0_gnn_ref(_layernorm(x, axis=-1), edge_index, node_vec1, L0_gnn_f_w1, L0_gnn_f_b1, L0_gnn_f_w2, L0_gnn_f_b2, L0_gnn_s1_w, L0_gnn_s1_b, L0_gnn_b1_w, L0_gnn_b1_b, L0_gnn_wq, L0_gnn_bq, L0_gnn_wk, L0_gnn_bk, L0_gnn_wv, L0_gnn_bv, L0_gnn_wo, L0_gnn_bo, L0_gnn_s2_w, L0_gnn_s2_b, L0_gnn_b2_w, L0_gnn_b2_b, L0_gnn_m_w1, L0_gnn_m_b1, L0_gnn_m_w2, L0_gnn_m_b2)
    x = x + _L0_ffn_ref(_layernorm(x, axis=-1)[None], L0_ffn_router_w, L0_ffn_router_b, L0_ffn_gate_up_proj, L0_ffn_gate_up_proj_bias, L0_ffn_down_proj, L0_ffn_down_proj_bias)[0]
    return x

_drawn_inputs = setup_inputs


def setup_inputs(seed=0):
    import zlib

    import numpy as np

    out = dict(_drawn_inputs(seed))
    spreads = {'L0_gnn_f_b1': (0.0, 0.8),
     'L0_gnn_f_b2': (0.0, 0.8),
     'L0_gnn_s1_b': (0.0, 0.404),
     'L0_gnn_b1_b': (0.0, 0.1),
     'L0_gnn_bq': (0.0, 0.8),
     'L0_gnn_bk': (0.0, 0.8),
     'L0_gnn_bv': (0.0, 0.1),
     'L0_gnn_bo': (0.0, 0.1),
     'L0_gnn_s2_b': (0.0, 0.1),
     'L0_gnn_b2_b': (0.0, 0.315),
     'L0_gnn_m_b1': (0.0, 0.1),
     'L0_gnn_m_b2': (0.0, 0.1),
     'L0_ffn_router_b': (0.0, 0.1),
     'L0_ffn_gate_up_proj_bias': (0.0, 0.1),
     'L0_ffn_down_proj_bias': (0.0, 0.1)}
    factors = {'node_vec1': 8.0,
     'L0_gnn_f_w1': 8.0,
     'L0_gnn_f_w2': 8.0,
     'L0_gnn_s1_w': 8.0,
     'L0_gnn_b1_w': 8.0,
     'L0_gnn_s2_w': 8.0,
     'L0_gnn_b2_w': 6.616}
    for name, (base, spread) in spreads.items():
        noise = np.random.default_rng([zlib.crc32(name.encode()), seed]).standard_normal(out[name].shape)
        drawn = base * np.exp(spread * noise) if base else spread * noise
        out[name] = jnp.asarray(drawn.astype(out[name].dtype))
    for name, factor in factors.items():
        out[name] = (out[name] * factor).astype(out[name].dtype)
    return out
```

```python
from contextlib import ExitStack

import numpy as np

import concourse.bass as bass
from concourse import mybir

F32 = mybir.dt.float32
F16 = mybir.dt.float16
I32 = mybir.dt.int32
ALU = mybir.AluOpType
ACT = mybir.ActivationFunctionType
AX = mybir.AxisListType

P = 128
NODES = 1250
D = 512
EDGES = 20000
LAYERS = 4
HEADS = 4
DH = D // HEADS
FREQS = 32
BASE_PERIOD = 16
COND = 16
EXPERTS = 8
FF = 1024
TOP_K = 2
EPS = 1e-5

TILES = -(-NODES // P)
PAD = TILES * P
LAST = NODES - (TILES - 1) * P
KT = D // P
CHUNKS = [(c, min(512, NODES - c)) for c in range(0, NODES, 512)]
NCH = len(CHUNKS)
W_SCALE = 64.0
BACK = 1.0 / (W_SCALE * W_SCALE)
SCORE = DH ** -0.5 * BACK
MASKED = -1e30
MAX_SHIFT = 1e20
LEAST_SUM = 1e-20

EP = 125
ECOLS = EDGES // EP
HALF = PAD // 2
FIELD = 4096
GROUP = 32
assert GROUP * EP < FIELD and ECOLS % GROUP == 0
NGROUPS = ECOLS // GROUP
BLK = 8
BLKS = GROUP // BLK
SWEEPS = TILES // 2

NROWS = 96
MATS = 4
PASSES = ((0, 0), (0, 1), (1, 0))


def hold(eng, sem, value, passed):
    eng.wait_ge(sem, value)
    eng.sem_inc(passed, 1)


def split_matmuls(pe, out, stationary, moving, n_k):
    for k in range(n_k):
        for i, (a, b) in enumerate(PASSES):
            ins = pe.matmul(out, stationary(a, k), moving(b, k), start=k == 0 and i == 0,
                            stop=k == n_k - 1 and i == len(PASSES) - 1)
    return ins


def build(nc, io):
    with ExitStack() as whole:
        def sb(name, shape, dt=F32):
            return whole.enter_context(nc.sbuf_tensor(name, shape, dt))

        g = sb("g", [P, TILES, D])
        ident = sb("ident", [P, P])
        bias_cols = sb("bias_cols", [P, 3 * LAYERS * KT])
        gu_cols = sb("gu_cols", [P, 3, EXPERTS * 2 * FF // P])
        with ExitStack() as gnn:
            def gsb(name, shape, dt=F32):
                return gnn.enter_context(nc.sbuf_tensor(name, shape, dt))
            log_count = gsb("log_count", [P, TILES, NODES])
            cond_stack = gsb("cond_stack", [NROWS, PAD], F16)
            norm_stack = gsb("norm_stack", [NROWS, LAYERS * MATS, D], F16)
            prepare(nc, io, g, ident, bias_cols, gu_cols, log_count, cond_stack, norm_stack)
            attention_layers(nc, io, g, ident, bias_cols, log_count, cond_stack, norm_stack)
        experts(nc, io, g, ident, gu_cols)


def prepare(nc, io, g, ident, bias_cols, gu_cols, log_count, cond_stack, norm_stack):
    with ExitStack() as ctx:
        def sb(name, shape, dt=F32):
            return ctx.enter_context(nc.sbuf_tensor(name, shape, dt))

        def sem(name):
            return ctx.enter_context(nc.semaphore(name))

        bank = [ctx.enter_context(nc.psum_tensor(f"pre_bank{i}", [P, 512], F32)) for i in range(8)]
        norm_raw = sb("norm_raw", [NROWS, LAYERS * MATS, D])
        edges = sb("edges", [EP, 2, ECOLS], I32)
        src_rel = sb("src_rel", [EP, ECOLS])
        dst_low = sb("dst_low", [EP, ECOLS])
        dst_weight = sb("dst_weight", [EP, ECOLS])
        columns = sb("columns", [P, HALF], F16)
        src_hot = sb("src_hot", [EP, BLK, 2 * P], F16)
        dst_hot = sb("dst_hot", [EP, BLK, HALF], F16)
        packed = sb("packed", [P, 2, HALF], I32)
        high = sb("high", [P, 2, HALF], I32)
        at_least_1 = sb("at_least_1", [P, 2, NODES])
        logs = sb("logs", [P, 2, NODES])
        noise = sb("noise", [2 * FREQS, NODES])
        turns = sb("turns", [2 * FREQS, NODES])
        freq_row = sb("freq_row", [2 * FREQS, 1], I32)
        freq = sb("freq", [2 * FREQS, 4])
        f1 = sb("f1", [2 * FREQS, COND])
        f1b = sb("f1b", [COND, 1])
        f2 = sb("f2", [COND, NROWS])
        f2b = sb("f2b", [NROWS, 1])
        sig = sb("sig", [COND, NODES])
        hidden = sb("hidden", [COND, NODES])
        stats = sb("stats", [P, TILES, 6])
        mv = sb("mv", [P, TILES, 2])
        rstd = sb("rstd", [P, TILES])
        minus_half = sb("minus_half", [P, TILES])
        bias_rows = sb("bias_rows", [3 * LAYERS * KT, P])
        gu_rows = sb("gu_rows", [P, P])
        counts = log_count[:].bitcast(I32)

        edges_in = sem("edges_in")
        x_in = sem("x_in")
        noise_in = sem("noise_in")
        small_in = sem("small_in")
        norm_in = sem("norm_in")
        zeroed = sem("zeroed")
        const_ready = sem("const_ready")
        edge_step = sem("edge_step")
        hot_ready = sem("hot_ready")
        hot_free = sem("hot_free")
        counted = sem("counted")
        count_free = sem("count_free")
        unpacked = sem("unpacked")
        unpack_step = sem("unpack_step")
        added = sem("added")
        adding = sem("adding")
        clamped = sem("clamped")
        logged = sem("logged")
        table_step = sem("table_step")
        cond_step = sem("cond_step")
        cond_act = sem("cond_act")
        cond_mm = sem("cond_mm")
        norm_step = sem("norm_step")
        norm_split = sem("norm_split")
        x_step = sem("x_step")
        rstd_ready = sem("rstd_ready")
        turned = sem("turned")

        block = ctx.enter_context(nc.Block())

        @block.sync
        def _(sp):
            sp.dma_start(edges[:, 0, :], io["src"].rearrange("(p j) -> p j", p=EP)).then_inc(edges_in, 16)
            sp.dma_start(edges[:, 1, :], io["dst"].rearrange("(p j) -> p j", p=EP)).then_inc(edges_in, 16)
            sp.dma_start(noise[:], io["node_vec1"].rearrange("n a -> a n").partition_broadcast(2 * FREQS)
                         .rearrange("p a n -> p (a n)")).then_inc(noise_in, 16)
            sp.dma_start(f1[:], io["L0_gnn_f_w1"]).then_inc(noise_in, 16)
            sp.dma_start(f1b[:], io["L0_gnn_f_b1"].rearrange("(c a) -> c a", a=1)).then_inc(noise_in, 16)
            sp.wait_ge(zeroed, 7)
            for r in range(3):
                sp.dma_start(f2[:, 32 * r + 1:32 * r + 1 + COND], io["L0_gnn_f_w2"]).then_inc(noise_in, 16)
                sp.dma_start(f2b[32 * r + 1:32 * r + 1 + COND, :],
                             io["L0_gnn_f_b2"].rearrange("(c a) -> c a", a=1)).then_inc(noise_in, 16)
            sp.dma_start(g[:, 0:TILES - 1, :], io["x"][0:(TILES - 1) * P, :].rearrange("(t p) d -> p t d", p=P)
                         ).then_inc(x_in, 16)
            sp.dma_start(g[0:LAST, TILES - 1, :], io["x"][(TILES - 1) * P:NODES, :]).then_inc(x_in, 16)
            for n, name in enumerate(("bq", "bk", "m_b1")):
                sp.dma_start(bias_rows[16 * n:16 * n + 16, :],
                             io["L0_gnn_" + name].rearrange("l (t f) -> (l t) f", f=P)).then_inc(small_in, 16)
            sp.dma_start(gu_rows[:], io["L0_ffn_gate_up_proj_bias"].rearrange("e (t f) -> (e t) f", f=P)
                         ).then_inc(small_in, 16)
            raw = norm_raw[:].rearrange("c (l m) d -> c l m d", m=MATS)
            for m, name in enumerate(("s1", "b1", "s2", "b2")):
                for r in range(3):
                    sp.dma_start(raw[32 * r + 1:32 * r + 1 + COND, :, m, :],
                                 io[f"L0_gnn_{name}_w"].rearrange("l c d -> c l d")).then_inc(norm_in, 16)
                    sp.dma_start(raw[32 * r:32 * r + 1, :, m, :],
                                 io[f"L0_gnn_{name}_b"].rearrange("(a l) d -> a l d", a=1)).then_inc(norm_in, 16)

        @block.gpsimd
        def _(pool):
            pool.memset(f2[:], 0.0).then_inc(zeroed, 1)
            pool.memset(g[96:P, TILES - 1, :], 0.0).then_inc(zeroed, 1)
            pool.memset(f2b[:], 0.0).then_inc(zeroed, 1)
            pool.memset(norm_raw[:], 0.0).then_inc(zeroed, 1)
            pool.wait_ge(zeroed, 4)
            for r in range(3):
                pool.memset(f2b[32 * r:32 * r + 1, :], 1.0).then_inc(zeroed, 1)
            pool.wait_ge(zeroed, 7)
            pool.iota(columns[:], [[1, HALF]], base=0, channel_multiplier=0,
                      allow_small_or_imprecise_dtypes=True).then_inc(const_ready, 1)
            pool.iota(freq_row[:], [[1, 1]], base=1, channel_multiplier=1).then_inc(const_ready, 1)
            pool.memset(ident[:], 0.0).then_inc(const_ready, 1)
            pool.memset(minus_half[:], -0.5).then_inc(const_ready, 1)
            pool.wait_ge(const_ready, 4)
            pool.affine_select(out=ident[:], in_=ident[:], compare_op=ALU.not_equal, fill=1.0, base=0,
                               pattern=[[-1, P]], channel_multiplier=1).then_inc(const_ready, 1)
            pool.wait_ge(x_step, 2)
            pool.tensor_scalar(rstd[:], mv[:, :, 1], EPS, None, ALU.add).then_inc(rstd_ready, 1)
            pool.wait_ge(rstd_ready, 1)
            pool.tensor_tensor(rstd[:], rstd[:], minus_half[:], ALU.pow).then_inc(rstd_ready, 1)
            with pool.Fori(0, SWEEPS) as s:
                for n in range(NGROUPS):
                    hold(pool, unpacked, s * NGROUPS + (n + 1), adding)
                    rows = counts[:, bass.ds(s * 2, 2), :]
                    pool.tensor_tensor(rows[:, :, 0:HALF], rows[:, :, 0:HALF], packed[:], ALU.add)
                    pool.tensor_tensor(rows[:, :, HALF:NODES], rows[:, :, HALF:NODES],
                                       high[:, :, 0:NODES - HALF], ALU.add).then_inc(added, 1)

        @block.vector
        def _(dve):
            dve.memset(counts, 0).then_inc(edge_step, 1)
            dve.wait_ge(edges_in, 32)
            dve.tensor_copy(src_rel[:], edges[:, 0, :]).then_inc(edge_step, 1)
            dve.tensor_copy(dst_low[:], edges[:, 1, :]).then_inc(edge_step, 1)
            dve.wait_ge(edge_step, 3)
            dve.tensor_scalar(dst_weight[:], dst_low[:], float(HALF), None, ALU.is_ge).then_inc(edge_step, 1)
            dve.wait_ge(edge_step, 4)
            dve.scalar_tensor_tensor(dst_low[:], dst_weight[:], -float(HALF), dst_low[:], ALU.mult, ALU.add
                                     ).then_inc(edge_step, 1)
            dve.wait_ge(edge_step, 5)
            dve.tensor_scalar(dst_weight[:], dst_weight[:], float(FIELD - 1), 1.0, ALU.mult, ALU.add
                              ).then_inc(edge_step, 1)
            dve.wait_ge(edge_step, 6)
            dve.wait_ge(const_ready, 5)

            step = [0]

            def chain(ins):
                step[0] += 1
                ins.then_inc(cond_step, 1)
                dve.wait_ge(cond_step, step[0])

            chain(dve.tensor_copy(freq[:, 0:1], freq_row[:]))
            chain(dve.tensor_scalar(freq[32:64, 0:1], freq[32:64, 0:1], float(FREQS), None, ALU.subtract))
            chain(dve.tensor_scalar(freq[:, 1:2], freq[:, 0:1], 2.0 * np.pi / BASE_PERIOD, None, ALU.mult))
            dve.memset(freq[:, 2:4], 0.0).then_inc(cond_step, 1)
            step[0] += 1
            dve.wait_ge(cond_step, step[0])
            chain(dve.memset(freq[32:64, 2:3], 0.25))
            chain(dve.memset(freq[32:64, 3:4], np.pi / 2))
            dve.wait_ge(noise_in, 16 * 9)
            chain(dve.tensor_scalar(noise[:], noise[:], freq[:, 1:2], None, ALU.mult))
            chain(dve.tensor_scalar(turns[:], noise[:], 1.0 / (2 * np.pi), freq[:, 2:3], ALU.mult, ALU.add))
            magic = 1.5 * 2.0 ** 23
            chain(dve.tensor_scalar(turns[:], turns[:], magic, None, ALU.add))
            chain(dve.tensor_scalar(turns[:], turns[:], magic, None, ALU.subtract))
            first = 6.28125
            chain(dve.scalar_tensor_tensor(noise[:], turns[:], -first, noise[:], ALU.mult, ALU.add))
            chain(dve.scalar_tensor_tensor(noise[:], turns[:], -(2 * np.pi - first), noise[:], ALU.mult, ALU.add))
            chain(dve.tensor_scalar(noise[:], noise[:], freq[:, 3:4], 3.1415925, ALU.add, ALU.min))
            chain(dve.tensor_scalar(noise[:], noise[:], -3.1415925, None, ALU.max))
            for c, (c0, cn) in enumerate(CHUNKS):
                dve.wait_ge(cond_act, 2 + c)
                dve.scalar_tensor_tensor(hidden[:, c0:c0 + cn], bank[c][0:COND, 0:cn], f1b[:, 0:1],
                                         sig[:, c0:c0 + cn], ALU.add, ALU.mult).then_inc(cond_step, 1)
            step[0] += NCH
            cond_hidden = step[0]
            assert cond_hidden == COND_HIDDEN
            chain(dve.memset(cond_stack[:, NODES:PAD], 0.0))
            for c, (c0, cn) in enumerate(CHUNKS):
                dve.wait_ge(cond_mm, NCH + 1 + c)
                chain(dve.tensor_scalar(cond_stack[:, c0:c0 + cn], bank[3 + c][0:NROWS, 0:cn], f2b[:, 0:1], None,
                                        ALU.add))
                chain(dve.scalar_tensor_tensor(cond_stack[32:64, c0:c0 + cn], bank[3 + c][32:64, 0:cn],
                                               f2b[32:64, 0:1], cond_stack[32:64, c0:c0 + cn],
                                               ALU.add, ALU.subtract))
            dve.wait_ge(x_in, 32)
            for t in range(TILES):
                ins = dve.bn_stats(stats[:, t, :], g[:, t, :])
            ins.then_inc(x_step, 1)
            dve.wait_ge(x_step, 1)
            for t in range(TILES):
                ins = dve.bn_aggr(mv[:, t, :], stats[:, t, :])
            ins.then_inc(x_step, 1)
            dve.wait_ge(rstd_ready, 2)
            for t in range(TILES):
                dve.tensor_scalar(g[:, t, :], g[:, t, :], mv[:, t, 0:1], rstd[:, t:t + 1], ALU.subtract, ALU.mult)
            dve.wait_ge(turned, 2)
            nb = 3 * LAYERS * KT
            dve.tensor_scalar(bias_cols[:], bank[6][:, 0:nb], W_SCALE, None, ALU.mult)
            gu = bank[7][:, 0:P]
            dve.tensor_scalar(gu_cols[:, 0, :], gu, 1.702, None, ALU.mult)
            dve.tensor_scalar(gu_cols[:, 1, :], gu, W_SCALE, None, ALU.mult)
            dve.tensor_scalar(gu_cols[:, 2, :], gu, 1.0, W_SCALE, ALU.add, ALU.mult).then_inc(x_step, 1)
            dve.wait_ge(norm_in, 16 * 24)
            raw = norm_raw[:].rearrange("c (l m) d -> c l m d", m=MATS)
            for r in range(3):
                for m in (0, 2):
                    ins = dve.tensor_scalar(raw[32 * r:32 * r + 1, :, m, :], raw[32 * r:32 * r + 1, :, m, :],
                                            1.0, None, ALU.add)
            ins.then_inc(norm_step, 1)
            dve.wait_ge(norm_step, 1)
            dve.tensor_copy(norm_stack[:], norm_raw[:]).then_inc(norm_step, 1)
            dve.wait_ge(norm_step, 2)
            dve.tensor_tensor(norm_stack[64:96], norm_raw[64:96], norm_stack[64:96], ALU.subtract
                              ).then_inc(norm_step, 1)

            def hots(s, n, b):
                for u in range(BLK):
                    j = b * BLK + (n * GROUP + u)
                    dve.wait_ge(hot_free, s * ECOLS + (j + 1))
                    dve.tensor_scalar(src_hot[:, u, :], columns[0:EP, 0:2 * P], src_rel[:, bass.ds(j, 1)], None,
                                      ALU.is_equal)
                    dve.tensor_scalar(dst_hot[:, u, :], columns[0:EP, :], dst_low[:, bass.ds(j, 1)],
                                      dst_weight[:, bass.ds(j, 1)], ALU.is_equal, ALU.mult).then_inc(hot_ready, 1)

            def unpack(s, n):
                base = s * NGROUPS
                dve.wait_ge(counted, base + (n + 1))
                dve.wait_ge(added, base + (n + 1))
                for i in range(2):
                    for h in range(2):
                        ins = dve.tensor_copy(packed[:, i, h * (HALF // 2):(h + 1) * (HALF // 2)],
                                              bank[4 * (n % 2) + 2 * i + h][:, 0:HALF // 2])
                ins.then_inc(count_free, 1)
                dve.wait_ge(count_free, base + (n + 2))
                dve.tensor_scalar(high[:], packed[:], 12, None, ALU.arith_shift_right).then_inc(unpack_step, 1)
                dve.wait_ge(unpack_step, base + (n + 1))
                dve.tensor_scalar(packed[:], packed[:], FIELD - 1, None, ALU.bitwise_and).then_inc(unpacked, 1)

            dve.sem_inc(hot_free, BLK)
            dve.sem_inc(count_free, 1)
            dve.sem_inc(added, 1)
            with dve.Fori(0, SWEEPS) as s:
                for n in range(NGROUPS):
                    hots(s, n, 0)
                    if n:
                        unpack(s, n - 1)
                    with dve.Fori(1, BLKS) as b:
                        hots(s, n, b)
                dve.wait_ge(hot_ready, s * ECOLS + ECOLS)
                dve.tensor_scalar(src_rel[:], src_rel[:], 2.0 * P, None, ALU.subtract).then_inc(table_step, 1)
                dve.wait_ge(table_step, s + 1)
                unpack(s, NGROUPS - 1)
            dve.wait_ge(added, SWEEPS * NGROUPS + 1)
            for i in range(TILES + 1):
                if i < TILES:
                    if i >= 2:
                        dve.wait_ge(logged, i - 1)
                    dve.tensor_scalar(at_least_1[:, i % 2, :], counts[:, i, :], 1.0, None, ALU.max
                                      ).then_inc(clamped, 1)
                if i:
                    t = i - 1
                    dve.wait_ge(clamped, i)
                    dve.tensor_scalar(log_count[:, t, :], counts[:, t, :], 1.0, MASKED, ALU.is_lt, ALU.mult
                                      ).then_inc(table_step, 1)
                    dve.wait_ge(logged, i)
                    dve.wait_ge(table_step, SWEEPS + i)
                    dve.scalar_tensor_tensor(log_count[:, t, :], logs[:, t % 2, :], 1.0 / SCORE,
                                             log_count[:, t, :], ALU.mult, ALU.add)

        @block.scalar
        def _(act):
            act.wait_ge(cond_step, COND_ARGS)
            act.activation(noise[:], noise[:], ACT.Sin).then_inc(cond_act, 1)
            for c, (c0, cn) in enumerate(CHUNKS):
                act.wait_ge(cond_mm, 1 + c)
                act.activation(sig[:, c0:c0 + cn], bank[c][0:COND, 0:cn], ACT.Sigmoid, bias=f1b[:, 0:1]
                               ).then_inc(cond_act, 1)
            for t in range(TILES):
                act.wait_ge(clamped, t + 1)
                if t >= 2:
                    act.wait_ge(table_step, SWEEPS + t)
                act.activation(logs[:, t % 2, :], at_least_1[:, t % 2, :], ACT.Ln).then_inc(logged, 1)

        @block.tensor
        def _(pe):
            pe.wait_ge(const_ready, 5)
            pe.wait_ge(small_in, 64)
            nb = 3 * LAYERS * KT
            pe.transpose(bank[6][:, 0:nb], bias_rows[:], ident[0:nb, 0:nb]).then_inc(turned, 1)
            pe.transpose(bank[7][:, 0:P], gu_rows[:], ident[:]).then_inc(turned, 1)
            pe.wait_ge(noise_in, 16 * 9)
            pe.wait_ge(cond_act, 1)
            for c, (c0, cn) in enumerate(CHUNKS):
                pe.matmul(bank[c][0:COND, 0:cn], f1[:], noise[:, c0:c0 + cn], start=True, stop=True
                          ).then_inc(cond_mm, 1)
            for c, (c0, cn) in enumerate(CHUNKS):
                pe.wait_ge(cond_step, COND_HIDDEN - NCH + 1 + c)
                pe.matmul(bank[3 + c][0:NROWS, 0:cn], f2[:], hidden[:, c0:c0 + cn], start=True, stop=True
                          ).then_inc(cond_mm, 1)
            pe.wait_ge(x_step, 3)

            def count(s, n, b, first=False, last=False):
                for u in range(BLK):
                    j = b * BLK + (n * GROUP + u)
                    pe.wait_ge(hot_ready, s * ECOLS + (j + 1))
                    for i in range(2):
                        for h in range(2):
                            ins = pe.matmul(bank[4 * (n % 2) + 2 * i + h][:, 0:HALF // 2],
                                            src_hot[:, u, i * P:(i + 1) * P],
                                            dst_hot[:, u, h * (HALF // 2):(h + 1) * (HALF // 2)],
                                            start=first and u == 0, stop=last and u == BLK - 1)
                    if last and u == BLK - 1:
                        ins.then_inc(counted, 1)
                        pe.wait_ge(counted, s * NGROUPS + (n + 1))
                        pe.sem_inc(hot_free, 1)
                    else:
                        ins.then_inc(hot_free, 1)

            with pe.Fori(0, SWEEPS) as s:
                for n in range(NGROUPS):
                    pe.wait_ge(count_free, s * NGROUPS + (n + 1 if n == 0 else n))
                    count(s, n, 0, first=True)
                    with pe.Fori(1, BLKS - 1) as b:
                        count(s, n, b)
                    count(s, n, BLKS - 1, last=True)


COND_ARGS = 14
COND_HIDDEN = COND_ARGS + NCH


def attention_layers(nc, io, g, ident, bias_cols, log_count, cond_stack, norm_stack):
    LNG = TILES // 2
    QKV = 2 * NCH + 3
    V_SETS = [range(a, min(a + 4, TILES)) for a in range(0, TILES, 4)]
    T_SETS = [range(a, min(a + 4, TILES)) for a in range(0, TILES, 4)]
    PAIRS = TILES // 2
    LAG = 2
    NP = 4
    W_USES = 7
    with ExitStack() as ctx:
        def sb(name, shape, dt=F32):
            return ctx.enter_context(nc.sbuf_tensor("gnn_" + name, shape, dt))

        def sem(name):
            return ctx.enter_context(nc.semaphore(name))

        bank = [ctx.enter_context(nc.psum_tensor(f"gnn_bank{i}", [P, 512], F32)) for i in range(8)]
        s_bank, t_bank, o_bank = bank[0:3], bank[3:6], bank[6:8]
        yT = sb("yT", [P, 2, KT, PAD], F16)
        qk = sb("qk", [P, 2, 2, PAD], F16)
        v = sb("v", [P, 2, TILES, DH], F16)
        room = sb("room", [P, 3, 512])
        probs = sb("probs", [P, NP, PAD])
        pT = sb("pT", [P, 2, 2, TILES, 2, P], F16)
        oT = sb("oT", [P, 2, HEADS, PAD], F16)
        raw = sb("raw", [P, KT * D])
        w_qkv = sb("w_qkv", [P, 2, 3, KT, DH], F16)
        w_o = sb("w_o", [P, 2, KT, D], F16)
        bv_rows = sb("bv_rows", [P, D])
        out_bias = sb("out_bias", [P, D])
        qk_bias = sb("qk_bias", [P, 2])
        hidden_bias = sb("hidden_bias", [P, KT])
        best = sb("best", [P, 2, NCH])
        shift = sb("shift", [P, 2])
        total = sb("total", [P, 2])
        inverse = sb("inverse", [P, 2])
        stats = sb("stats", [P, 2, 6])
        mv = sb("mv", [P, 2, 2])
        rstd = sb("rstd", [P, 2])
        minus_half = sb("minus_half", [P, 2])
        y = qk[:].rearrange("p a b n -> p (a b n)").bitcast(F32)[:, 0:4 * D].rearrange("p (s d) -> p s d", s=4)
        hT = probs[:].rearrange("p s n -> p (s n)").bitcast(F16).rearrange("p (a t n) -> p a t n", a=2, t=KT)
        pT_flat = pT[:].rearrange("p s a t b n -> p (s a t b n)")
        w_m1 = pT_flat[:, 0:2 * KT * D].rearrange("p (a k d) -> p a k d", a=2, k=KT)
        w_m2 = pT_flat[:, 2 * KT * D:4 * KT * D].rearrange("p (a k d) -> p a k d", a=2, k=KT)

        names = ("start passed_pool passed_dve passed_act passed_pe recip_ready qk_lo raw_in w_scaled w_hi w_ready bv_in bv_ready ob_in ob_free ob_added "
                 "stats_ready mv_ready var_eps rstd_ready norm_mm y_part y_ready y_turned y_hi y_lo "
                 "res_ready res_free bias_ready proj_ready qkv_hi v_sum v_lo s_ready best_ready "
                 "shift_ready exp_ready inv_ready p_ready p_turned p_hi p_lo o_ready o_hi o_lo "
                 "mlp_ready hidden h_zero h_hi h_ready")
        S = {n: sem("g_" + n) for n in names.split()}
        block = ctx.enter_context(nc.Block())

        @block.sync
        def _(sp):
            def load(L, use, dst, src):
                sp.wait_ge(S["w_ready"], L * W_USES + (use + 1))
                for a, b in zip(dst, src):
                    sp.dma_start(a, b).then_inc(S["raw_in"], 16)

            def square(name, L):
                return io["L0_gnn_" + name][bass.ds(L, 1), :, :].rearrange("a (k p) n -> p (a k) n", p=P)

            with sp.Fori(0, LAYERS) as L:
                sp.wait_ge(S["res_free"], L * 2 * TILES + 1)
                sp.dma_start(bv_rows[:], io["L0_gnn_bv"][bass.ds(L, 1), :].partition_broadcast(P)
                             .rearrange("p a n -> p (a n)")).then_inc(S["bv_in"], 16)
                for h in range(HEADS):
                    load(L, h, [raw[:, n * KT * DH:(n + 1) * KT * DH].rearrange("p (k c) -> p k c", k=KT)
                                          for n in range(3)],
                         [io["L0_gnn_" + w][bass.ds(L, 1), :, h * DH:(h + 1) * DH]
                          .rearrange("a (k p) c -> p (a k) c", p=P) for w in ("wq", "wk", "wv")])
                    if h == 0:
                        sp.wait_ge(S["ob_free"], L * 2 + 1)
                        sp.dma_start(out_bias[:], io["L0_gnn_bo"][bass.ds(L, 1), :].partition_broadcast(P)
                                     .rearrange("p a n -> p (a n)")).then_inc(S["ob_in"], 16)
                load(L, 4, [raw[:].rearrange("p (k n) -> p k n", k=KT)], [square("wo", L)])
                sp.wait_ge(S["ob_free"], L * 2 + 2)
                sp.dma_start(out_bias[:], io["L0_gnn_m_b2"][bass.ds(L, 1), :].partition_broadcast(P)
                             .rearrange("p a n -> p (a n)")).then_inc(S["ob_in"], 16)
                load(L, 5, [raw[:].rearrange("p (k n) -> p k n", k=KT)], [square("m_w1", L)])
                load(L, 6, [raw[:].rearrange("p (k n) -> p k n", k=KT)], [square("m_w2", L)])
        RAW_IN = [48, 96, 144, 192, 208, 224, 240]

        @block.gpsimd
        def _(pool):
            pool.memset(minus_half[:], -0.5).then_inc(S["start"], 1)
            pool.sem_inc(S["w_ready"], 1)
            pool.sem_inc(S["ob_free"], 1)
            pool.wait_ge(S["start"], 1)

            def split(L, use, n, hi, lo):
                hold(pool, S["raw_in"], L * RAW_IN[-1] + RAW_IN[use], S["passed_pool"])
                pool.tensor_scalar(raw[:, 0:n], raw[:, 0:n], W_SCALE, None, ALU.mult).then_inc(S["w_scaled"], 1)
                hold(pool, S["w_scaled"], L * W_USES + (use + 1), S["passed_pool"])
                pool.tensor_copy(hi, raw[:, 0:n]).then_inc(S["w_hi"], 1)
                pool.wait_ge(S["w_hi"], L * W_USES + (use + 1))
                pool.tensor_tensor(lo, raw[:, 0:n], hi, ALU.subtract).then_inc(S["w_ready"], 1)

            def split_head(L, h):
                split(L, h, 3 * KT * DH, w_qkv[:, 0].rearrange("p w k c -> p (w k c)"),
                      w_qkv[:, 1].rearrange("p w k c -> p (w k c)"))

            def split_square(L, use, w):
                split(L, use, KT * D, w[:, 0].rearrange("p k d -> p (k d)"), w[:, 1].rearrange("p k d -> p (k d)"))

            def rsqrt(L, first, group):
                n = L * 2 * LNG + (first + group + 1)
                hold(pool, S["mv_ready"], n, S["passed_pool"])
                pool.tensor_scalar(rstd[:], mv[:, :, 1], EPS, None, ALU.add).then_inc(S["var_eps"], 1)
                pool.wait_ge(S["var_eps"], n)
                pool.tensor_tensor(rstd[:], rstd[:], minus_half[:], ALU.pow).then_inc(S["rstd_ready"], 1)

            with pool.Fori(0, LAYERS) as L:
                split_head(L, 0)
                hold(pool, S["bv_in"], L * 16 + 16, S["passed_pool"])
                pool.tensor_scalar(bv_rows[:], bv_rows[:], W_SCALE, None, ALU.mult).then_inc(S["bv_ready"], 1)
                for n in range(LNG):
                    rsqrt(L, 0, n)
                for h in range(HEADS):
                    if h == 0:
                        pool.wait_ge(S["ob_in"], L * 32 + 16)
                        pool.wait_ge(S["y_ready"], L * 2 * TILES + TILES)
                        for t in range(TILES):
                            ins = pool.tensor_tensor(g[:, t, :], g[:, t, :], out_bias[:], ALU.add)
                        ins.then_inc(S["ob_added"], 1)
                        pool.wait_ge(S["ob_added"], L * 2 + 1)
                        pool.sem_inc(S["ob_free"], 1)
                    for t in range(TILES):
                        hold(pool, S["inv_ready"], L * HEADS * TILES + (h * TILES + t + 1), S["passed_pool"])
                        pool.tensor_scalar(probs[:, t % NP, 0:NODES], probs[:, t % NP, 0:NODES],
                                           inverse[:, t % 2:t % 2 + 1], None, ALU.mult).then_inc(S["p_ready"], 1)
                        if t == 6 and h == HEADS - 1:
                            split_square(L, 4, w_o)
                        if t == 6 and h < HEADS - 1:
                            pool.wait_ge(S["proj_ready"], L * HEADS * QKV + (h + 1) * QKV)
                            split_head(L, h + 1)
                pool.wait_ge(S["o_ready"], L * HEADS * PAIRS + HEADS * PAIRS)
                split_square(L, 5, w_m1)
                for n in range(LNG):
                    rsqrt(L, LNG, n)
                split_square(L, 6, w_m2)
                pool.wait_ge(S["ob_in"], L * 32 + 32)
                pool.wait_ge(S["y_ready"], L * 2 * TILES + 2 * TILES)
                for t in range(TILES):
                    ins = pool.tensor_tensor(g[:, t, :], g[:, t, :], out_bias[:], ALU.add)
                ins.then_inc(S["ob_added"], 1)
                pool.wait_ge(S["ob_added"], L * 2 + 2)
                pool.sem_inc(S["ob_free"], 1)
                pool.memset(hT[:, :, :, NODES:PAD], 0.0).then_inc(S["h_zero"], 1)
                for n in range(KT * NCH):
                    f, (c0, cn) = n // NCH, CHUNKS[n % NCH]
                    hold(pool, S["hidden"], L * KT * NCH + (n + 1), S["passed_pool"])
                    pool.tensor_copy(hT[:, 0, f, c0:c0 + cn], room[:, n % 3, 0:cn]).then_inc(S["h_hi"], 1)
                    pool.wait_ge(S["h_hi"], L * KT * NCH + (n + 1))
                    pool.tensor_tensor(hT[:, 1, f, c0:c0 + cn], room[:, n % 3, 0:cn], hT[:, 0, f, c0:c0 + cn],
                                       ALU.subtract).then_inc(S["h_ready"], 1)

        @block.vector
        def _(dve):
            dve.sem_inc(S["res_free"], 2)

            def norm_front(L, first, n):
                group = L * 2 * LNG + (first * LNG + n + 1)
                for j in range(2):
                    ins = dve.bn_stats(stats[:, j, :], g[:, 2 * n + j, :])
                ins.then_inc(S["stats_ready"], 1)
                hold(dve, S["stats_ready"], group, S["passed_dve"])
                for j in range(2):
                    ins = dve.bn_aggr(mv[:, j, :], stats[:, j, :])
                ins.then_inc(S["mv_ready"], 1)
                dve.wait_ge(S["mv_ready"], group)
                for j in range(2):
                    tile = L * 2 * TILES + (first * TILES + 2 * n + j + 1)
                    dve.wait_ge(S["norm_mm"], tile)
                    dve.scalar_tensor_tensor(y[:, 2 * (n % 2) + j, :], g[:, 2 * n + j, :], mv[:, j, 0:1],
                                             bank[j][:], ALU.subtract, ALU.mult).then_inc(S["y_part"], 1)
                dve.wait_ge(S["rstd_ready"], group)
                for j in range(2):
                    tile = L * 2 * TILES + (first * TILES + 2 * n + j + 1)
                    dve.wait_ge(S["y_part"], tile)
                    slot = y[:, 2 * (n % 2) + j, :]
                    dve.scalar_tensor_tensor(slot, slot, rstd[:, j:j + 1], bank[2 + j][:], ALU.mult, ALU.add
                                             ).then_inc(S["y_ready"], 1)

            def norm_back(L, first, n):
                for j in range(2):
                    t = 2 * n + j
                    tile = L * 2 * TILES + (first * TILES + t + 1)
                    dve.wait_ge(S["y_hi"], tile)
                    dve.tensor_tensor(yT[:, 1, :, t * P:(t + 1) * P],
                                      bank[4 + j][:].rearrange("p (k n) -> p k n", k=KT),
                                      yT[:, 0, :, t * P:(t + 1) * P], ALU.subtract).then_inc(S["y_lo"], 1)

            def residual(L, first, t):
                n = L * 2 * TILES + (first * TILES + t + 1)
                dve.wait_ge(S["res_ready"], n)
                dve.scalar_tensor_tensor(g[:, t, :], bank[6 + t % 2][:], BACK, g[:, t, :], ALU.mult, ALU.add
                                         ).then_inc(S["res_free"], 1)

            with dve.Fori(0, LAYERS) as L:
                dve.tensor_copy(hidden_bias[:], bias_cols[:, bass.ds(L * KT + 2 * LAYERS * KT, KT)]
                                ).then_inc(S["bias_ready"], 1)
                for n in range(LNG + 1):
                    if n < LNG:
                        norm_front(L, 0, n)
                    if n:
                        norm_back(L, 0, n - 1)
                with dve.Fori(0, HEADS) as H:
                    it = L * HEADS + H
                    dve.memset(qk[:, :, :, NODES:PAD], 0.0)
                    dve.memset(probs[:, :, NODES:PAD], 0.0)
                    dve.tensor_copy(qk_bias[:, 0:1], bias_cols[:, bass.ds(it, 1)])
                    dve.tensor_copy(qk_bias[:, 1:2], bias_cols[:, bass.ds(it + LAYERS * KT, 1)]
                                    ).then_inc(S["bias_ready"], 1)
                    dve.wait_ge(S["bias_ready"], it + L + 2)
                    for w in (1, 0):
                        for c, (c0, cn) in enumerate(CHUNKS):
                            dve.wait_ge(S["qkv_hi"], it * QKV + ((1 - w) * NCH + c + 1))
                            dve.scalar_tensor_tensor(qk[:, w, 1, c0:c0 + cn], s_bank[c][:, 0:cn], qk_bias[:, w:w + 1],
                                                     qk[:, w, 0, c0:c0 + cn], ALU.add, ALU.subtract
                                                     ).then_inc(S["qk_lo"], 1)
                    dve.wait_ge(S["bv_ready"], L + 1)
                    for c, tiles in enumerate(V_SETS):
                        n = len(tiles)
                        dve.wait_ge(S["proj_ready"], it * QKV + (2 * NCH + c + 1))
                        dve.tensor_tensor(room[:, c, 0:n * DH].rearrange("p (t d) -> p t d", d=DH),
                                          s_bank[c][:, 0:n * DH].rearrange("p (t d) -> p t d", d=DH),
                                          bv_rows[:, bass.ds(H * DH, DH)].unsqueeze(1).to_broadcast([P, n, DH]),
                                          ALU.add).then_inc(S["v_sum"], 1)
                    dve.wait_ge(S["qkv_hi"], it * QKV + QKV)
                    for c, tiles in enumerate(V_SETS):
                        n = len(tiles)
                        dve.tensor_tensor(v[:, 1, tiles[0]:tiles[0] + n, :],
                                          room[:, c, 0:n * DH].rearrange("p (t d) -> p t d", d=DH),
                                          v[:, 0, tiles[0]:tiles[0] + n, :], ALU.subtract).then_inc(S["v_lo"], 1)

                    def scores_max(t):
                        for c, (c0, cn) in enumerate(CHUNKS):
                            hold(dve, S["s_ready"], it * NCH * TILES + (NCH * t + c + 1), S["passed_dve"])
                            if c:
                                hold(dve, S["best_ready"], it * NCH * TILES + (NCH * t + c), S["passed_dve"])
                            dve.tensor_tensor_reduce(probs[:, t % NP, c0:c0 + cn], s_bank[c][:, 0:cn],
                                                     log_count[:, t, c0:c0 + cn], 1.0,
                                                     best[:, t % 2, c - 1:c] if c else 2 * MASKED, ALU.add, ALU.max,
                                                     best[:, t % 2, c:c + 1]).then_inc(S["best_ready"], 1)
                        dve.wait_ge(S["best_ready"], it * NCH * TILES + (NCH * t + NCH))
                        dve.tensor_scalar(shift[:, t % 2:t % 2 + 1], best[:, t % 2, NCH - 1:NCH], -SCORE, MAX_SHIFT,
                                          ALU.mult, ALU.min).then_inc(S["shift_ready"], 1)

                    def inverse_sum(t):
                        dve.wait_ge(S["exp_ready"], it * TILES + (t + 1))
                        slot = inverse[:, t % 2:t % 2 + 1]
                        dve.tensor_scalar(total[:, t % 2:t % 2 + 1], total[:, t % 2:t % 2 + 1], LEAST_SUM, None,
                                          ALU.max).then_inc(S["recip_ready"], 1)
                        dve.wait_ge(S["recip_ready"], it * TILES + (t + 1))
                        dve.reciprocal(slot, total[:, t % 2:t % 2 + 1]).then_inc(S["inv_ready"], 1)

                    def turned_rest(t):
                        for c, blocks in enumerate(T_SETS):
                            n = len(blocks)
                            dve.wait_ge(S["p_hi"], it * 3 * TILES + (3 * t + c + 1))
                            a = pT[:, (t // 2) % 2, :, blocks[0]:blocks[0] + n, t % 2, :]
                            dve.tensor_tensor(a[:, 1], t_bank[c][:, 0:n * P].rearrange("p (b n) -> p b n", n=P),
                                              a[:, 0], ALU.subtract).then_inc(S["p_lo"], 1)

                    def out_rest(pair):
                        dve.wait_ge(S["o_hi"], it * PAIRS + (pair + 1))
                        dst = oT[:, :, bass.ds(H, 1), pair * 2 * P:(pair + 1) * 2 * P]
                        dve.tensor_tensor(dst[:, 1, 0], o_bank[pair % 2][:, 0:2 * P], dst[:, 0, 0], ALU.subtract
                                          ).then_inc(S["o_lo"], 1)

                    for i in range(TILES + LAG):
                        if i < TILES:
                            scores_max(i)
                        if 1 <= i <= TILES:
                            inverse_sum(i - 1)
                        t = i - LAG
                        if t >= 0:
                            turned_rest(t)
                        if t >= 3 and t % 2 == 1:
                            out_rest((t - 3) // 2)
                    out_rest(PAIRS - 1)

                for n in range(LNG + 1):
                    if n < LNG:
                        if n == 0:
                            dve.wait_ge(S["ob_added"], L * 2 + 1)
                        residual(L, 0, 2 * n)
                        residual(L, 0, 2 * n + 1)
                        dve.wait_ge(S["res_free"], L * 2 * TILES + (2 * n + 4))
                        norm_front(L, 1, n)
                    if n:
                        norm_back(L, 1, n - 1)
                dve.wait_ge(S["h_zero"], L + 1)
                dve.wait_ge(S["ob_added"], L * 2 + 2)
                for t in range(TILES):
                    residual(L, 1, t)
                dve.wait_ge(S["res_free"], L * 2 * TILES + (2 * TILES + 2))

        @block.scalar
        def _(act):
            def norm_hi(L, first, t):
                act.wait_ge(S["y_turned"], L * 2 * TILES + (first * TILES + t + 1))
                act.activation(yT[:, 0, :, t * P:(t + 1) * P], bank[4 + t % 2][:].rearrange("p (k n) -> p k n", k=KT),
                               ACT.Copy).then_inc(S["y_hi"], 1)

            with act.Fori(0, LAYERS) as L:
                for t in range(TILES):
                    norm_hi(L, 0, t)
                with act.Fori(0, HEADS) as H:
                    it = L * HEADS + H
                    act.wait_ge(S["bias_ready"], it + L + 2)
                    for w in (1, 0):
                        for c, (c0, cn) in enumerate(CHUNKS):
                            act.wait_ge(S["proj_ready"], it * QKV + ((1 - w) * NCH + c + 1))
                            act.activation(qk[:, w, 0, c0:c0 + cn], s_bank[c][:, 0:cn], ACT.Identity,
                                           bias=qk_bias[:, w:w + 1]).then_inc(S["qkv_hi"], 1)
                    for c, tiles in enumerate(V_SETS):
                        n = len(tiles)
                        act.wait_ge(S["v_sum"], it * 3 + (c + 1))
                        act.activation(v[:, 0, tiles[0]:tiles[0] + n, :],
                                       room[:, c, 0:n * DH].rearrange("p (t d) -> p t d", d=DH), ACT.Copy
                                       ).then_inc(S["qkv_hi"], 1)

                    def turned_hi(t):
                        for c, blocks in enumerate(T_SETS):
                            n = len(blocks)
                            act.wait_ge(S["p_turned"], it * 3 * TILES + (3 * t + c + 1))
                            act.activation(pT[:, (t // 2) % 2, 0, blocks[0]:blocks[0] + n, t % 2, :],
                                           t_bank[c][:, 0:n * P].rearrange("p (b n) -> p b n", n=P), ACT.Copy
                                           ).then_inc(S["p_hi"], 1)

                    def out_hi(pair):
                        hold(act, S["o_ready"], it * PAIRS + (pair + 1), S["passed_act"])
                        act.activation(oT[:, 0, bass.ds(H, 1), pair * 2 * P:(pair + 1) * 2 * P],
                                       o_bank[pair % 2][:, 0:2 * P].unsqueeze(1), ACT.Copy).then_inc(S["o_hi"], 1)

                    for i in range(TILES + LAG):
                        if i < TILES:
                            act.wait_ge(S["shift_ready"], it * TILES + (i + 1))
                            act.activation(probs[:, i % NP, 0:NODES], probs[:, i % NP, 0:NODES], ACT.Exp,
                                           bias=shift[:, i % 2:i % 2 + 1], scale=SCORE,
                                           accum_out=total[:, i % 2:i % 2 + 1]).then_inc(S["exp_ready"], 1)
                        t = i - LAG
                        if t >= 0:
                            turned_hi(t)
                        if t >= 3 and t % 2 == 1:
                            out_hi((t - 3) // 2)
                    out_hi(PAIRS - 1)
                for t in range(TILES):
                    norm_hi(L, 1, t)
                for n in range(KT * NCH):
                    f, (c0, cn) = n // NCH, CHUNKS[n % NCH]
                    act.wait_ge(S["mlp_ready"], L * KT * NCH + (n + 1))
                    act.wait_ge(S["h_ready"], L * KT * NCH + (n - 2)) if n >= 3 else None
                    act.activation(room[:, n % 3, 0:cn], bank[n % 4][:, 0:cn], ACT.Relu,
                                   bias=hidden_bias[:, f:f + 1]
                                   ).then_inc(S["hidden"], 1)

        @block.tensor
        def _(pe):
            def norm_weights(L, first, t):
                if t >= 2:
                    hold(pe, S["y_ready"], L * 2 * TILES + (first * TILES + t - 1), S["passed_pe"])
                for m in range(2):
                    ins = pe.matmul(bank[2 * m + t % 2][:], cond_stack[:, t * P:(t + 1) * P],
                                    norm_stack[:, bass.ds(L * MATS + (2 * first + m), 1), :]
                                    .rearrange("c a d -> c (a d)"), start=True, stop=True)
                ins.then_inc(S["norm_mm"], 1)

            def norm_turn(L, first, t):
                n = L * 2 * TILES + (first * TILES + t)
                pe.wait_ge(S["y_ready"], n + 1)
                if first or t >= 2:
                    pe.wait_ge(S["y_lo"], n - 1)
                for k in range(KT):
                    ins = pe.transpose(bank[4 + t % 2][:, k * P:(k + 1) * P], y[:, t % 4, k * P:(k + 1) * P], ident[:])
                ins.then_inc(S["y_turned"], 1)

            with pe.Fori(0, LAYERS) as L:
                for n in range(LNG + 1):
                    if n < LNG:
                        norm_weights(L, 0, 2 * n)
                        norm_weights(L, 0, 2 * n + 1)
                    if n:
                        norm_turn(L, 0, 2 * n - 2)
                        norm_turn(L, 0, 2 * n - 1)
                hold(pe, S["y_lo"], L * 2 * TILES + TILES, S["passed_pe"])
                with pe.Fori(0, HEADS) as H:
                    it = L * HEADS + H
                    pe.wait_ge(S["w_ready"], L * W_USES + H + 2)
                    for n, w in enumerate((1, 0)):
                        for c, (c0, cn) in enumerate(CHUNKS):
                            if n:
                                pe.wait_ge(S["qk_lo"], it * 2 * NCH + (c + 1))
                            split_matmuls(pe, s_bank[c][:, 0:cn], lambda a, k: w_qkv[:, a, w, k, :],
                                     lambda b, k: yT[:, b, k, c0:c0 + cn], KT).then_inc(S["proj_ready"], 1)
                    for c, tiles in enumerate(V_SETS):
                        pe.wait_ge(S["qk_lo"], it * 2 * NCH + (NCH + c + 1))
                        for j, t in enumerate(tiles):
                            ins = split_matmuls(pe, s_bank[c][:, j * DH:(j + 1) * DH],
                                           lambda a, k: yT[:, a, k, t * P:(t + 1) * P],
                                           lambda b, k: w_qkv[:, b, 2, k, :], KT)
                        ins.then_inc(S["proj_ready"], 1)

                    def score(t):
                        for c, (c0, cn) in enumerate(CHUNKS):
                            if t:
                                pe.wait_ge(S["best_ready"], it * NCH * TILES + (NCH * (t - 1) + c + 1))
                            else:
                                pe.wait_ge(S["v_sum"], it * 3 + (c + 1))
                            split_matmuls(pe, s_bank[c][:, 0:cn], lambda a, k: qk[:, 0, a, t * P:(t + 1) * P],
                                     lambda b, k: qk[:, 1, b, c0:c0 + cn], 1).then_inc(S["s_ready"], 1)

                    def turn(t):
                        pe.wait_ge(S["p_ready"], it * TILES + (t + 1))
                        for c, blocks in enumerate(T_SETS):
                            if t:
                                pe.wait_ge(S["p_lo"], it * 3 * TILES + (3 * (t - 1) + c + 1))
                            for j, b in enumerate(blocks):
                                ins = pe.transpose(t_bank[c][:, j * P:(j + 1) * P],
                                                   probs[:, t % NP, b * P:(b + 1) * P], ident[:])
                            ins.then_inc(S["p_turned"], 1)

                    def values(pair):
                        pe.wait_ge(S["p_lo"], it * 3 * TILES + 3 * (2 * pair + 2))
                        if pair == 0:
                            pe.wait_ge(S["v_lo"], it * 3 + 3)
                        if pair >= 2:
                            pe.wait_ge(S["o_lo"], it * PAIRS + (pair - 1))
                        split_matmuls(pe, o_bank[pair % 2][:, 0:2 * P], lambda a, k: v[:, a, k, :],
                                 lambda b, k: pT[:, pair % 2, b, k, :, :].rearrange("p s n -> p (s n)"), TILES
                                 ).then_inc(S["o_ready"], 1)

                    for i in range(TILES + LAG):
                        if i < TILES:
                            score(i)
                        t = i - LAG
                        if t >= 0:
                            turn(t)
                        if t >= 2 and t % 2 == 0:
                            values(t // 2 - 1)
                    values(PAIRS - 1)
                    pe.wait_ge(S["o_lo"], it * PAIRS + PAIRS)

                pe.wait_ge(S["w_ready"], L * W_USES + 6)
                for n in range(LNG + 1):
                    if n < LNG:
                        for j in range(2):
                            t = 2 * n + j
                            pe.wait_ge(S["res_free"], L * 2 * TILES + (t + 1))
                            split_matmuls(pe, bank[6 + j][:], lambda a, k: oT[:, a, k, t * P:(t + 1) * P],
                                     lambda b, k: w_o[:, b, k, :], HEADS).then_inc(S["res_ready"], 1)
                            norm_weights(L, 1, t)
                    if n:
                        norm_turn(L, 1, 2 * n - 2)
                        norm_turn(L, 1, 2 * n - 1)
                pe.wait_ge(S["y_lo"], L * 2 * TILES + 2 * TILES)
                pe.wait_ge(S["w_ready"], L * W_USES + 7)
                for n in range(KT * NCH):
                    f, (c0, cn) = n // NCH, CHUNKS[n % NCH]
                    if n >= 4:
                        pe.wait_ge(S["hidden"], L * KT * NCH + (n - 3))
                    split_matmuls(pe, bank[n % 4][:, 0:cn], lambda a, k: w_m1[:, a, k, f * P:(f + 1) * P],
                             lambda b, k: yT[:, b, k, c0:c0 + cn], KT).then_inc(S["mlp_ready"], 1)
                pe.wait_ge(S["h_ready"], L * KT * NCH + KT * NCH)
                pe.wait_ge(S["w_ready"], L * W_USES + 8)
                for t in range(TILES):
                    pe.wait_ge(S["res_free"], L * 2 * TILES + (TILES + t + 1))
                    split_matmuls(pe, bank[6 + t % 2][:], lambda a, k: hT[:, a, k, t * P:(t + 1) * P],
                             lambda b, k: w_m2[:, b, k, :], KT).then_inc(S["res_ready"], 1)


def experts(nc, io, g, ident, gu_cols):
    I_T = FF // P
    ROUND = 2
    with ExitStack() as ctx:
        def sb(name, shape, dt=F32):
            return ctx.enter_context(nc.sbuf_tensor("moe_" + name, shape, dt))

        bank = [ctx.enter_context(nc.psum_tensor(f"moe_bank{i}", [P, 512], F32)) for i in range(8)]
        x_in = sb("x", [P, TILES, D])
        xT = sb("xT", [P, 2, KT, PAD], F16)
        acc = sb("acc", [P, TILES, D])
        actT = sb("actT", [P, 2, I_T, PAD], F16)
        y = sb("y", [P, 2, D])
        raw_gu = sb("raw_gu", [P, 2, 2, KT, P])
        w_gu = sb("w_gu", [P, ROUND, 2, 2, KT, P], F16)
        raw_down = sb("raw_down", [P, 2, D])
        w_down = sb("w_down", [P, 2, I_T, D], F16)
        sig = sb("sig", [P, 2, 512])
        gated = sb("gated", [P, 2, 512])
        raw_router = sb("raw_router", [P, KT, EXPERTS])
        w_router = sb("w_router", [P, 2, KT, EXPERTS], F16)
        router_b = sb("router_b", [P, EXPERTS])
        down_b = sb("down_b", [EXPERTS, D])
        logits = sb("logits", [P, TILES, EXPERTS])
        top = sb("top", [P, TILES])
        weight = sb("weight", [P, TILES, EXPERTS])
        share = sb("share", [P, TILES, EXPERTS])
        weightT = sb("weightT", [EXPERTS, PAD])
        greater = sb("greater", [P, TILES, EXPERTS, EXPERTS])
        equal = sb("equal", [P, TILES, EXPERTS, EXPERTS])
        before = sb("before", [P, EXPERTS, EXPERTS])
        rank = sb("rank", [P, TILES, EXPERTS])
        whole = sb("whole", [P, TILES])
        stats = sb("stats", [P, TILES, 6])
        mv = sb("mv", [P, TILES, 2])
        rstd = sb("rstd", [P, TILES])
        minus_half = sb("minus_half", [P, TILES])

        names = ("start x_in small_in raw_in_0 raw_in_1 raw_scaled raw_hi w_ready down_in_0 down_in_1 down_scaled down_hi "
                 "down_ready x_step rstd_step y_ready y_turned y_hi y_lo router_step router_mm route route_exp "
                 "weight_turned bias_mm acc_ready pair_ready sig_ready gated_ready act_ready act_hi act_lo "
                 "down_mm down_free out_done passed_pool passed_dve passed_act passed_pe")
        S = {n: ctx.enter_context(nc.semaphore("m_" + n)) for n in names.split()}
        block = ctx.enter_context(nc.Block())
        PAIRS = I_T * NCH

        @block.sync
        def _(sp):
            sp.wait_ge(S["start"], 1)
            sp.dma_start(x_in[:, 0:TILES - 1, :], io["x"][0:(TILES - 1) * P, :].rearrange("(t p) d -> p t d", p=P)
                         ).then_inc(S["x_in"], 16)
            sp.dma_start(x_in[0:LAST, TILES - 1, :], io["x"][(TILES - 1) * P:NODES, :]).then_inc(S["x_in"], 16)
            sp.dma_start(raw_router[:], io["L0_ffn_router_w"].rearrange("(k p) e -> p k e", p=P)
                         ).then_inc(S["small_in"], 16)
            sp.dma_start(router_b[:], io["L0_ffn_router_b"].rearrange("(a e) -> a e", a=1).partition_broadcast(P)
                         .rearrange("p a e -> p (a e)")).then_inc(S["small_in"], 16)
            sp.dma_start(down_b[:], io["L0_ffn_down_proj_bias"]).then_inc(S["small_in"], 16)
            with sp.Fori(0, EXPERTS) as e:
                gate_up = io["L0_ffn_gate_up_proj"][bass.ds(e, 1), :, :].rearrange("a (k p) n -> p (a k) n", p=P)
                down = io["L0_ffn_down_proj"][bass.ds(e, 1), :, :].rearrange("a (i p) n -> p (a i) n", p=P)
                for i in range(I_T):
                    sp.wait_ge(S["w_ready"], e * I_T + (i + 1))
                    for u in range(2):
                        sp.dma_start(raw_gu[:, i % 2, u], gate_up[:, :, u * FF + i * P:u * FF + (i + 1) * P]
                                     ).then_inc(S[f"raw_in_{i % 2}"], 16)
                    sp.wait_ge(S["down_ready"], e * I_T + (i + 1))
                    sp.dma_start(raw_down[:, i % 2, :], down[:, i, :]).then_inc(S[f"down_in_{i % 2}"], 16)
            sp.wait_ge(S["down_free"], (EXPERTS + 1) * TILES)
            sp.dma_start(io["out"][0:(TILES - 1) * P, :].rearrange("(t p) d -> p t d", p=P), acc[:, 0:TILES - 1, :]
                         ).then_inc(S["out_done"], 16)
            sp.dma_start(io["out"][(TILES - 1) * P:NODES, :], acc[0:LAST, TILES - 1, :]).then_inc(S["out_done"], 16)
            sp.wait_ge(S["out_done"], 32)

        @block.gpsimd
        def _(pool):
            pool.memset(x_in[96:P, TILES - 1, :], 0.0).then_inc(S["start"], 1)
            pool.wait_ge(S["start"], 1)
            pool.memset(minus_half[:], -0.5).then_inc(S["rstd_step"], 1)
            pool.memset(before[:], 1.0).then_inc(S["rstd_step"], 1)
            pool.sem_inc(S["w_ready"], 2)
            pool.sem_inc(S["down_ready"], 2)
            pool.wait_ge(S["rstd_step"], 2)
            pool.affine_select(out=before[:], in_=before[:], compare_op=ALU.is_gt, fill=0.0, base=0,
                               pattern=[[1, EXPERTS], [-1, EXPERTS]], channel_multiplier=0
                               ).then_inc(S["rstd_step"], 1)
            pool.wait_ge(S["x_step"], 3)
            pool.tensor_scalar(rstd[:], mv[:, :, 1], EPS, None, ALU.add).then_inc(S["rstd_step"], 1)
            pool.wait_ge(S["rstd_step"], 4)
            pool.tensor_tensor(rstd[:], rstd[:], minus_half[:], ALU.pow).then_inc(S["rstd_step"], 1)
            with pool.Fori(0, EXPERTS) as e:
                for i in range(I_T):
                    n = e * I_T + (i + 1)
                    raw = raw_gu[:, i % 2].rearrange("p u k c -> p (u k c)")
                    hi = w_gu[:, i % 2, 0].rearrange("p u k c -> p (u k c)")
                    lo = w_gu[:, i % 2, 1].rearrange("p u k c -> p (u k c)")
                    hold(pool, S[f"raw_in_{i % 2}"], (e * (I_T // 2) + (i // 2 + 1)) * 32, S["passed_pool"])
                    pool.tensor_scalar(raw, raw, W_SCALE, None, ALU.mult).then_inc(S["raw_scaled"], 1)
                    hold(pool, S["raw_scaled"], n, S["passed_pool"])
                    hold(pool, S["pair_ready"], e * PAIRS + NCH * (i + 1), S["passed_pool"])
                    pool.tensor_copy(hi, raw).then_inc(S["raw_hi"], 1)
                    pool.wait_ge(S["raw_hi"], n)
                    pool.tensor_tensor(lo, raw, hi, ALU.subtract).then_inc(S["w_ready"], 1)
                    hold(pool, S[f"down_in_{i % 2}"], (e * (I_T // 2) + (i // 2 + 1)) * 16, S["passed_pool"])
                    pool.tensor_scalar(raw_down[:, i % 2], raw_down[:, i % 2], W_SCALE, None, ALU.mult
                                       ).then_inc(S["down_scaled"], 1)
                    hold(pool, S["down_scaled"], n, S["passed_pool"])
                    if i == 0:
                        hold(pool, S["down_mm"], e * TILES + 1, S["passed_pool"])
                    pool.tensor_copy(w_down[:, 0, i], raw_down[:, i % 2]).then_inc(S["down_hi"], 1)
                    pool.wait_ge(S["down_hi"], n)
                    pool.tensor_tensor(w_down[:, 1, i], raw_down[:, i % 2], w_down[:, 0, i], ALU.subtract
                                       ).then_inc(S["down_ready"], 1)

        @block.vector
        def _(dve):
            dve.wait_ge(S["x_in"], 32)
            for t in range(TILES):
                ins = dve.tensor_tensor(g[:, t, :], g[:, t, :], x_in[:, t, :], ALU.add)
            ins.then_inc(S["x_step"], 1)
            dve.memset(actT[:, :, :, NODES:PAD], 0.0)
            dve.wait_ge(S["small_in"], 48)
            dve.tensor_scalar(raw_router[:], raw_router[:], W_SCALE, None, ALU.mult).then_inc(S["router_step"], 1)
            dve.wait_ge(S["router_step"], 1)
            dve.tensor_copy(w_router[:, 0], raw_router[:]).then_inc(S["router_step"], 1)
            dve.wait_ge(S["router_step"], 2)
            dve.tensor_tensor(w_router[:, 1], raw_router[:], w_router[:, 0], ALU.subtract
                              ).then_inc(S["router_step"], 1)
            dve.wait_ge(S["x_step"], 1)
            for t in range(TILES):
                ins = dve.bn_stats(stats[:, t, :], g[:, t, :])
            ins.then_inc(S["x_step"], 1)
            dve.wait_ge(S["x_step"], 2)
            for t in range(TILES):
                ins = dve.bn_aggr(mv[:, t, :], stats[:, t, :])
            ins.then_inc(S["x_step"], 1)
            dve.wait_ge(S["rstd_step"], 5)
            dve.wait_ge(S["x_step"], 3)
            for t in range(TILES + 1):
                if t < TILES:
                    dve.tensor_scalar(y[:, t % 2, :], g[:, t, :], mv[:, t, 0:1], rstd[:, t:t + 1], ALU.subtract,
                                      ALU.mult).then_inc(S["y_ready"], 1)
                if t:
                    a = t - 1
                    dve.wait_ge(S["y_hi"], a + 1)
                    dve.tensor_tensor(xT[:, 1, :, a * P:(a + 1) * P],
                                      bank[a % 2][:].rearrange("p (k n) -> p k n", k=KT),
                                      xT[:, 0, :, a * P:(a + 1) * P], ALU.subtract).then_inc(S["y_lo"], 1)

            def route(ins, at):
                ins.then_inc(S["route"], 1)
                dve.wait_ge(S["route"], at)

            dve.wait_ge(S["router_mm"], 1)
            route(dve.scalar_tensor_tensor(logits[:], bank[2][:, 0:TILES * EXPERTS]
                                           .rearrange("p (t e) -> p t e", t=TILES), 1.0 / W_SCALE,
                                           router_b[:].unsqueeze(1).to_broadcast([P, TILES, EXPERTS]),
                                           ALU.mult, ALU.add), 1)
            route(dve.tensor_reduce(top[:], logits[:], AX.X, ALU.max), 2)
            four = [P, TILES, EXPERTS, EXPERTS]
            other, own = logits[:].unsqueeze(2).to_broadcast(four), logits[:].unsqueeze(3).to_broadcast(four)
            dve.tensor_tensor(greater[:], other, own, ALU.is_gt)
            route(dve.tensor_tensor(equal[:], other, own, ALU.is_equal), 3)
            route(dve.tensor_tensor(equal[:], equal[:], before[:].unsqueeze(1).to_broadcast(four), ALU.mult), 4)
            route(dve.tensor_tensor(equal[:], equal[:], greater[:], ALU.add), 5)
            route(dve.tensor_reduce(rank[:], equal[:], AX.X, ALU.add), 6)
            flat = [P, TILES, EXPERTS]
            route(dve.tensor_tensor(weight[:], logits[:], top[:].unsqueeze(2).to_broadcast(flat), ALU.subtract), 7)
            dve.wait_ge(S["route_exp"], 1)
            route(dve.scalar_tensor_tensor(weight[:], rank[:], float(TOP_K), weight[:], ALU.is_lt, ALU.mult), 8)
            route(dve.tensor_reduce(whole[:], weight[:], AX.X, ALU.add), 9)
            route(dve.reciprocal(whole[:], whole[:]), 10)
            route(dve.tensor_tensor(weight[:], weight[:], whole[:].unsqueeze(2).to_broadcast(flat), ALU.mult), 11)
            dve.tensor_scalar(share[:], weight[:], BACK, None, ALU.mult)
            for c in range(NCH):
                dve.wait_ge(S["weight_turned"], c + 1)
                n = min(4, TILES - 4 * c) * P
                ins = dve.tensor_copy(weightT[:, c * 512:c * 512 + n], bank[3 + c][0:EXPERTS, 0:n])
            ins.then_inc(S["route"], 1)
            for t in range(TILES):
                dve.wait_ge(S["bias_mm"], t + 1)
                dve.tensor_tensor(acc[:, t, :], bank[6 + t % 2][:], g[:, t, :], ALU.add).then_inc(S["down_free"], 1)
            dve.wait_ge(S["down_free"], TILES)
            with dve.Fori(0, EXPERTS) as e:
                for m in range(PAIRS + 1):
                    if m < PAIRS:
                        i, (c0, cn) = m // NCH, CHUNKS[m % NCH]
                        n = e * PAIRS + (m + 1)
                        gate, up = bank[m % 3][:, 0:cn], bank[3 + m % 3][:, 0:cn]
                        col = e * (2 * I_T) + i
                        dve.wait_ge(S["sig_ready"], n)
                        if m >= 2:
                            dve.wait_ge(S["act_lo"], e * PAIRS + (m - 1))
                        dve.scalar_tensor_tensor(gated[:, m % 2, 0:cn], gate, gu_cols[:, 1, bass.ds(col, 1)],
                                                 sig[:, m % 2, 0:cn], ALU.add, ALU.mult
                                                 ).then_inc(S["gated_ready"], 1)
                        dve.wait_ge(S["gated_ready"], n)
                        dve.scalar_tensor_tensor(gated[:, m % 2, 0:cn], up,
                                                 gu_cols[:, 2, bass.ds(col + I_T, 1)],
                                                 gated[:, m % 2, 0:cn], ALU.add, ALU.mult
                                                 ).then_inc(S["act_ready"], 1)
                    if m:
                        i, (c0, cn) = (m - 1) // NCH, CHUNKS[(m - 1) % NCH]
                        dve.wait_ge(S["act_hi"], e * PAIRS + m)
                        dve.scalar_tensor_tensor(actT[:, 1, i, c0:c0 + cn], gated[:, (m - 1) % 2, 0:cn],
                                                 1.0 / W_SCALE, actT[:, 0, i, c0:c0 + cn], ALU.mult,
                                                 ALU.subtract).then_inc(S["act_lo"], 1)
                for t in range(TILES):
                    dve.wait_ge(S["down_mm"], e * TILES + (t + 2))
                    dve.scalar_tensor_tensor(acc[:, t, :], bank[6 + t % 2][:], share[:, t, bass.ds(e, 1)],
                                             acc[:, t, :], ALU.mult, ALU.add).then_inc(S["down_free"], 1)
                dve.wait_ge(S["down_free"], e * TILES + 2 * TILES)

        @block.scalar
        def _(act):
            for t in range(TILES):
                act.wait_ge(S["y_turned"], t + 1)
                act.activation(xT[:, 0, :, t * P:(t + 1) * P], bank[t % 2][:].rearrange("p (k n) -> p k n", k=KT),
                               ACT.Copy).then_inc(S["y_hi"], 1)
            act.wait_ge(S["route"], 7)
            act.activation(weight[:], weight[:], ACT.Exp).then_inc(S["route_exp"], 1)
            with act.Fori(0, EXPERTS) as e:
                for m in range(PAIRS + 1):
                    if m < PAIRS:
                        i, (c0, cn) = m // NCH, CHUNKS[m % NCH]
                        hold(act, S["pair_ready"], e * PAIRS + (m + 1 + 2 * NCH), S["passed_act"])
                        act.activation(sig[:, m % 2, 0:cn], bank[m % 3][:, 0:cn], ACT.Sigmoid,
                                       bias=gu_cols[:, 0, bass.ds(e * (2 * I_T) + i, 1)], scale=1.702 / W_SCALE
                                       ).then_inc(S["sig_ready"], 1)
                    if m:
                        i, (c0, cn) = (m - 1) // NCH, CHUNKS[(m - 1) % NCH]
                        act.wait_ge(S["act_ready"], e * PAIRS + m)
                        act.activation(actT[:, 0, i, c0:c0 + cn], gated[:, (m - 1) % 2, 0:cn], ACT.Copy,
                                       scale=1.0 / W_SCALE).then_inc(S["act_hi"], 1)

        @block.tensor
        def _(pe):
            pe.sem_inc(S["down_mm"], 1)
            pe.sem_inc(S["pair_ready"], 2 * NCH)
            for t in range(TILES):
                pe.wait_ge(S["y_ready"], t + 1)
                if t >= 2:
                    pe.wait_ge(S["y_lo"], t - 1)
                for k in range(KT):
                    ins = pe.transpose(bank[t % 2][:, k * P:(k + 1) * P], y[:, t % 2, k * P:(k + 1) * P], ident[:])
                ins.then_inc(S["y_turned"], 1)
            pe.wait_ge(S["y_lo"], TILES)
            pe.wait_ge(S["router_step"], 3)
            for t in range(TILES):
                ins = split_matmuls(pe, bank[2][:, t * EXPERTS:(t + 1) * EXPERTS],
                                    lambda a, k: xT[:, a, k, t * P:(t + 1) * P],
                                    lambda b, k: w_router[:, b, k, :], KT)
            ins.then_inc(S["router_mm"], 1)
            pe.wait_ge(S["route"], 11)
            for c in range(NCH):
                for t in range(4 * c, min(4 * c + 4, TILES)):
                    ins = pe.transpose(bank[3 + c][0:EXPERTS, (t % 4) * P:(t % 4 + 1) * P], weight[:, t, :], ident[:])
                ins.then_inc(S["weight_turned"], 1)
            pe.wait_ge(S["route"], 12)
            for t in range(TILES):
                if t >= 2:
                    pe.wait_ge(S["down_free"], t - 1)
                pe.matmul(bank[6 + t % 2][:], weightT[:, t * P:(t + 1) * P], down_b[:], start=True, stop=True
                          ).then_inc(S["bias_mm"], 1)
            with pe.Fori(0, EXPERTS) as e:
                for m in range(PAIRS):
                    i, (c0, cn) = m // NCH, CHUNKS[m % NCH]
                    if m % NCH == 0:
                        pe.wait_ge(S["w_ready"], e * I_T + (i + 3))
                    if m >= 3:
                        pe.wait_ge(S["act_ready"], e * PAIRS + (m - 2))
                    for u in range(2):
                        ins = split_matmuls(pe, bank[3 * u + m % 3][:, 0:cn],
                                            lambda a, k: w_gu[:, i % 2, a, u, k, :],
                                            lambda b, k: xT[:, b, k, c0:c0 + cn], KT)
                    ins.then_inc(S["pair_ready"], 1)
                pe.wait_ge(S["down_ready"], e * I_T + (I_T + 2))
                pe.wait_ge(S["act_lo"], e * PAIRS + PAIRS)
                for t in range(TILES):
                    pe.wait_ge(S["down_free"], e * TILES + (TILES + t - 1))
                    split_matmuls(pe, bank[6 + t % 2][:], lambda a, i: actT[:, a, i, t * P:(t + 1) * P],
                                  lambda b, i: w_down[:, b, i, :], I_T).then_inc(S["down_mm"], 1)


_INS = ["x", "src", "dst", "node_vec1"] + ["L0_gnn_" + n for n in (
    "f_w1", "f_b1", "f_w2", "f_b2", "s1_w", "s1_b", "b1_w", "b1_b", "wq", "bq", "wk", "bk", "wv", "bv", "wo", "bo",
    "s2_w", "s2_b", "b2_w", "b2_b", "m_w1", "m_b1", "m_w2", "m_b2")] + ["L0_ffn_" + n for n in (
        "router_w", "router_b", "gate_up_proj", "gate_up_proj_bias", "down_proj", "down_proj_bias")]


def kernel(**inputs):
    import concourse.bacc as _bacc
    from concourse.bass_utils import run_bass_kernel_spmd as _run

    nc = _bacc.Bacc("TRN2", target_bir_lowering=False, num_devices=1, dynamic_dma_scratch_size=1024)
    arrays, io = {}, {}
    for name in _INS:
        a = np.ascontiguousarray(inputs[name])
        arrays[f"in_{name}"] = a
        io[name] = nc.dram_tensor(f"in_{name}", a.shape, mybir.dt.from_np(a.dtype), kind="ExternalInput").ap()
    io["out"] = nc.dram_tensor("out_x", (NODES, D), F32, kind="ExternalOutput").ap()
    build(nc, io)
    r = _run(nc, [arrays], core_ids=[0])
    return r.results[0]["out_x"]
```

```python
from contextlib import ExitStack

import numpy as np

import concourse.bass as bass
from concourse import mybir

F32 = mybir.dt.float32
F16 = mybir.dt.float16
I32 = mybir.dt.int32
ALU = mybir.AluOpType
ACT = mybir.ActivationFunctionType
AX = mybir.AxisListType

P = 128
NODES = 1250
D = 512
EDGES = 20000
LAYERS = 4
HEADS = 4
DH = D // HEADS
FREQS = 32
BASE_PERIOD = 16
COND = 16
EXPERTS = 8
FF = 1024
TOP_K = 2
EPS = 1e-5

TILES = -(-NODES // P)
PAD = TILES * P
LAST = NODES - (TILES - 1) * P
KT = D // P
CHUNKS = [(c, min(512, NODES - c)) for c in range(0, NODES, 512)]
NCH = len(CHUNKS)
W_SCALE = 64.0
BACK = 1.0 / (W_SCALE * W_SCALE)
SCORE = DH ** -0.5 * BACK
MASKED = -1e30
MAX_SHIFT = 1e20
LEAST_SUM = 1e-20

EP = 125
ECOLS = EDGES // EP
HALF = PAD // 2
FIELD = 4096
GROUP = 32
assert GROUP * EP < FIELD and ECOLS % GROUP == 0
NGROUPS = ECOLS // GROUP
BLK = 8
BLKS = GROUP // BLK
SWEEPS = TILES // 2

NROWS = 96
MATS = 4
PASSES = ((0, 0), (0, 1), (1, 0))


def hold(eng, sem, value, passed):
    eng.wait_ge(sem, value)
    eng.sem_inc(passed, 1)


def split_matmuls(pe, out, stationary, moving, n_k):
    for k in range(n_k):
        for i, (a, b) in enumerate(PASSES):
            ins = pe.matmul(out, stationary(a, k), moving(b, k), start=k == 0 and i == 0,
                            stop=k == n_k - 1 and i == len(PASSES) - 1)
    return ins


def build(nc, io):
    with ExitStack() as whole:
        def sb(name, shape, dt=F32):
            return whole.enter_context(nc.sbuf_tensor(name, shape, dt))

        g = sb("g", [P, TILES, D])
        ident = sb("ident", [P, P])
        bias_cols = sb("bias_cols", [P, 3 * LAYERS * KT])
        gu_cols = sb("gu_cols", [P, 3, EXPERTS * 2 * FF // P])
        with ExitStack() as gnn:
            def gsb(name, shape, dt=F32):
                return gnn.enter_context(nc.sbuf_tensor(name, shape, dt))
            log_count = gsb("log_count", [P, TILES, NODES])
            cond_stack = gsb("cond_stack", [NROWS, PAD], F16)
            norm_stack = gsb("norm_stack", [NROWS, LAYERS * MATS + 2, D], F16)
            prepare(nc, io, g, ident, bias_cols, gu_cols, log_count, cond_stack, norm_stack)
            attention_layers(nc, io, g, ident, bias_cols, log_count, cond_stack, norm_stack)
        experts(nc, io, g, ident, gu_cols)


def prepare(nc, io, g, ident, bias_cols, gu_cols, log_count, cond_stack, norm_stack):
    with ExitStack() as ctx:
        def sb(name, shape, dt=F32):
            return ctx.enter_context(nc.sbuf_tensor(name, shape, dt))

        def sem(name):
            return ctx.enter_context(nc.semaphore(name))

        bank = [ctx.enter_context(nc.psum_tensor(f"pre_bank{i}", [P, 512], F32)) for i in range(8)]
        norm_raw = sb("norm_raw", [NROWS, LAYERS * MATS, D])
        edges = sb("edges", [EP, 2, ECOLS], I32)
        src_rel = sb("src_rel", [EP, ECOLS])
        dst_low = sb("dst_low", [EP, ECOLS])
        dst_weight = sb("dst_weight", [EP, ECOLS])
        columns = sb("columns", [P, HALF], F16)
        src_hot = sb("src_hot", [EP, BLK, 2 * P], F16)
        dst_hot = sb("dst_hot", [EP, BLK, HALF], F16)
        packed = sb("packed", [P, 2, HALF], I32)
        high = sb("high", [P, 2, HALF], I32)
        at_least_1 = sb("at_least_1", [P, 2, NODES])
        logs = sb("logs", [P, 2, NODES])
        noise = sb("noise", [2 * FREQS, NODES])
        turns = sb("turns", [2 * FREQS, NODES])
        freq_row = sb("freq_row", [2 * FREQS, 1], I32)
        freq = sb("freq", [2 * FREQS, 4])
        f1 = sb("f1", [2 * FREQS, COND])
        f1b = sb("f1b", [COND, 1])
        f2 = sb("f2", [COND, NROWS])
        f2b = sb("f2b", [NROWS, 1])
        sig = sb("sig", [COND, NODES])
        hidden = sb("hidden", [COND, NODES])
        stats = sb("stats", [P, TILES, 6])
        mv = sb("mv", [P, TILES, 2])
        rstd = sb("rstd", [P, TILES])
        minus_half = sb("minus_half", [P, TILES])
        bias_rows = sb("bias_rows", [3 * LAYERS * KT, P])
        gu_rows = sb("gu_rows", [P, P])
        counts = log_count[:].bitcast(I32)

        edges_in = sem("edges_in")
        x_in = sem("x_in")
        noise_in = sem("noise_in")
        small_in = sem("small_in")
        norm_in = sem("norm_in")
        zeroed = sem("zeroed")
        const_ready = sem("const_ready")
        edge_step = sem("edge_step")
        hot_ready = sem("hot_ready")
        hot_free = sem("hot_free")
        counted = sem("counted")
        count_free = sem("count_free")
        unpacked = sem("unpacked")
        unpack_step = sem("unpack_step")
        added = sem("added")
        adding = sem("adding")
        clamped = sem("clamped")
        logged = sem("logged")
        table_step = sem("table_step")
        cond_step = sem("cond_step")
        cond_act = sem("cond_act")
        cond_mm = sem("cond_mm")
        norm_step = sem("norm_step")
        norm_split = sem("norm_split")
        x_step = sem("x_step")
        rstd_ready = sem("rstd_ready")
        turned = sem("turned")

        block = ctx.enter_context(nc.Block())

        @block.sync
        def _(sp):
            sp.dma_start(edges[:, 0, :], io["src"].rearrange("(p j) -> p j", p=EP)).then_inc(edges_in, 16)
            sp.dma_start(edges[:, 1, :], io["dst"].rearrange("(p j) -> p j", p=EP)).then_inc(edges_in, 16)
            sp.dma_start(noise[:], io["node_vec1"].rearrange("n a -> a n").partition_broadcast(2 * FREQS)
                         .rearrange("p a n -> p (a n)")).then_inc(noise_in, 16)
            sp.dma_start(f1[:], io["L0_gnn_f_w1"]).then_inc(noise_in, 16)
            sp.dma_start(f1b[:], io["L0_gnn_f_b1"].rearrange("(c a) -> c a", a=1)).then_inc(noise_in, 16)
            sp.wait_ge(zeroed, 7)
            for r in range(3):
                sp.dma_start(f2[:, 32 * r + 1:32 * r + 1 + COND], io["L0_gnn_f_w2"]).then_inc(noise_in, 16)
                sp.dma_start(f2b[32 * r + 1:32 * r + 1 + COND, :],
                             io["L0_gnn_f_b2"].rearrange("(c a) -> c a", a=1)).then_inc(noise_in, 16)
            sp.dma_start(g[:, 0:TILES - 1, :], io["x"][0:(TILES - 1) * P, :].rearrange("(t p) d -> p t d", p=P)
                         ).then_inc(x_in, 16)
            sp.dma_start(g[0:LAST, TILES - 1, :], io["x"][(TILES - 1) * P:NODES, :]).then_inc(x_in, 16)
            for n, name in enumerate(("bq", "bk", "m_b1")):
                sp.dma_start(bias_rows[16 * n:16 * n + 16, :],
                             io["L0_gnn_" + name].rearrange("l (t f) -> (l t) f", f=P)).then_inc(small_in, 16)
            sp.dma_start(gu_rows[:], io["L0_ffn_gate_up_proj_bias"].rearrange("e (t f) -> (e t) f", f=P)
                         ).then_inc(small_in, 16)
            raw = norm_raw[:].rearrange("c (l m) d -> c l m d", m=MATS)
            for m, name in enumerate(("s1", "b1", "s2", "b2")):
                for r in range(3):
                    sp.dma_start(raw[32 * r + 1:32 * r + 1 + COND, :, m, :],
                                 io[f"L0_gnn_{name}_w"].rearrange("l c d -> c l d")).then_inc(norm_in, 16)
                    sp.dma_start(raw[32 * r:32 * r + 1, :, m, :],
                                 io[f"L0_gnn_{name}_b"].rearrange("(a l) d -> a l d", a=1)).then_inc(norm_in, 16)

        @block.gpsimd
        def _(pool):
            pool.memset(f2[:], 0.0).then_inc(zeroed, 1)
            pool.memset(g[96:P, TILES - 1, :], 0.0).then_inc(zeroed, 1)
            pool.memset(f2b[:], 0.0).then_inc(zeroed, 1)
            pool.memset(norm_raw[:], 0.0).then_inc(zeroed, 1)
            pool.wait_ge(zeroed, 4)
            for r in range(3):
                pool.memset(f2b[32 * r:32 * r + 1, :], 1.0).then_inc(zeroed, 1)
            pool.wait_ge(zeroed, 7)
            pool.iota(columns[:], [[1, HALF]], base=0, channel_multiplier=0,
                      allow_small_or_imprecise_dtypes=True).then_inc(const_ready, 1)
            pool.iota(freq_row[:], [[1, 1]], base=1, channel_multiplier=1).then_inc(const_ready, 1)
            pool.memset(ident[:], 0.0).then_inc(const_ready, 1)
            pool.memset(minus_half[:], -0.5).then_inc(const_ready, 1)
            pool.wait_ge(const_ready, 4)
            pool.affine_select(out=ident[:], in_=ident[:], compare_op=ALU.not_equal, fill=1.0, base=0,
                               pattern=[[-1, P]], channel_multiplier=1).then_inc(const_ready, 1)
            pool.wait_ge(x_step, 2)
            pool.tensor_scalar(rstd[:], mv[:, :, 1], EPS, None, ALU.add).then_inc(rstd_ready, 1)
            pool.wait_ge(rstd_ready, 1)
            pool.tensor_tensor(rstd[:], rstd[:], minus_half[:], ALU.pow).then_inc(rstd_ready, 1)
            with pool.Fori(0, SWEEPS) as s:
                for n in range(NGROUPS):
                    hold(pool, unpacked, s * NGROUPS + (n + 1), adding)
                    rows = counts[:, bass.ds(s * 2, 2), :]
                    pool.tensor_tensor(rows[:, :, 0:HALF], rows[:, :, 0:HALF], packed[:], ALU.add)
                    pool.tensor_tensor(rows[:, :, HALF:NODES], rows[:, :, HALF:NODES],
                                       high[:, :, 0:NODES - HALF], ALU.add).then_inc(added, 1)

        @block.vector
        def _(dve):
            dve.memset(norm_stack[:, LAYERS * MATS:, :], 0.0)
            dve.memset(counts, 0).then_inc(edge_step, 1)
            dve.wait_ge(edges_in, 32)
            dve.tensor_copy(src_rel[:], edges[:, 0, :]).then_inc(edge_step, 1)
            dve.tensor_copy(dst_low[:], edges[:, 1, :]).then_inc(edge_step, 1)
            dve.wait_ge(edge_step, 3)
            dve.tensor_scalar(dst_weight[:], dst_low[:], float(HALF), None, ALU.is_ge).then_inc(edge_step, 1)
            dve.wait_ge(edge_step, 4)
            dve.scalar_tensor_tensor(dst_low[:], dst_weight[:], -float(HALF), dst_low[:], ALU.mult, ALU.add
                                     ).then_inc(edge_step, 1)
            dve.wait_ge(edge_step, 5)
            dve.tensor_scalar(dst_weight[:], dst_weight[:], float(FIELD - 1), 1.0, ALU.mult, ALU.add
                              ).then_inc(edge_step, 1)
            dve.wait_ge(edge_step, 6)
            dve.wait_ge(const_ready, 5)

            step = [0]

            def chain(ins):
                step[0] += 1
                ins.then_inc(cond_step, 1)
                dve.wait_ge(cond_step, step[0])

            chain(dve.tensor_copy(freq[:, 0:1], freq_row[:]))
            chain(dve.tensor_scalar(freq[32:64, 0:1], freq[32:64, 0:1], float(FREQS), None, ALU.subtract))
            chain(dve.tensor_scalar(freq[:, 1:2], freq[:, 0:1], 2.0 * np.pi / BASE_PERIOD, None, ALU.mult))
            dve.memset(freq[:, 2:4], 0.0).then_inc(cond_step, 1)
            step[0] += 1
            dve.wait_ge(cond_step, step[0])
            chain(dve.memset(freq[32:64, 2:3], 0.25))
            chain(dve.memset(freq[32:64, 3:4], np.pi / 2))
            dve.wait_ge(noise_in, 16 * 9)
            chain(dve.tensor_scalar(noise[:], noise[:], freq[:, 1:2], None, ALU.mult))
            chain(dve.tensor_scalar(turns[:], noise[:], 1.0 / (2 * np.pi), freq[:, 2:3], ALU.mult, ALU.add))
            magic = 1.5 * 2.0 ** 23
            chain(dve.tensor_scalar(turns[:], turns[:], magic, None, ALU.add))
            chain(dve.tensor_scalar(turns[:], turns[:], magic, None, ALU.subtract))
            first = 6.28125
            chain(dve.scalar_tensor_tensor(noise[:], turns[:], -first, noise[:], ALU.mult, ALU.add))
            chain(dve.scalar_tensor_tensor(noise[:], turns[:], -(2 * np.pi - first), noise[:], ALU.mult, ALU.add))
            chain(dve.tensor_scalar(noise[:], noise[:], freq[:, 3:4], 3.1415925, ALU.add, ALU.min))
            chain(dve.tensor_scalar(noise[:], noise[:], -3.1415925, None, ALU.max))
            for c, (c0, cn) in enumerate(CHUNKS):
                dve.wait_ge(cond_act, 2 + c)
                dve.scalar_tensor_tensor(hidden[:, c0:c0 + cn], bank[c][0:COND, 0:cn], f1b[:, 0:1],
                                         sig[:, c0:c0 + cn], ALU.add, ALU.mult).then_inc(cond_step, 1)
            step[0] += NCH
            cond_hidden = step[0]
            assert cond_hidden == COND_HIDDEN
            chain(dve.memset(cond_stack[:, NODES:PAD], 0.0))
            for c, (c0, cn) in enumerate(CHUNKS):
                dve.wait_ge(cond_mm, NCH + 1 + c)
                chain(dve.tensor_scalar(cond_stack[:, c0:c0 + cn], bank[3 + c][0:NROWS, 0:cn], f2b[:, 0:1], None,
                                        ALU.add))
                chain(dve.scalar_tensor_tensor(cond_stack[32:64, c0:c0 + cn], bank[3 + c][32:64, 0:cn],
                                               f2b[32:64, 0:1], cond_stack[32:64, c0:c0 + cn],
                                               ALU.add, ALU.subtract))
            dve.wait_ge(x_in, 32)
            for t in range(TILES):
                ins = dve.bn_stats(stats[:, t, :], g[:, t, :])
            ins.then_inc(x_step, 1)
            dve.wait_ge(x_step, 1)
            for t in range(TILES):
                ins = dve.bn_aggr(mv[:, t, :], stats[:, t, :])
            ins.then_inc(x_step, 1)
            dve.wait_ge(rstd_ready, 2)
            for t in range(TILES):
                dve.tensor_scalar(g[:, t, :], g[:, t, :], mv[:, t, 0:1], rstd[:, t:t + 1], ALU.subtract, ALU.mult)
            dve.wait_ge(turned, 2)
            nb = 3 * LAYERS * KT
            dve.tensor_scalar(bias_cols[:], bank[6][:, 0:nb], W_SCALE, None, ALU.mult)
            gu = bank[7][:, 0:P]
            dve.tensor_scalar(gu_cols[:, 0, :], gu, 1.702, None, ALU.mult)
            dve.tensor_scalar(gu_cols[:, 1, :], gu, W_SCALE, None, ALU.mult)
            dve.tensor_scalar(gu_cols[:, 2, :], gu, 1.0, W_SCALE, ALU.add, ALU.mult).then_inc(x_step, 1)
            dve.wait_ge(norm_in, 16 * 24)
            raw = norm_raw[:].rearrange("c (l m) d -> c l m d", m=MATS)
            for r in range(3):
                for m in (0, 2):
                    ins = dve.tensor_scalar(raw[32 * r:32 * r + 1, :, m, :], raw[32 * r:32 * r + 1, :, m, :],
                                            1.0, None, ALU.add)
            ins.then_inc(norm_step, 1)
            dve.wait_ge(norm_step, 1)
            dve.tensor_copy(norm_stack[:, 0:LAYERS * MATS, :], norm_raw[:]).then_inc(norm_step, 1)
            dve.wait_ge(norm_step, 2)
            dve.tensor_tensor(norm_stack[64:96, 0:LAYERS * MATS], norm_raw[64:96], norm_stack[64:96, 0:LAYERS * MATS], ALU.subtract
                              ).then_inc(norm_step, 1)

            def hots(s, n, b):
                for u in range(BLK):
                    j = b * BLK + (n * GROUP + u)
                    dve.wait_ge(hot_free, s * ECOLS + (j + 1))
                    dve.tensor_scalar(src_hot[:, u, :], columns[0:EP, 0:2 * P], src_rel[:, bass.ds(j, 1)], None,
                                      ALU.is_equal)
                    dve.tensor_scalar(dst_hot[:, u, :], columns[0:EP, :], dst_low[:, bass.ds(j, 1)],
                                      dst_weight[:, bass.ds(j, 1)], ALU.is_equal, ALU.mult).then_inc(hot_ready, 1)

            def unpack(s, n):
                base = s * NGROUPS
                dve.wait_ge(counted, base + (n + 1))
                dve.wait_ge(added, base + (n + 1))
                for i in range(2):
                    for h in range(2):
                        ins = dve.tensor_copy(packed[:, i, h * (HALF // 2):(h + 1) * (HALF // 2)],
                                              bank[4 * (n % 2) + 2 * i + h][:, 0:HALF // 2])
                ins.then_inc(count_free, 1)
                dve.wait_ge(count_free, base + (n + 2))
                dve.tensor_scalar(high[:], packed[:], 12, None, ALU.arith_shift_right).then_inc(unpack_step, 1)
                dve.wait_ge(unpack_step, base + (n + 1))
                dve.tensor_scalar(packed[:], packed[:], FIELD - 1, None, ALU.bitwise_and).then_inc(unpacked, 1)

            dve.sem_inc(hot_free, BLK)
            dve.sem_inc(count_free, 1)
            dve.sem_inc(added, 1)
            with dve.Fori(0, SWEEPS) as s:
                for n in range(NGROUPS):
                    hots(s, n, 0)
                    if n:
                        unpack(s, n - 1)
                    with dve.Fori(1, BLKS) as b:
                        hots(s, n, b)
                dve.wait_ge(hot_ready, s * ECOLS + ECOLS)
                dve.tensor_scalar(src_rel[:], src_rel[:], 2.0 * P, None, ALU.subtract).then_inc(table_step, 1)
                dve.wait_ge(table_step, s + 1)
                unpack(s, NGROUPS - 1)
            dve.wait_ge(added, SWEEPS * NGROUPS + 1)
            for i in range(TILES + 1):
                if i < TILES:
                    if i >= 2:
                        dve.wait_ge(logged, i - 1)
                    dve.tensor_scalar(at_least_1[:, i % 2, :], counts[:, i, :], 1.0, None, ALU.max
                                      ).then_inc(clamped, 1)
                if i:
                    t = i - 1
                    dve.wait_ge(clamped, i)
                    dve.tensor_scalar(log_count[:, t, :], counts[:, t, :], 1.0, MASKED, ALU.is_lt, ALU.mult
                                      ).then_inc(table_step, 1)
                    dve.wait_ge(logged, i)
                    dve.wait_ge(table_step, SWEEPS + i)
                    dve.scalar_tensor_tensor(log_count[:, t, :], logs[:, t % 2, :], 1.0 / SCORE,
                                             log_count[:, t, :], ALU.mult, ALU.add)

        @block.scalar
        def _(act):
            act.wait_ge(cond_step, COND_ARGS)
            act.activation(noise[:], noise[:], ACT.Sin).then_inc(cond_act, 1)
            for c, (c0, cn) in enumerate(CHUNKS):
                act.wait_ge(cond_mm, 1 + c)
                act.activation(sig[:, c0:c0 + cn], bank[c][0:COND, 0:cn], ACT.Sigmoid, bias=f1b[:, 0:1]
                               ).then_inc(cond_act, 1)
            for t in range(TILES):
                act.wait_ge(clamped, t + 1)
                if t >= 2:
                    act.wait_ge(table_step, SWEEPS + t)
                act.activation(logs[:, t % 2, :], at_least_1[:, t % 2, :], ACT.Ln).then_inc(logged, 1)

        @block.tensor
        def _(pe):
            pe.wait_ge(const_ready, 5)
            pe.wait_ge(small_in, 64)
            nb = 3 * LAYERS * KT
            pe.transpose(bank[6][:, 0:nb], bias_rows[:], ident[0:nb, 0:nb]).then_inc(turned, 1)
            pe.transpose(bank[7][:, 0:P], gu_rows[:], ident[:]).then_inc(turned, 1)
            pe.wait_ge(noise_in, 16 * 9)
            pe.wait_ge(cond_act, 1)
            for c, (c0, cn) in enumerate(CHUNKS):
                pe.matmul(bank[c][0:COND, 0:cn], f1[:], noise[:, c0:c0 + cn], start=True, stop=True
                          ).then_inc(cond_mm, 1)
            for c, (c0, cn) in enumerate(CHUNKS):
                pe.wait_ge(cond_step, COND_HIDDEN - NCH + 1 + c)
                pe.matmul(bank[3 + c][0:NROWS, 0:cn], f2[:], hidden[:, c0:c0 + cn], start=True, stop=True
                          ).then_inc(cond_mm, 1)
            pe.wait_ge(x_step, 3)

            def count(s, n, b, first=False, last=False):
                for u in range(BLK):
                    j = b * BLK + (n * GROUP + u)
                    pe.wait_ge(hot_ready, s * ECOLS + (j + 1))
                    for i in range(2):
                        for h in range(2):
                            ins = pe.matmul(bank[4 * (n % 2) + 2 * i + h][:, 0:HALF // 2],
                                            src_hot[:, u, i * P:(i + 1) * P],
                                            dst_hot[:, u, h * (HALF // 2):(h + 1) * (HALF // 2)],
                                            start=first and u == 0, stop=last and u == BLK - 1)
                    if last and u == BLK - 1:
                        ins.then_inc(counted, 1)
                        pe.wait_ge(counted, s * NGROUPS + (n + 1))
                        pe.sem_inc(hot_free, 1)
                    else:
                        ins.then_inc(hot_free, 1)

            with pe.Fori(0, SWEEPS) as s:
                for n in range(NGROUPS):
                    pe.wait_ge(count_free, s * NGROUPS + (n + 1 if n == 0 else n))
                    count(s, n, 0, first=True)
                    with pe.Fori(1, BLKS - 1) as b:
                        count(s, n, b)
                    count(s, n, BLKS - 1, last=True)


COND_ARGS = 14
COND_HIDDEN = COND_ARGS + NCH


def attention_layers(nc, io, g, ident, bias_cols, log_count, cond_stack, norm_stack):
    LNG = TILES // 2
    QKV = 2 * NCH + 3
    V_SETS = [range(a, min(a + 4, TILES)) for a in range(0, TILES, 4)]
    T_SETS = [range(a, min(a + 4, TILES)) for a in range(0, TILES, 4)]
    PAIRS = TILES // 2
    LAG = 2
    NP = 4
    W_USES = 7
    with ExitStack() as ctx:
        def sb(name, shape, dt=F32):
            return ctx.enter_context(nc.sbuf_tensor("gnn_" + name, shape, dt))

        def sem(name):
            return ctx.enter_context(nc.semaphore(name))

        bank = [ctx.enter_context(nc.psum_tensor(f"gnn_bank{i}", [P, 512], F32)) for i in range(8)]
        s_bank, t_bank, o_bank = bank[0:3], bank[3:6], bank[6:8]
        yT = sb("yT", [P, 2, KT, PAD], F16)
        qk = sb("qk", [P, 2, 2, PAD], F16)
        v = sb("v", [P, 2, TILES, DH], F16)
        room = sb("room", [P, 3, 512])
        probs = sb("probs", [P, NP, PAD])
        pT = sb("pT", [P, 2, 2, TILES, 2, P], F16)
        oT = sb("oT", [P, 2, HEADS, PAD], F16)
        raw = sb("raw", [P, KT * D])
        w_qkv = sb("w_qkv", [P, 2, 3, KT, DH], F16)
        w_o = sb("w_o", [P, 2, KT, D], F16)
        bv_rows = sb("bv_rows", [P, D])
        out_bias = sb("out_bias", [P, D])
        qk_bias = sb("qk_bias", [P, 2])
        hidden_bias = sb("hidden_bias", [P, KT])
        best = sb("best", [P, 2, NCH])
        shift = sb("shift", [P, 2])
        total = sb("total", [P, 2])
        inverse = sb("inverse", [P, 2])
        stats = sb("stats", [P, 2, 6])
        mv = sb("mv", [P, 2, 2])
        rstd = sb("rstd", [P, 2])
        minus_half = sb("minus_half", [P, 2])
        diagonal = sb("diagonal", [P, NP, P])
        head_w = [w_qkv[:, a].rearrange("p w k c -> p (w k c)") for a in range(2)]

        def square_w(w):
            return [w[:, a].rearrange("p k d -> p (k d)") for a in range(2)]

        y = qk[:].rearrange("p a b n -> p (a b n)").bitcast(F32)[:, 0:4 * D].rearrange("p (s d) -> p s d", s=4)
        hT = probs[:].rearrange("p s n -> p (s n)").bitcast(F16).rearrange("p (a t n) -> p a t n", a=2, t=KT)
        pT_flat = pT[:].rearrange("p s a t b n -> p (s a t b n)")
        w_m1 = pT_flat[:, 0:2 * KT * D].rearrange("p (a k d) -> p a k d", a=2, k=KT)
        w_m2 = pT_flat[:, 2 * KT * D:4 * KT * D].rearrange("p (a k d) -> p a k d", a=2, k=KT)

        names = ("start passed_pool passed_dve passed_act passed_pe recip_ready qk_lo raw_in w_scaled w_hi w_ready bv_in bv_ready ob_in ob_free ob_added "
                 "stats_ready mv_ready var_eps rstd_ready norm_mm y_part y_ready y_turned y_hi y_lo "
                 "res_ready res_free bias_ready proj_ready qkv_hi v_sum v_lo s_ready best_ready "
                 "shift_ready exp_ready inv_ready p_ready p_turned p_hi p_lo o_ready o_hi o_lo "
                 "mlp_ready hidden h_zero h_hi h_ready")
        S = {n: sem("g_" + n) for n in names.split()}
        block = ctx.enter_context(nc.Block())

        @block.sync
        def _(sp):
            def load(L, use, dst, src):
                sp.wait_ge(S["w_ready"], L * W_USES + (use + 1))
                for a, b in zip(dst, src):
                    sp.dma_start(a, b).then_inc(S["raw_in"], 16)

            def square(name, L):
                return io["L0_gnn_" + name][bass.ds(L, 1), :, :].rearrange("a (k p) n -> p (a k) n", p=P)

            with sp.Fori(0, LAYERS) as L:
                for h in range(HEADS):
                    load(L, h, [raw[:, n * KT * DH:(n + 1) * KT * DH].rearrange("p (k c) -> p k c", k=KT)
                                          for n in range(3)],
                         [io["L0_gnn_" + w][bass.ds(L, 1), :, h * DH:(h + 1) * DH]
                          .rearrange("a (k p) c -> p (a k) c", p=P) for w in ("wq", "wk", "wv")])
                    if h == 0:
                        sp.wait_ge(S["res_free"], L * 2 * TILES + 1)
                        sp.dma_start(bv_rows[:], io["L0_gnn_bv"][bass.ds(L, 1), :].partition_broadcast(P)
                                     .rearrange("p a n -> p (a n)")).then_inc(S["bv_in"], 16)
                        sp.wait_ge(S["ob_free"], L * 2 + 1)
                        sp.dma_start(out_bias[:], io["L0_gnn_bo"][bass.ds(L, 1), :].partition_broadcast(P)
                                     .rearrange("p a n -> p (a n)")).then_inc(S["ob_in"], 16)
                load(L, 4, [raw[:].rearrange("p (k n) -> p k n", k=KT)], [square("wo", L)])
                sp.wait_ge(S["ob_free"], L * 2 + 2)
                sp.dma_start(out_bias[:], io["L0_gnn_m_b2"][bass.ds(L, 1), :].partition_broadcast(P)
                             .rearrange("p a n -> p (a n)")).then_inc(S["ob_in"], 16)
                load(L, 5, [raw[:].rearrange("p (k n) -> p k n", k=KT)], [square("m_w1", L)])
                load(L, 6, [raw[:].rearrange("p (k n) -> p k n", k=KT)], [square("m_w2", L)])
        RAW_IN = HEADS * 48 + 3 * 16

        @block.gpsimd
        def _(pool):
            pool.memset(minus_half[:], -0.5).then_inc(S["start"], 1)
            pool.sem_inc(S["w_ready"], 1)
            pool.sem_inc(S["ob_free"], 1)
            pool.wait_ge(S["start"], 1)

            def scale(L, use, raw_in, n):
                hold(pool, S["raw_in"], L * RAW_IN + raw_in, S["passed_pool"])
                pool.tensor_scalar(raw[:, 0:n], raw[:, 0:n], W_SCALE, None, ALU.mult).then_inc(S["w_scaled"], 1)

            def rest_part(L, use, n, hi, lo):
                pool.wait_ge(S["w_hi"], L * W_USES + (use + 1))
                pool.tensor_tensor(lo, raw[:, 0:n], hi, ALU.subtract).then_inc(S["w_ready"], 1)

            def rsqrt(L, first, group):
                n = L * 2 * LNG + (first + group + 1)
                hold(pool, S["mv_ready"], n, S["passed_pool"])
                pool.tensor_scalar(rstd[:], mv[:, :, 1], EPS, None, ALU.add).then_inc(S["var_eps"], 1)
                pool.wait_ge(S["var_eps"], n)
                pool.tensor_tensor(rstd[:], rstd[:], minus_half[:], ALU.pow).then_inc(S["rstd_ready"], 1)

            def head(L, h, use, raw_in, n, hi, lo):
                for t in range(TILES):
                    hold(pool, S["inv_ready"], L * HEADS * TILES + (h * TILES + t + 1), S["passed_pool"])
                    pool.tensor_scalar(diagonal[:, t % NP, :], ident[:], inverse[:, t % 2:t % 2 + 1], None, ALU.mult
                                       ).then_inc(S["p_ready"], 1)
                    if t == 1:
                        scale(L, use, raw_in, n)
                    if t == 5:
                        rest_part(L, use, n, hi, lo)

            with pool.Fori(0, LAYERS) as L:
                scale(L, 0, 48, 3 * KT * DH)
                hold(pool, S["w_scaled"], L * W_USES + 1, S["passed_pool"])
                pool.tensor_copy(head_w[0], raw[:, 0:3 * KT * DH]).then_inc(S["w_hi"], 1)
                rest_part(L, 0, 3 * KT * DH, *head_w)
                for n in range(LNG):
                    rsqrt(L, 0, n)
                hold(pool, S["bv_in"], L * 16 + 16, S["passed_pool"])
                pool.tensor_scalar(bv_rows[:], bv_rows[:], W_SCALE, None, ALU.mult).then_inc(S["bv_ready"], 1)
                pool.wait_ge(S["ob_in"], L * 32 + 16)
                pool.wait_ge(S["y_ready"], L * 2 * TILES + TILES)
                for t in range(TILES):
                    ins = pool.tensor_tensor(g[:, t, :], g[:, t, :], out_bias[:], ALU.add)
                ins.then_inc(S["ob_added"], 1)
                pool.wait_ge(S["ob_added"], L * 2 + 1)
                pool.sem_inc(S["ob_free"], 1)
                with pool.Fori(0, HEADS - 1) as H:
                    head(L, H, H + 1, H * 48 + 96, 3 * KT * DH, *head_w)
                head(L, HEADS - 1, HEADS, HEADS * 48 + 16, KT * D, *square_w(w_o))
                scale(L, 5, HEADS * 48 + 32, KT * D)
                hold(pool, S["p_turned"], L * HEADS * 3 * TILES + HEADS * 3 * TILES, S["passed_pool"])
                pool.memset(hT[:, :, :, NODES:PAD], 0.0).then_inc(S["h_zero"], 1)
                for n in range(LNG):
                    rsqrt(L, LNG, n)
                    if n == 0:
                        rest_part(L, 5, KT * D, *square_w(w_m1))
                    if n == 2:
                        scale(L, 6, HEADS * 48 + 48, KT * D)
                    if n == 3:
                        rest_part(L, 6, KT * D, *square_w(w_m2))
                pool.wait_ge(S["ob_in"], L * 32 + 32)
                pool.wait_ge(S["y_ready"], L * 2 * TILES + 2 * TILES)
                for t in range(TILES):
                    ins = pool.tensor_tensor(g[:, t, :], g[:, t, :], out_bias[:], ALU.add)
                ins.then_inc(S["ob_added"], 1)
                pool.wait_ge(S["ob_added"], L * 2 + 2)
                pool.sem_inc(S["ob_free"], 1)
            for n in range(LNG):
                rsqrt(LAYERS, 0, n)

        @block.vector
        def _(dve):
            dve.sem_inc(S["res_free"], 2)

            def norm_front(L, first, n):
                group = L * 2 * LNG + (first * LNG + n + 1)
                for j in range(2):
                    ins = dve.bn_stats(stats[:, j, :], g[:, 2 * n + j, :])
                ins.then_inc(S["stats_ready"], 1)
                hold(dve, S["stats_ready"], group, S["passed_dve"])
                for j in range(2):
                    ins = dve.bn_aggr(mv[:, j, :], stats[:, j, :])
                ins.then_inc(S["mv_ready"], 1)
                dve.wait_ge(S["mv_ready"], group)
                for j in range(2):
                    tile = L * 2 * TILES + (first * TILES + 2 * n + j + 1)
                    dve.wait_ge(S["norm_mm"], tile)
                    dve.scalar_tensor_tensor(y[:, 2 * (n % 2) + j, :], g[:, 2 * n + j, :], mv[:, j, 0:1],
                                             bank[j][:], ALU.subtract, ALU.mult).then_inc(S["y_part"], 1)
                dve.wait_ge(S["rstd_ready"], group)
                for j in range(2):
                    tile = L * 2 * TILES + (first * TILES + 2 * n + j + 1)
                    dve.wait_ge(S["y_part"], tile)
                    slot = y[:, 2 * (n % 2) + j, :]
                    dve.scalar_tensor_tensor(slot, slot, rstd[:, j:j + 1], bank[2 + j][:], ALU.mult, ALU.add
                                             ).then_inc(S["y_ready"], 1)

            def norm_back(L, first, n):
                for j in range(2):
                    t = 2 * n + j
                    tile = L * 2 * TILES + (first * TILES + t + 1)
                    dve.wait_ge(S["y_hi"], tile)
                    dve.tensor_tensor(yT[:, 1, :, t * P:(t + 1) * P],
                                      bank[4 + j][:].rearrange("p (k n) -> p k n", k=KT),
                                      yT[:, 0, :, t * P:(t + 1) * P], ALU.subtract).then_inc(S["y_lo"], 1)

            def residual(L, first, t):
                n = L * 2 * TILES + (first * TILES + t + 1)
                dve.wait_ge(S["res_ready"], n)
                dve.scalar_tensor_tensor(g[:, t, :], bank[6 + t % 2][:], BACK, g[:, t, :], ALU.mult, ALU.add
                                         ).then_inc(S["res_free"], 1)

            def head_bias(it):
                dve.tensor_copy(qk_bias[:, 0:1], bias_cols[:, bass.ds(it, 1)])
                dve.tensor_copy(qk_bias[:, 1:2], bias_cols[:, bass.ds(it + LAYERS * KT, 1)]
                                ).then_inc(S["bias_ready"], 1)

            def project_rest(it, w):
                for c, (c0, cn) in enumerate(CHUNKS):
                    dve.wait_ge(S["qkv_hi"], it * QKV + ((1 - w) * NCH + c + 1))
                    dve.scalar_tensor_tensor(qk[:, w, 1, c0:c0 + cn], s_bank[c][:, 0:cn], qk_bias[:, w:w + 1],
                                             qk[:, w, 0, c0:c0 + cn], ALU.add, ALU.subtract
                                             ).then_inc(S["qk_lo"], 1)

            def project_v(L, H, it):
                dve.wait_ge(S["bv_ready"], L + 1)
                for c, tiles in enumerate(V_SETS):
                    n = len(tiles)
                    dve.wait_ge(S["proj_ready"], it * QKV + (2 * NCH + c + 1))
                    dve.tensor_tensor(room[:, c, 0:n * DH].rearrange("p (t d) -> p t d", d=DH),
                                      t_bank[c][:, 0:n * DH].rearrange("p (t d) -> p t d", d=DH),
                                      bv_rows[:, bass.ds(H * DH, DH)].unsqueeze(1).to_broadcast([P, n, DH]),
                                      ALU.add).then_inc(S["v_sum"], 1)
                dve.wait_ge(S["qkv_hi"], it * QKV + QKV)
                for c, tiles in enumerate(V_SETS):
                    n = len(tiles)
                    dve.tensor_tensor(v[:, 1, tiles[0]:tiles[0] + n, :],
                                      room[:, c, 0:n * DH].rearrange("p (t d) -> p t d", d=DH),
                                      v[:, 0, tiles[0]:tiles[0] + n, :], ALU.subtract).then_inc(S["v_lo"], 1)

            def head(L, H, more):
                it = L * HEADS + H
                def scores_max(t):
                    for c, (c0, cn) in enumerate(CHUNKS):
                        hold(dve, S["s_ready"], it * NCH * TILES + (NCH * t + c + 1), S["passed_dve"])
                        if c:
                            hold(dve, S["best_ready"], it * NCH * TILES + (NCH * t + c), S["passed_dve"])
                        dve.tensor_tensor_reduce(probs[:, t % NP, c0:c0 + cn], s_bank[c][:, 0:cn],
                                                 log_count[:, t, c0:c0 + cn], 1.0,
                                                 best[:, t % 2, c - 1:c] if c else 2 * MASKED, ALU.add, ALU.max,
                                                 best[:, t % 2, c:c + 1]).then_inc(S["best_ready"], 1)
                    dve.wait_ge(S["best_ready"], it * NCH * TILES + (NCH * t + NCH))
                    dve.tensor_scalar(shift[:, t % 2:t % 2 + 1], best[:, t % 2, NCH - 1:NCH], -SCORE, MAX_SHIFT,
                                      ALU.mult, ALU.min).then_inc(S["shift_ready"], 1)

                def inverse_sum(t):
                    dve.wait_ge(S["exp_ready"], it * TILES + (t + 1))
                    slot = inverse[:, t % 2:t % 2 + 1]
                    dve.tensor_scalar(total[:, t % 2:t % 2 + 1], total[:, t % 2:t % 2 + 1], LEAST_SUM, None,
                                      ALU.max).then_inc(S["recip_ready"], 1)
                    dve.wait_ge(S["recip_ready"], it * TILES + (t + 1))
                    dve.reciprocal(slot, total[:, t % 2:t % 2 + 1]).then_inc(S["inv_ready"], 1)

                def turned_rest(t):
                    for c, blocks in enumerate(T_SETS):
                        n = len(blocks)
                        dve.wait_ge(S["p_hi"], it * 3 * TILES + (3 * t + c + 1))
                        a = pT[:, (t // 2) % 2, :, blocks[0]:blocks[0] + n, t % 2, :]
                        dve.tensor_tensor(a[:, 1], t_bank[c][:, 0:n * P].rearrange("p (b n) -> p b n", n=P),
                                          a[:, 0], ALU.subtract).then_inc(S["p_lo"], 1)

                def out_rest(pair):
                    dve.wait_ge(S["o_hi"], it * PAIRS + (pair + 1))
                    dst = oT[:, :, bass.ds(H, 1), pair * 2 * P:(pair + 1) * 2 * P]
                    dve.tensor_tensor(dst[:, 1, 0], o_bank[pair % 2][:, 0:2 * P], dst[:, 0, 0], ALU.subtract
                                      ).then_inc(S["o_lo"], 1)

                for i in range(TILES + LAG):
                    if i < TILES:
                        scores_max(i)
                    if i == 0:
                        project_v(L, H, it)
                    if 1 <= i <= TILES:
                        inverse_sum(i - 1)
                    if more and i == TILES:
                        head_bias(it + 1)
                        project_rest(it + 1, 1)
                    if more and i == TILES + 1:
                        project_rest(it + 1, 0)
                    t = i - LAG
                    if t >= 0:
                        turned_rest(t)
                    if t >= 3 and t % 2 == 1:
                        out_rest((t - 3) // 2)
                out_rest(PAIRS - 1)
            for n in range(LNG + 1):
                if n < LNG:
                    norm_front(0, 0, n)
                if n:
                    norm_back(0, 0, n - 1)
            with dve.Fori(0, LAYERS) as L:
                dve.tensor_copy(hidden_bias[:], bias_cols[:, bass.ds(L * KT + 2 * LAYERS * KT, KT)]
                                ).then_inc(S["bias_ready"], 1)
                dve.memset(qk[:, :, :, NODES:PAD], 0.0)
                dve.memset(probs[:, :, NODES:PAD], 0.0)
                head_bias(L * HEADS)
                dve.wait_ge(S["bias_ready"], L * (HEADS + 1) + 2)
                project_rest(L * HEADS, 1)
                project_rest(L * HEADS, 0)
                with dve.Fori(0, HEADS - 1) as H:
                    head(L, H, True)
                head(L, HEADS - 1, False)

                for n in range(LNG + 1):
                    if n < LNG:
                        if n == 0:
                            dve.wait_ge(S["ob_added"], L * 2 + 1)
                        residual(L, 0, 2 * n)
                        residual(L, 0, 2 * n + 1)
                        dve.wait_ge(S["res_free"], L * 2 * TILES + (2 * n + 4))
                        norm_front(L, 1, n)
                    if n:
                        norm_back(L, 1, n - 1)
                dve.wait_ge(S["h_zero"], L + 1)
                for n in range(KT * NCH + 1):
                    if n < KT * NCH:
                        f, (c0, cn) = n // NCH, CHUNKS[n % NCH]
                        if n >= 3:
                            dve.wait_ge(S["h_ready"], L * KT * NCH + (n - 2))
                        dve.wait_ge(S["mlp_ready"], L * KT * NCH + (n + 1))
                        dve.tensor_scalar(room[:, n % 3, 0:cn], bank[n % 4][:, 0:cn], hidden_bias[:, f:f + 1], 0.0,
                                          ALU.add, ALU.max).then_inc(S["hidden"], 1)
                    if n:
                        f, (c0, cn) = (n - 1) // NCH, CHUNKS[(n - 1) % NCH]
                        dve.wait_ge(S["h_hi"], L * KT * NCH + n)
                        dve.tensor_tensor(hT[:, 1, f, c0:c0 + cn], room[:, (n - 1) % 3, 0:cn],
                                          hT[:, 0, f, c0:c0 + cn], ALU.subtract).then_inc(S["h_ready"], 1)
                dve.wait_ge(S["ob_added"], L * 2 + 2)
                for n in range(LNG + 1):
                    if n < LNG:
                        residual(L, 1, 2 * n)
                        residual(L, 1, 2 * n + 1)
                        dve.wait_ge(S["res_free"], L * 2 * TILES + (TILES + 2 * n + 4))
                        norm_front(L + 1, 0, n)
                    if n:
                        norm_back(L + 1, 0, n - 1)

        @block.scalar
        def _(act):
            def norm_hi(L, first, t):
                act.wait_ge(S["y_turned"], L * 2 * TILES + (first * TILES + t + 1))
                act.activation(yT[:, 0, :, t * P:(t + 1) * P], bank[4 + t % 2][:].rearrange("p (k n) -> p k n", k=KT),
                               ACT.Copy).then_inc(S["y_hi"], 1)

            def project_hi(it, w):
                for c, (c0, cn) in enumerate(CHUNKS):
                    act.wait_ge(S["proj_ready"], it * QKV + ((1 - w) * NCH + c + 1))
                    act.activation(qk[:, w, 0, c0:c0 + cn], s_bank[c][:, 0:cn], ACT.Identity,
                                   bias=qk_bias[:, w:w + 1]).then_inc(S["qkv_hi"], 1)

            def project_v_hi(it):
                for c, tiles in enumerate(V_SETS):
                    n = len(tiles)
                    act.wait_ge(S["v_sum"], it * 3 + (c + 1))
                    act.activation(v[:, 0, tiles[0]:tiles[0] + n, :],
                                   room[:, c, 0:n * DH].rearrange("p (t d) -> p t d", d=DH), ACT.Copy
                                   ).then_inc(S["qkv_hi"], 1)

            def weights_hi(L, use, n, hi):
                act.wait_ge(S["w_scaled"], L * W_USES + (use + 1))
                act.activation(hi, raw[:, 0:n], ACT.Copy).then_inc(S["w_hi"], 1)

            def head(L, H, more, next_w):
                it = L * HEADS + H

                def turned_hi(t):
                    for c, blocks in enumerate(T_SETS):
                        n = len(blocks)
                        act.wait_ge(S["p_turned"], it * 3 * TILES + (3 * t + c + 1))
                        act.activation(pT[:, (t // 2) % 2, 0, blocks[0]:blocks[0] + n, t % 2, :],
                                       t_bank[c][:, 0:n * P].rearrange("p (b n) -> p b n", n=P), ACT.Copy
                                       ).then_inc(S["p_hi"], 1)

                def out_hi(pair):
                    hold(act, S["o_ready"], it * PAIRS + (pair + 1), S["passed_act"])
                    act.activation(oT[:, 0, bass.ds(H, 1), pair * 2 * P:(pair + 1) * 2 * P],
                                   o_bank[pair % 2][:, 0:2 * P].unsqueeze(1), ACT.Copy).then_inc(S["o_hi"], 1)

                for i in range(TILES + LAG):
                    if i < TILES:
                        act.wait_ge(S["shift_ready"], it * TILES + (i + 1))
                        act.activation(probs[:, i % NP, 0:NODES], probs[:, i % NP, 0:NODES], ACT.Exp,
                                       bias=shift[:, i % 2:i % 2 + 1], scale=SCORE,
                                       accum_out=total[:, i % 2:i % 2 + 1]).then_inc(S["exp_ready"], 1)
                    if i == 0:
                        project_v_hi(it)
                    if more and i == TILES:
                        act.wait_ge(S["bias_ready"], it + L + 3)
                        project_hi(it + 1, 1)
                    if more and i == TILES + 1:
                        project_hi(it + 1, 0)
                    t = i - LAG
                    if t >= 0:
                        turned_hi(t)
                    if t >= 3 and t % 2 == 1:
                        out_hi((t - 3) // 2)
                    if i == 5:
                        weights_hi(L, H + 1, *next_w)
                out_hi(PAIRS - 1)

            for t in range(TILES):
                norm_hi(0, 0, t)
            with act.Fori(0, LAYERS) as L:
                act.wait_ge(S["bias_ready"], L * (HEADS + 1) + 2)
                project_hi(L * HEADS, 1)
                project_hi(L * HEADS, 0)
                with act.Fori(0, HEADS - 1) as H:
                    head(L, H, True, (3 * KT * DH, head_w[0]))
                head(L, HEADS - 1, False, (KT * D, square_w(w_o)[0]))
                weights_hi(L, 5, KT * D, square_w(w_m1)[0])
                for t in range(TILES):
                    norm_hi(L, 1, t)
                    if t == 5:
                        weights_hi(L, 6, KT * D, square_w(w_m2)[0])
                for n in range(KT * NCH):
                    f, (c0, cn) = n // NCH, CHUNKS[n % NCH]
                    act.wait_ge(S["hidden"], L * KT * NCH + (n + 1))
                    act.activation(hT[:, 0, f, c0:c0 + cn], room[:, n % 3, 0:cn], ACT.Copy
                                   ).then_inc(S["h_hi"], 1)
                for t in range(TILES):
                    norm_hi(L + 1, 0, t)

        @block.tensor
        def _(pe):
            def norm_weights(L, first, t):
                if t >= 2:
                    hold(pe, S["y_ready"], L * 2 * TILES + (first * TILES + t - 1), S["passed_pe"])
                for m in range(2):
                    ins = pe.matmul(bank[2 * m + t % 2][:], cond_stack[:, t * P:(t + 1) * P],
                                    norm_stack[:, bass.ds(L * MATS + (2 * first + m), 1), :]
                                    .rearrange("c a d -> c (a d)"), start=True, stop=True)
                ins.then_inc(S["norm_mm"], 1)

            def norm_turn(L, first, t, start=False):
                n = L * 2 * TILES + (first * TILES + t)
                pe.wait_ge(S["y_ready"], n + 1)
                if not start or t >= 2:
                    pe.wait_ge(S["y_lo"], n - 1)
                for k in range(KT):
                    ins = pe.transpose(bank[4 + t % 2][:, k * P:(k + 1) * P], y[:, t % 4, k * P:(k + 1) * P], ident[:])
                ins.then_inc(S["y_turned"], 1)

            def project(L, H, it, w):
                if w:
                    pe.wait_ge(S["w_ready"], L * W_USES + (H + 2))
                for c, (c0, cn) in enumerate(CHUNKS):
                    if not w:
                        pe.wait_ge(S["qk_lo"], it * 2 * NCH + (c + 1))
                    elif not (isinstance(H, int) and H == 0):
                        pe.wait_ge(S["best_ready"], (it - 1) * NCH * TILES + (NCH * (TILES - 1) + c + 1))
                    split_matmuls(pe, s_bank[c][:, 0:cn], lambda a, k: w_qkv[:, a, w, k, :],
                                  lambda b, k: yT[:, b, k, c0:c0 + cn], KT).then_inc(S["proj_ready"], 1)

            def project_v(it):
                for c, tiles in enumerate(V_SETS):
                    for j, t in enumerate(tiles):
                        ins = split_matmuls(pe, t_bank[c][:, j * DH:(j + 1) * DH],
                                            lambda a, k: yT[:, a, k, t * P:(t + 1) * P],
                                            lambda b, k: w_qkv[:, b, 2, k, :], KT)
                    ins.then_inc(S["proj_ready"], 1)

            def head(L, H, more):
                it = L * HEADS + H

                def score(t):
                    for c, (c0, cn) in enumerate(CHUNKS):
                        if t:
                            pe.wait_ge(S["best_ready"], it * NCH * TILES + (NCH * (t - 1) + c + 1))
                        else:
                            pe.wait_ge(S["qk_lo"], it * 2 * NCH + 2 * NCH)
                        split_matmuls(pe, s_bank[c][:, 0:cn], lambda a, k: qk[:, 0, a, t * P:(t + 1) * P],
                                 lambda b, k: qk[:, 1, b, c0:c0 + cn], 1).then_inc(S["s_ready"], 1)

                def turn(t):
                    pe.wait_ge(S["p_ready"], it * TILES + (t + 1))
                    for c, blocks in enumerate(T_SETS):
                        if t:
                            pe.wait_ge(S["p_lo"], it * 3 * TILES + (3 * (t - 1) + c + 1))
                        else:
                            pe.wait_ge(S["v_sum"], it * 3 + (c + 1))
                        for j, b in enumerate(blocks):
                            ins = pe.matmul(t_bank[c][:, j * P:(j + 1) * P], probs[:, t % NP, b * P:(b + 1) * P],
                                            diagonal[:, t % NP, :], start=True, stop=True)
                        ins.then_inc(S["p_turned"], 1)

                def values(pair):
                    pe.wait_ge(S["p_lo"], it * 3 * TILES + 3 * (2 * pair + 2))
                    if pair == 0:
                        pe.wait_ge(S["v_lo"], it * 3 + 3)
                    if pair >= 2:
                        pe.wait_ge(S["o_lo"], it * PAIRS + (pair - 1))
                    split_matmuls(pe, o_bank[pair % 2][:, 0:2 * P], lambda a, k: v[:, a, k, :],
                             lambda b, k: pT[:, pair % 2, b, k, :, :].rearrange("p s n -> p (s n)"), TILES
                             ).then_inc(S["o_ready"], 1)

                for i in range(TILES + LAG):
                    if i < TILES:
                        score(i)
                    if i == 0:
                        project_v(it)
                    if more and i == TILES:
                        project(L, H + 1, it + 1, 1)
                    if more and i == TILES + 1:
                        project(L, H + 1, it + 1, 0)
                    t = i - LAG
                    if t >= 0:
                        turn(t)
                    if t >= 2 and t % 2 == 0:
                        values(t // 2 - 1)
                values(PAIRS - 1)
                pe.wait_ge(S["o_lo"], it * PAIRS + PAIRS)

            for n in range(LNG + 1):
                if n < LNG:
                    norm_weights(0, 0, 2 * n)
                    norm_weights(0, 0, 2 * n + 1)
                if n:
                    norm_turn(0, 0, 2 * n - 2, start=True)
                    norm_turn(0, 0, 2 * n - 1, start=True)
            with pe.Fori(0, LAYERS) as L:
                pe.wait_ge(S["y_lo"], L * 2 * TILES + TILES)
                project(L, 0, L * HEADS, 1)
                project(L, 0, L * HEADS, 0)
                with pe.Fori(0, HEADS - 1) as H:
                    head(L, H, True)
                head(L, HEADS - 1, False)

                pe.wait_ge(S["w_ready"], L * W_USES + 6)
                for n in range(LNG + 1):
                    if n < LNG:
                        for j in range(2):
                            t = 2 * n + j
                            pe.wait_ge(S["res_free"], L * 2 * TILES + (t + 1))
                            split_matmuls(pe, bank[6 + j][:], lambda a, k: oT[:, a, k, t * P:(t + 1) * P],
                                     lambda b, k: w_o[:, b, k, :], HEADS).then_inc(S["res_ready"], 1)
                            norm_weights(L, 1, t)
                    if n:
                        norm_turn(L, 1, 2 * n - 2)
                        norm_turn(L, 1, 2 * n - 1)
                pe.wait_ge(S["y_lo"], L * 2 * TILES + 2 * TILES)
                pe.wait_ge(S["w_ready"], L * W_USES + 7)
                for n in range(KT * NCH):
                    f, (c0, cn) = n // NCH, CHUNKS[n % NCH]
                    if n >= 4:
                        pe.wait_ge(S["hidden"], L * KT * NCH + (n - 3))
                    split_matmuls(pe, bank[n % 4][:, 0:cn], lambda a, k: w_m1[:, a, k, f * P:(f + 1) * P],
                             lambda b, k: yT[:, b, k, c0:c0 + cn], KT).then_inc(S["mlp_ready"], 1)
                pe.wait_ge(S["h_ready"], L * KT * NCH + KT * NCH)
                pe.wait_ge(S["w_ready"], L * W_USES + 8)
                for n in range(LNG + 1):
                    if n < LNG:
                        for j in range(2):
                            t = 2 * n + j
                            pe.wait_ge(S["res_free"], L * 2 * TILES + (TILES + t + 1))
                            split_matmuls(pe, bank[6 + j][:], lambda a, k: hT[:, a, k, t * P:(t + 1) * P],
                                          lambda b, k: w_m2[:, b, k, :], KT).then_inc(S["res_ready"], 1)
                            norm_weights(L + 1, 0, t)
                    if n:
                        norm_turn(L + 1, 0, 2 * n - 2)
                        norm_turn(L + 1, 0, 2 * n - 1)


def experts(nc, io, g, ident, gu_cols):
    I_T = FF // P
    ROUND = 2
    with ExitStack() as ctx:
        def sb(name, shape, dt=F32):
            return ctx.enter_context(nc.sbuf_tensor("moe_" + name, shape, dt))

        bank = [ctx.enter_context(nc.psum_tensor(f"moe_bank{i}", [P, 512], F32)) for i in range(8)]
        x_in = sb("x", [P, TILES, D])
        xT = sb("xT", [P, 2, KT, PAD], F16)
        acc = sb("acc", [P, TILES, D])
        actT = sb("actT", [P, 2, I_T, PAD], F16)
        y = sb("y", [P, 2, D])
        raw_gu = sb("raw_gu", [P, 2, 2, KT, P])
        w_gu = sb("w_gu", [P, ROUND, 2, 2, KT, P], F16)
        raw_down = sb("raw_down", [P, 2, D])
        w_down = sb("w_down", [P, 2, I_T, D], F16)
        sig = sb("sig", [P, 2, 512])
        gated = sb("gated", [P, 2, 512])
        raw_router = sb("raw_router", [P, KT, EXPERTS])
        w_router = sb("w_router", [P, 2, KT, EXPERTS], F16)
        router_b = sb("router_b", [P, EXPERTS])
        down_b = sb("down_b", [EXPERTS, D])
        logits = sb("logits", [P, TILES, EXPERTS])
        top = sb("top", [P, TILES])
        weight = sb("weight", [P, TILES, EXPERTS])
        share = sb("share", [P, TILES, EXPERTS])
        weightT = sb("weightT", [EXPERTS, PAD])
        greater = sb("greater", [P, TILES, EXPERTS, EXPERTS])
        equal = sb("equal", [P, TILES, EXPERTS, EXPERTS])
        before = sb("before", [P, EXPERTS, EXPERTS])
        rank = sb("rank", [P, TILES, EXPERTS])
        whole = sb("whole", [P, TILES])
        stats = sb("stats", [P, TILES, 6])
        mv = sb("mv", [P, TILES, 2])
        rstd = sb("rstd", [P, TILES])
        minus_half = sb("minus_half", [P, TILES])

        names = ("start x_in small_in raw_in_0 raw_in_1 raw_scaled raw_hi w_ready down_in_0 down_in_1 down_scaled down_hi "
                 "down_ready x_step rstd_step y_ready y_turned y_hi y_lo router_step router_mm route route_exp "
                 "weight_turned bias_mm acc_ready pair_ready sig_ready gated_ready act_ready act_hi act_lo "
                 "down_mm down_free out_done passed_pool passed_dve passed_act passed_pe")
        S = {n: ctx.enter_context(nc.semaphore("m_" + n)) for n in names.split()}
        block = ctx.enter_context(nc.Block())
        PAIRS = I_T * NCH

        @block.sync
        def _(sp):
            sp.wait_ge(S["start"], 1)
            sp.dma_start(x_in[:, 0:TILES - 1, :], io["x"][0:(TILES - 1) * P, :].rearrange("(t p) d -> p t d", p=P)
                         ).then_inc(S["x_in"], 16)
            sp.dma_start(x_in[0:LAST, TILES - 1, :], io["x"][(TILES - 1) * P:NODES, :]).then_inc(S["x_in"], 16)
            sp.dma_start(raw_router[:], io["L0_ffn_router_w"].rearrange("(k p) e -> p k e", p=P)
                         ).then_inc(S["small_in"], 16)
            sp.dma_start(router_b[:], io["L0_ffn_router_b"].rearrange("(a e) -> a e", a=1).partition_broadcast(P)
                         .rearrange("p a e -> p (a e)")).then_inc(S["small_in"], 16)
            sp.dma_start(down_b[:], io["L0_ffn_down_proj_bias"]).then_inc(S["small_in"], 16)
            with sp.Fori(0, EXPERTS) as e:
                gate_up = io["L0_ffn_gate_up_proj"][bass.ds(e, 1), :, :].rearrange("a (k p) n -> p (a k) n", p=P)
                down = io["L0_ffn_down_proj"][bass.ds(e, 1), :, :].rearrange("a (i p) n -> p (a i) n", p=P)
                for i in range(I_T + 1):
                    if i < I_T:
                        sp.wait_ge(S["w_ready"], e * I_T + (i + 1))
                        for u in range(2):
                            sp.dma_start(raw_gu[:, i % 2, u], gate_up[:, :, u * FF + i * P:u * FF + (i + 1) * P]
                                         ).then_inc(S[f"raw_in_{i % 2}"], 16)
                    if i:
                        sp.wait_ge(S["down_ready"], e * I_T + i)
                        sp.dma_start(raw_down[:, (i - 1) % 2, :], down[:, i - 1, :]
                                     ).then_inc(S[f"down_in_{(i - 1) % 2}"], 16)
            sp.wait_ge(S["down_free"], (EXPERTS + 1) * TILES)
            sp.dma_start(io["out"][0:(TILES - 1) * P, :].rearrange("(t p) d -> p t d", p=P), acc[:, 0:TILES - 1, :]
                         ).then_inc(S["out_done"], 16)
            sp.dma_start(io["out"][(TILES - 1) * P:NODES, :], acc[0:LAST, TILES - 1, :]).then_inc(S["out_done"], 16)
            sp.wait_ge(S["out_done"], 32)

        @block.gpsimd
        def _(pool):
            pool.memset(x_in[96:P, TILES - 1, :], 0.0).then_inc(S["start"], 1)
            pool.wait_ge(S["start"], 1)
            pool.memset(minus_half[:], -0.5).then_inc(S["rstd_step"], 1)
            pool.memset(before[:], 1.0).then_inc(S["rstd_step"], 1)
            pool.sem_inc(S["w_ready"], 2)
            pool.sem_inc(S["down_ready"], 2)
            pool.wait_ge(S["rstd_step"], 2)
            pool.affine_select(out=before[:], in_=before[:], compare_op=ALU.is_gt, fill=0.0, base=0,
                               pattern=[[1, EXPERTS], [-1, EXPERTS]], channel_multiplier=0
                               ).then_inc(S["rstd_step"], 1)
            pool.wait_ge(S["x_step"], 3)
            pool.tensor_scalar(rstd[:], mv[:, :, 1], EPS, None, ALU.add).then_inc(S["rstd_step"], 1)
            pool.wait_ge(S["rstd_step"], 4)
            pool.tensor_tensor(rstd[:], rstd[:], minus_half[:], ALU.pow).then_inc(S["rstd_step"], 1)
            def flat(x):
                return x.rearrange("p u k c -> p (u k c)")

            with pool.Fori(0, EXPERTS) as e:
                for i in range(I_T + 1):
                    if i < I_T:
                        n = e * I_T + (i + 1)
                        raw = flat(raw_gu[:, i % 2])
                        hold(pool, S[f"raw_in_{i % 2}"], (e * (I_T // 2) + (i // 2 + 1)) * 32, S["passed_pool"])
                        pool.tensor_scalar(raw, raw, W_SCALE, None, ALU.mult).then_inc(S["raw_scaled"], 1)
                        pool.wait_ge(S["raw_hi"], n)
                        pool.tensor_tensor(flat(w_gu[:, i % 2, 1]), raw, flat(w_gu[:, i % 2, 0]), ALU.subtract
                                           ).then_inc(S["w_ready"], 1)
                    if i:
                        j = i - 1
                        hold(pool, S[f"down_in_{j % 2}"], (e * (I_T // 2) + (j // 2 + 1)) * 16, S["passed_pool"])
                        pool.tensor_scalar(raw_down[:, j % 2], raw_down[:, j % 2], W_SCALE, None, ALU.mult
                                           ).then_inc(S["down_scaled"], 1)
                        pool.wait_ge(S["down_hi"], e * I_T + i)
                        pool.tensor_tensor(w_down[:, 1, j], raw_down[:, j % 2], w_down[:, 0, j], ALU.subtract
                                           ).then_inc(S["down_ready"], 1)

        @block.vector
        def _(dve):
            dve.wait_ge(S["x_in"], 32)
            for t in range(TILES):
                ins = dve.tensor_tensor(g[:, t, :], g[:, t, :], x_in[:, t, :], ALU.add)
            ins.then_inc(S["x_step"], 1)
            dve.memset(actT[:, :, :, NODES:PAD], 0.0)
            dve.wait_ge(S["small_in"], 48)
            dve.tensor_scalar(raw_router[:], raw_router[:], W_SCALE, None, ALU.mult).then_inc(S["router_step"], 1)
            dve.wait_ge(S["router_step"], 1)
            dve.tensor_copy(w_router[:, 0], raw_router[:]).then_inc(S["router_step"], 1)
            dve.wait_ge(S["router_step"], 2)
            dve.tensor_tensor(w_router[:, 1], raw_router[:], w_router[:, 0], ALU.subtract
                              ).then_inc(S["router_step"], 1)
            dve.wait_ge(S["x_step"], 1)
            for t in range(TILES):
                ins = dve.bn_stats(stats[:, t, :], g[:, t, :])
            ins.then_inc(S["x_step"], 1)
            dve.wait_ge(S["x_step"], 2)
            for t in range(TILES):
                ins = dve.bn_aggr(mv[:, t, :], stats[:, t, :])
            ins.then_inc(S["x_step"], 1)
            dve.wait_ge(S["rstd_step"], 5)
            dve.wait_ge(S["x_step"], 3)
            for t in range(TILES + 1):
                if t < TILES:
                    dve.tensor_scalar(y[:, t % 2, :], g[:, t, :], mv[:, t, 0:1], rstd[:, t:t + 1], ALU.subtract,
                                      ALU.mult).then_inc(S["y_ready"], 1)
                if t:
                    a = t - 1
                    dve.wait_ge(S["y_hi"], a + 1)
                    dve.tensor_tensor(xT[:, 1, :, a * P:(a + 1) * P],
                                      bank[a % 2][:].rearrange("p (k n) -> p k n", k=KT),
                                      xT[:, 0, :, a * P:(a + 1) * P], ALU.subtract).then_inc(S["y_lo"], 1)

            def route(ins, at):
                ins.then_inc(S["route"], 1)
                dve.wait_ge(S["route"], at)

            dve.wait_ge(S["router_mm"], 1)
            route(dve.scalar_tensor_tensor(logits[:], bank[2][:, 0:TILES * EXPERTS]
                                           .rearrange("p (t e) -> p t e", t=TILES), 1.0 / W_SCALE,
                                           router_b[:].unsqueeze(1).to_broadcast([P, TILES, EXPERTS]),
                                           ALU.mult, ALU.add), 1)
            route(dve.tensor_reduce(top[:], logits[:], AX.X, ALU.max), 2)
            four = [P, TILES, EXPERTS, EXPERTS]
            other, own = logits[:].unsqueeze(2).to_broadcast(four), logits[:].unsqueeze(3).to_broadcast(four)
            dve.tensor_tensor(greater[:], other, own, ALU.is_gt)
            route(dve.tensor_tensor(equal[:], other, own, ALU.is_equal), 3)
            route(dve.tensor_tensor(equal[:], equal[:], before[:].unsqueeze(1).to_broadcast(four), ALU.mult), 4)
            route(dve.tensor_tensor(equal[:], equal[:], greater[:], ALU.add), 5)
            route(dve.tensor_reduce(rank[:], equal[:], AX.X, ALU.add), 6)
            flat = [P, TILES, EXPERTS]
            route(dve.tensor_tensor(weight[:], logits[:], top[:].unsqueeze(2).to_broadcast(flat), ALU.subtract), 7)
            dve.wait_ge(S["route_exp"], 1)
            route(dve.scalar_tensor_tensor(weight[:], rank[:], float(TOP_K), weight[:], ALU.is_lt, ALU.mult), 8)
            route(dve.tensor_reduce(whole[:], weight[:], AX.X, ALU.add), 9)
            route(dve.reciprocal(whole[:], whole[:]), 10)
            route(dve.tensor_tensor(weight[:], weight[:], whole[:].unsqueeze(2).to_broadcast(flat), ALU.mult), 11)
            dve.tensor_scalar(share[:], weight[:], BACK, None, ALU.mult)
            for c in range(NCH):
                dve.wait_ge(S["weight_turned"], c + 1)
                n = min(4, TILES - 4 * c) * P
                ins = dve.tensor_copy(weightT[:, c * 512:c * 512 + n], bank[3 + c][0:EXPERTS, 0:n])
            ins.then_inc(S["route"], 1)
            for t in range(TILES):
                dve.wait_ge(S["bias_mm"], t + 1)
                dve.tensor_tensor(acc[:, t, :], bank[6 + t % 2][:], g[:, t, :], ALU.add).then_inc(S["down_free"], 1)
            dve.wait_ge(S["down_free"], TILES)
            with dve.Fori(0, EXPERTS) as e:
                for m in range(PAIRS + 1):
                    if m < PAIRS:
                        i, (c0, cn) = m // NCH, CHUNKS[m % NCH]
                        n = e * PAIRS + (m + 1)
                        gate, up = bank[m % 3][:, 0:cn], bank[3 + m % 3][:, 0:cn]
                        col = e * (2 * I_T) + i
                        dve.wait_ge(S["sig_ready"], n)
                        if m >= 2:
                            dve.wait_ge(S["act_lo"], e * PAIRS + (m - 1))
                        dve.scalar_tensor_tensor(gated[:, m % 2, 0:cn], gate, gu_cols[:, 1, bass.ds(col, 1)],
                                                 sig[:, m % 2, 0:cn], ALU.add, ALU.mult
                                                 ).then_inc(S["gated_ready"], 1)
                        dve.wait_ge(S["gated_ready"], n)
                        dve.scalar_tensor_tensor(gated[:, m % 2, 0:cn], up,
                                                 gu_cols[:, 2, bass.ds(col + I_T, 1)],
                                                 gated[:, m % 2, 0:cn], ALU.add, ALU.mult
                                                 ).then_inc(S["act_ready"], 1)
                    if m:
                        i, (c0, cn) = (m - 1) // NCH, CHUNKS[(m - 1) % NCH]
                        dve.wait_ge(S["act_hi"], e * PAIRS + m)
                        dve.scalar_tensor_tensor(actT[:, 1, i, c0:c0 + cn], gated[:, (m - 1) % 2, 0:cn],
                                                 1.0 / W_SCALE, actT[:, 0, i, c0:c0 + cn], ALU.mult,
                                                 ALU.subtract).then_inc(S["act_lo"], 1)
                for t in range(TILES):
                    dve.wait_ge(S["down_mm"], e * TILES + (t + 2))
                    dve.scalar_tensor_tensor(acc[:, t, :], bank[6 + t % 2][:], share[:, t, bass.ds(e, 1)],
                                             acc[:, t, :], ALU.mult, ALU.add).then_inc(S["down_free"], 1)
                dve.wait_ge(S["down_free"], e * TILES + 2 * TILES)

        @block.scalar
        def _(act):
            for t in range(TILES):
                act.wait_ge(S["y_turned"], t + 1)
                act.activation(xT[:, 0, :, t * P:(t + 1) * P], bank[t % 2][:].rearrange("p (k n) -> p k n", k=KT),
                               ACT.Copy).then_inc(S["y_hi"], 1)
            act.wait_ge(S["route"], 7)
            act.activation(weight[:], weight[:], ACT.Exp).then_inc(S["route_exp"], 1)
            def gate_up_hi(e, i):
                act.wait_ge(S["raw_scaled"], e * I_T + (i + 1))
                act.activation(w_gu[:, i % 2, 0].rearrange("p u k c -> p (u k c)"),
                               raw_gu[:, i % 2].rearrange("p u k c -> p (u k c)"), ACT.Copy
                               ).then_inc(S["raw_hi"], 1)

            with act.Fori(0, EXPERTS) as e:
                gate_up_hi(e, 0)
                gate_up_hi(e, 1)
                for m in range(PAIRS + 1):
                    if m < PAIRS:
                        i, (c0, cn) = m // NCH, CHUNKS[m % NCH]
                        hold(act, S["pair_ready"], e * PAIRS + (m + 1 + 2 * NCH), S["passed_act"])
                        act.activation(sig[:, m % 2, 0:cn], bank[m % 3][:, 0:cn], ACT.Sigmoid,
                                       bias=gu_cols[:, 0, bass.ds(e * (2 * I_T) + i, 1)], scale=1.702 / W_SCALE
                                       ).then_inc(S["sig_ready"], 1)
                        if i and i < I_T - 1 and m % NCH == 0:
                            gate_up_hi(e, i + 1)
                        if m % NCH == 2:
                            act.wait_ge(S["down_scaled"], e * I_T + (i + 1))
                            act.activation(w_down[:, 0, i], raw_down[:, i % 2], ACT.Copy).then_inc(S["down_hi"], 1)
                    if m:
                        i, (c0, cn) = (m - 1) // NCH, CHUNKS[(m - 1) % NCH]
                        act.wait_ge(S["act_ready"], e * PAIRS + m)
                        act.activation(actT[:, 0, i, c0:c0 + cn], gated[:, (m - 1) % 2, 0:cn], ACT.Copy,
                                       scale=1.0 / W_SCALE).then_inc(S["act_hi"], 1)

        @block.tensor
        def _(pe):
            pe.sem_inc(S["down_mm"], 1)
            pe.sem_inc(S["pair_ready"], 2 * NCH)
            for t in range(TILES):
                pe.wait_ge(S["y_ready"], t + 1)
                if t >= 2:
                    pe.wait_ge(S["y_lo"], t - 1)
                for k in range(KT):
                    ins = pe.transpose(bank[t % 2][:, k * P:(k + 1) * P], y[:, t % 2, k * P:(k + 1) * P], ident[:])
                ins.then_inc(S["y_turned"], 1)
            pe.wait_ge(S["y_lo"], TILES)
            pe.wait_ge(S["router_step"], 3)
            for t in range(TILES):
                ins = split_matmuls(pe, bank[2][:, t * EXPERTS:(t + 1) * EXPERTS],
                                    lambda a, k: xT[:, a, k, t * P:(t + 1) * P],
                                    lambda b, k: w_router[:, b, k, :], KT)
            ins.then_inc(S["router_mm"], 1)
            pe.wait_ge(S["route"], 11)
            for c in range(NCH):
                for t in range(4 * c, min(4 * c + 4, TILES)):
                    ins = pe.transpose(bank[3 + c][0:EXPERTS, (t % 4) * P:(t % 4 + 1) * P], weight[:, t, :], ident[:])
                ins.then_inc(S["weight_turned"], 1)
            pe.wait_ge(S["route"], 12)
            for t in range(TILES):
                if t >= 2:
                    pe.wait_ge(S["down_free"], t - 1)
                pe.matmul(bank[6 + t % 2][:], weightT[:, t * P:(t + 1) * P], down_b[:], start=True, stop=True
                          ).then_inc(S["bias_mm"], 1)
            with pe.Fori(0, EXPERTS) as e:
                for m in range(PAIRS):
                    i, (c0, cn) = m // NCH, CHUNKS[m % NCH]
                    if m % NCH == 0:
                        pe.wait_ge(S["w_ready"], e * I_T + (i + 3))
                    if m >= 3:
                        pe.wait_ge(S["act_ready"], e * PAIRS + (m - 2))
                    for u in range(2):
                        ins = split_matmuls(pe, bank[3 * u + m % 3][:, 0:cn],
                                            lambda a, k: w_gu[:, i % 2, a, u, k, :],
                                            lambda b, k: xT[:, b, k, c0:c0 + cn], KT)
                    ins.then_inc(S["pair_ready"], 1)
                pe.wait_ge(S["down_ready"], e * I_T + (I_T + 2))
                pe.wait_ge(S["act_lo"], e * PAIRS + PAIRS)
                for t in range(TILES):
                    pe.wait_ge(S["down_free"], e * TILES + (TILES + t - 1))
                    split_matmuls(pe, bank[6 + t % 2][:], lambda a, i: actT[:, a, i, t * P:(t + 1) * P],
                                  lambda b, i: w_down[:, b, i, :], I_T).then_inc(S["down_mm"], 1)


_INS = ["x", "src", "dst", "node_vec1"] + ["L0_gnn_" + n for n in (
    "f_w1", "f_b1", "f_w2", "f_b2", "s1_w", "s1_b", "b1_w", "b1_b", "wq", "bq", "wk", "bk", "wv", "bv", "wo", "bo",
    "s2_w", "s2_b", "b2_w", "b2_b", "m_w1", "m_b1", "m_w2", "m_b2")] + ["L0_ffn_" + n for n in (
        "router_w", "router_b", "gate_up_proj", "gate_up_proj_bias", "down_proj", "down_proj_bias")]


def kernel(**inputs):
    import concourse.bacc as _bacc
    from concourse.bass_utils import run_bass_kernel_spmd as _run

    nc = _bacc.Bacc("TRN2", target_bir_lowering=False, num_devices=1, dynamic_dma_scratch_size=1024)
    arrays, io = {}, {}
    for name in _INS:
        a = np.ascontiguousarray(inputs[name])
        arrays[f"in_{name}"] = a
        io[name] = nc.dram_tensor(f"in_{name}", a.shape, mybir.dt.from_np(a.dtype), kind="ExternalInput").ap()
    io["out"] = nc.dram_tensor("out_x", (NODES, D), F32, kind="ExternalOutput").ap()
    build(nc, io)
    r = _run(nc, [arrays], core_ids=[0])
    return r.results[0]["out_x"]
```

```python
from contextlib import ExitStack

import numpy as np

import concourse.bass as bass
from concourse import mybir

F32 = mybir.dt.float32
F16 = mybir.dt.float16
I32 = mybir.dt.int32
ALU = mybir.AluOpType
ACT = mybir.ActivationFunctionType
AX = mybir.AxisListType

P = 128
NODES = 1250
D = 512
EDGES = 20000
LAYERS = 4
HEADS = 4
DH = D // HEADS
FREQS = 32
BASE_PERIOD = 16
COND = 16
EXPERTS = 8
FF = 1024
TOP_K = 2
EPS = 1e-5

TILES = -(-NODES // P)
PAD = TILES * P
LAST = NODES - (TILES - 1) * P
KT = D // P
CHUNKS = [(c, min(512, NODES - c)) for c in range(0, NODES, 512)]
NCH = len(CHUNKS)
W_SCALE = 64.0
BACK = 1.0 / (W_SCALE * W_SCALE)
SCORE = DH ** -0.5 * BACK
MASKED = -1e30
MAX_SHIFT = 1e20
LEAST_SUM = 1e-20

EP = 125
ECOLS = EDGES // EP
HALF = NODES // 2
FIELD = 4096
GROUP = 32
assert GROUP * EP < FIELD and ECOLS % GROUP == 0
NGROUPS = ECOLS // GROUP
BLK = 4
PAIRS_OF_BLOCKS = GROUP // (2 * BLK)
SWEEPS = 2
SWEEP = TILES // SWEEPS
ROUNDS = NGROUPS * SWEEPS
SPLIT = 2
EARLY = 3
COPIES = 7

NROWS = 96
MATS = 4
PASSES = ((0, 0), (0, 1), (1, 0))


def hold(eng, sem, value, passed):
    eng.wait_ge(sem, value)
    eng.sem_inc(passed, 1)


def split_matmuls(pe, out, stationary, moving, n_k):
    for k in range(n_k):
        for i, (a, b) in enumerate(PASSES):
            ins = pe.matmul(out, stationary(a, k), moving(b, k), start=k == 0 and i == 0,
                            stop=k == n_k - 1 and i == len(PASSES) - 1)
    return ins


def build(nc, io):
    with ExitStack() as whole:
        def sb(name, shape, dt=F32):
            return whole.enter_context(nc.sbuf_tensor(name, shape, dt))

        g = sb("g", [P, TILES, D])
        ident = sb("ident", [P, P])
        bias_cols = sb("bias_cols", [P, 3 * LAYERS * KT])
        gu_cols = sb("gu_cols", [P, 3, EXPERTS * 2 * FF // P])
        with ExitStack() as gnn:
            def gsb(name, shape, dt=F32):
                return gnn.enter_context(nc.sbuf_tensor(name, shape, dt))
            log_count = gsb("log_count", [P, TILES, NODES])
            cond_stack = gsb("cond_stack", [NROWS, PAD], F16)
            norm_stack = gsb("norm_stack", [NROWS, LAYERS * MATS + 2, D], F16)
            prepare(nc, io, g, ident, bias_cols, gu_cols, log_count, cond_stack, norm_stack)
            attention_layers(nc, io, g, ident, bias_cols, log_count, cond_stack, norm_stack)
        experts(nc, io, g, ident, gu_cols)


def prepare(nc, io, g, ident, bias_cols, gu_cols, log_count, cond_stack, norm_stack):
    with ExitStack() as ctx:
        def sb(name, shape, dt=F32):
            return ctx.enter_context(nc.sbuf_tensor(name, shape, dt))

        def sem(name):
            return ctx.enter_context(nc.semaphore(name))

        bank = [ctx.enter_context(nc.psum_tensor(f"pre_bank{i}", [P, 512], F32)) for i in range(8)]
        norm_raw = sb("norm_raw", [NROWS, LAYERS * MATS, D])
        edges = sb("edges", [EP, 2, ECOLS], I32)
        src = sb("src_number", [EP, ECOLS])
        dst_low = sb("dst_low", [EP, ECOLS])
        dst_weight = sb("dst_weight", [EP, ECOLS])
        columns = sb("columns", [P, PAD], F16)
        src_hot = sb("src_hot", [EP, 2 * BLK, SWEEP * P], F16)
        dst_hot = sb("dst_hot", [EP, 2 * BLK, HALF], F16)
        packed = sb("packed", [P, SWEEPS, SWEEP, HALF], I32)
        high = sb("high", [P, SWEEP, HALF], I32)
        at_least_1 = sb("at_least_1", [P, 2, NODES])
        logs = sb("logs", [P, 2, NODES])
        noise, turns = (at_least_1[0:2 * FREQS, i, :] for i in range(2))
        product = logs[0:2 * FREQS, 0, :]
        linear, sig, hidden = turns[0:COND], product[0:COND], logs[0:COND, 1, :]
        cond_raw = sb("cond_raw", [NROWS, NODES])
        freq_row = sb("freq_row", [2 * FREQS, 1], I32)
        freq = sb("freq", [2 * FREQS, 4])
        f1 = sb("f1", [2 * FREQS, COND])
        f1b = sb("f1b", [COND, 1])
        f2 = sb("f2", [COND, NROWS])
        f2b = sb("f2b", [NROWS, 1])
        stats = sb("stats", [P, TILES, 6])
        mv = sb("mv", [P, TILES, 2])
        rstd = sb("rstd", [P, TILES])
        minus_half = sb("minus_half", [P, TILES])
        bias_rows = sb("bias_rows", [3 * LAYERS * KT, P])
        gu_rows = sb("gu_rows", [P, P])
        counts = log_count[:].bitcast(I32)

        edges_in = sem("edges_in")
        x_in = sem("x_in")
        noise_in = sem("noise_in")
        small_in = sem("small_in")
        norm_in = sem("norm_in")
        zeroed = sem("zeroed")
        const_ready = sem("const_ready")
        edge_step = sem("edge_step")
        hot_ready = sem("hot_ready")
        hot_free = sem("hot_free")
        counted = sem("counted")
        copied = sem("copied")
        unpacked = sem("unpacked")
        unpack_step = sem("unpack_step")
        added = sem("added")
        clamped = sem("clamped")
        logged = sem("logged")
        table_step = sem("table_step")
        freq_step = sem("freq_step")
        args_step = sem("args_step")
        cond_act = sem("cond_act")
        cond_mm = sem("cond_mm")
        cond_pool = sem("cond_pool")
        norm_step = sem("norm_step")
        norm_hi = sem("norm_hi")
        stats_step = sem("stats_step")
        rstd_ready = sem("rstd_ready")
        turned = sem("turned")
        cols_step = sem("cols_step")
        ARGS = 10
        NOISE_IN = 16 * 9

        block = ctx.enter_context(nc.Block())

        @block.sync
        def _(sp):
            sp.dma_start(edges[:, 0, :], io["src"].rearrange("(p j) -> p j", p=EP)).then_inc(edges_in, 16)
            sp.dma_start(edges[:, 1, :], io["dst"].rearrange("(p j) -> p j", p=EP)).then_inc(edges_in, 16)
            sp.dma_start(noise, io["node_vec1"].rearrange("n a -> a n").partition_broadcast(2 * FREQS)
                         .rearrange("p a n -> p (a n)")).then_inc(noise_in, 16)
            sp.dma_start(f1[:], io["L0_gnn_f_w1"]).then_inc(noise_in, 16)
            sp.dma_start(f1b[:], io["L0_gnn_f_b1"].rearrange("(c a) -> c a", a=1)).then_inc(noise_in, 16)
            for n, name in enumerate(("bq", "bk", "m_b1")):
                sp.dma_start(bias_rows[16 * n:16 * n + 16, :],
                             io["L0_gnn_" + name].rearrange("l (t f) -> (l t) f", f=P)).then_inc(small_in, 16)
            sp.dma_start(gu_rows[:], io["L0_ffn_gate_up_proj_bias"].rearrange("e (t f) -> (e t) f", f=P)
                         ).then_inc(small_in, 16)
            sp.wait_ge(zeroed, 7)
            for r in range(3):
                sp.dma_start(f2[:, 32 * r + 1:32 * r + 1 + COND], io["L0_gnn_f_w2"]).then_inc(noise_in, 16)
                sp.dma_start(f2b[32 * r + 1:32 * r + 1 + COND, :],
                             io["L0_gnn_f_b2"].rearrange("(c a) -> c a", a=1)).then_inc(noise_in, 16)
            raw = norm_raw[:].rearrange("c (l m) d -> c l m d", m=MATS)
            for m, name in enumerate(("s1", "b1", "s2", "b2")):
                for r in range(3):
                    sp.dma_start(raw[32 * r + 1:32 * r + 1 + COND, :, m, :],
                                 io[f"L0_gnn_{name}_w"].rearrange("l c d -> c l d")).then_inc(norm_in, 16)
                    sp.dma_start(raw[32 * r:32 * r + 1, :, m, :],
                                 io[f"L0_gnn_{name}_b"].rearrange("(a l) d -> a l d", a=1)).then_inc(norm_in, 16)
            sp.dma_start(g[:, 0:TILES - 1, :], io["x"][0:(TILES - 1) * P, :].rearrange("(t p) d -> p t d", p=P)
                         ).then_inc(x_in, 16)
            sp.dma_start(g[0:LAST, TILES - 1, :], io["x"][(TILES - 1) * P:NODES, :]).then_inc(x_in, 16)

        @block.gpsimd
        def _(pool):
            pool.iota(columns[:], [[1, PAD]], base=0, channel_multiplier=0,
                      allow_small_or_imprecise_dtypes=True).then_inc(const_ready, 1)
            pool.iota(freq_row[:], [[1, 1]], base=1, channel_multiplier=1).then_inc(const_ready, 1)
            pool.memset(ident[:], 0.0).then_inc(const_ready, 1)
            pool.memset(minus_half[:], -0.5).then_inc(const_ready, 1)
            pool.wait_ge(const_ready, 4)
            pool.affine_select(out=ident[:], in_=ident[:], compare_op=ALU.not_equal, fill=1.0, base=0,
                               pattern=[[-1, P]], channel_multiplier=1).then_inc(const_ready, 1)
            pool.wait_ge(const_ready, 5)
            pool.memset(f2[:], 0.0).then_inc(zeroed, 1)
            pool.memset(g[96:P, TILES - 1, :], 0.0).then_inc(zeroed, 1)
            pool.memset(f2b[:], 0.0).then_inc(zeroed, 1)
            pool.memset(norm_raw[:], 0.0).then_inc(zeroed, 1)
            pool.wait_ge(zeroed, 4)
            for r in range(3):
                pool.memset(f2b[32 * r:32 * r + 1, :], 1.0).then_inc(zeroed, 1)
            pool.wait_ge(zeroed, 7)
            pool.sem_inc(added, 2)

            pool.wait_ge(noise_in, NOISE_IN)
            pool.wait_ge(freq_step, 6)
            magic = 1.5 * 2.0 ** 23
            first = 6.28125
            pool.tensor_scalar(noise, noise, freq[:, 1:2], None, ALU.mult).then_inc(args_step, 1)
            pool.wait_ge(args_step, 1)
            pool.tensor_scalar(turns, noise, 1.0 / (2 * np.pi), freq[:, 2:3], ALU.mult, ALU.add
                               ).then_inc(args_step, 1)
            pool.wait_ge(args_step, 2)
            pool.tensor_scalar(turns, turns, magic, None, ALU.add).then_inc(args_step, 1)
            pool.wait_ge(args_step, 3)
            pool.tensor_scalar(turns, turns, magic, None, ALU.subtract).then_inc(args_step, 1)
            pool.wait_ge(args_step, 4)
            pool.memset(counts, 0).then_inc(zeroed, 1)
            pool.wait_ge(zeroed, 8)

            raw = norm_raw[:].rearrange("c (l m) d -> c l m d", m=MATS)

            for u in range(ROUNDS + 1):
                half = (u + 1) % 2
                rows = counts[:, half * SWEEP:(half + 1) * SWEEP, :]
                pool.wait_ge(unpacked, u + 1)
                low = pool.tensor_tensor(rows[:, :, 0:HALF], rows[:, :, 0:HALF], packed[:, half], ALU.add)
                if u < ROUNDS:
                    pool.tensor_tensor(rows[:, :, HALF:NODES], rows[:, :, HALF:NODES], high[:, :, 0:NODES - HALF],
                                       ALU.add).then_inc(added, 1)
                else:
                    low.then_inc(added, 1)
                if u == 0:
                    for i, piece in enumerate((first, 2 * np.pi - first)):
                        pool.tensor_scalar(product, turns, piece, None, ALU.mult).then_inc(args_step, 1)
                        pool.wait_ge(args_step, 5 + 2 * i)
                        pool.tensor_tensor(noise, noise, product, ALU.subtract).then_inc(args_step, 1)
                        pool.wait_ge(args_step, 6 + 2 * i)
                    pool.tensor_scalar(noise, noise, freq[:, 3:4], 3.1415925, ALU.add, ALU.min
                                       ).then_inc(args_step, 1)
                    pool.wait_ge(args_step, 9)
                    pool.tensor_scalar(noise, noise, -3.1415925, None, ALU.max).then_inc(args_step, 1)
                    pool.wait_ge(args_step, ARGS)
                if u in (1, 2):
                    pool.wait_ge(norm_in, 16 * 24)
                    pool.wait_ge(added, u + 3)
                    for r in range(3):
                        row = raw[32 * r:32 * r + 1, :, 2 * (u - 1), :]
                        pool.tensor_scalar(row, row, 1.0, None, ALU.add).then_inc(norm_step, 1)
                        pool.wait_ge(norm_step, 3 * (u - 1) + r + 1)
                if u == 3:
                    pool.wait_ge(cond_act, 1 + 2 * NCH)
                    pool.tensor_tensor(hidden, linear, sig, ALU.mult).then_inc(cond_pool, 1)
                    pool.wait_ge(cond_pool, 1)
                if u == 4:
                    pool.wait_ge(cond_act, 1 + 3 * NCH)
                    pool.wait_ge(added, u + 3)
                    pool.memset(cond_stack[:, NODES:PAD], 0.0).then_inc(cond_pool, 1)
                    pool.tensor_copy(cond_stack[:, 0:NODES], cond_raw[:]).then_inc(cond_pool, 1)
                    pool.wait_ge(cond_pool, 3)
                    pool.tensor_tensor(cond_stack[32:64, 0:NODES], cond_raw[32:64], cond_stack[32:64, 0:NODES],
                                       ALU.subtract).then_inc(cond_pool, 1)
                    pool.wait_ge(cond_pool, 4)
                    pool.wait_ge(cols_step, 1)
                    pool.tensor_scalar(gu_cols[:, 2, :], gu_cols[:, 1, :], W_SCALE, None, ALU.add
                                       ).then_inc(cond_pool, 1)
                if u == 5:
                    pool.wait_ge(norm_hi, 1)
                    pool.wait_ge(added, u + 3)
                    pool.tensor_tensor(norm_stack[64:96, 0:LAYERS * MATS], norm_raw[64:96],
                                       norm_stack[64:96, 0:LAYERS * MATS], ALU.subtract).then_inc(norm_step, 1)
                    pool.wait_ge(norm_step, 7)
                if u == 6:
                    pool.wait_ge(stats_step, 2)
                    pool.tensor_scalar(rstd[:], mv[:, :, 1], EPS, None, ALU.add).then_inc(rstd_ready, 1)
                    pool.wait_ge(rstd_ready, 1)
                    pool.tensor_tensor(rstd[:], rstd[:], minus_half[:], ALU.pow).then_inc(rstd_ready, 1)
                    pool.wait_ge(rstd_ready, 2)
                    for t in range(TILES):
                        pool.tensor_scalar(g[:, t, :], g[:, t, :], mv[:, t, 0:1], rstd[:, t:t + 1], ALU.subtract,
                                           ALU.mult)

        @block.vector
        def _(dve):
            dve.memset(packed[:, 1], 0)
            dve.memset(norm_stack[:, LAYERS * MATS:, :], 0.0)
            dve.wait_ge(edges_in, 32)
            dve.tensor_copy(src[:], edges[:, 0, :]).then_inc(edge_step, 1)
            dve.tensor_copy(dst_low[:], edges[:, 1, :]).then_inc(edge_step, 1)
            dve.wait_ge(edge_step, 2)
            dve.tensor_scalar(dst_weight[:], dst_low[:], float(HALF), None, ALU.is_ge).then_inc(edge_step, 1)
            dve.wait_ge(edge_step, 3)
            dve.scalar_tensor_tensor(dst_low[:], dst_weight[:], -float(HALF), dst_low[:], ALU.mult, ALU.add
                                     ).then_inc(edge_step, 1)
            dve.wait_ge(edge_step, 4)
            dve.tensor_scalar(dst_weight[:], dst_weight[:], float(FIELD - 1), 1.0, ALU.mult, ALU.add
                              ).then_inc(edge_step, 1)
            dve.wait_ge(edge_step, 5)
            dve.wait_ge(const_ready, 5)
            dve.tensor_copy(freq[:, 0:1], freq_row[:]).then_inc(freq_step, 1)
            dve.wait_ge(freq_step, 1)
            dve.tensor_scalar(freq[32:64, 0:1], freq[32:64, 0:1], float(FREQS), None, ALU.subtract
                              ).then_inc(freq_step, 1)
            dve.memset(freq[:, 2:4], 0.0).then_inc(freq_step, 1)
            dve.wait_ge(freq_step, 3)
            dve.tensor_scalar(freq[:, 1:2], freq[:, 0:1], 2.0 * np.pi / BASE_PERIOD, None, ALU.mult
                              ).then_inc(freq_step, 1)
            dve.memset(freq[32:64, 2:3], 0.25).then_inc(freq_step, 1)
            dve.memset(freq[32:64, 3:4], np.pi / 2).then_inc(freq_step, 1)

            def hots(n, s, b, half):
                done = n * (SWEEPS * GROUP) + (s * GROUP + 2 * BLK * b + half * BLK)
                for u in range(BLK):
                    j = n * GROUP + (2 * BLK * b + (half * BLK + u))
                    slot = half * BLK + u
                    if u == 0:
                        dve.wait_ge(hot_free, n * (SWEEPS * 2 * PAIRS_OF_BLOCKS) +
                                    (s * 2 * PAIRS_OF_BLOCKS + 2 * b + half + 1))
                    dve.tensor_scalar(src_hot[:, slot, :], columns[0:EP, s * SWEEP * P:(s + 1) * SWEEP * P],
                                      src[:, bass.ds(j, 1)], None, ALU.is_equal)
                    dve.tensor_scalar(dst_hot[:, slot, :], columns[0:EP, 0:HALF], dst_low[:, bass.ds(j, 1)],
                                      dst_weight[:, bass.ds(j, 1)], ALU.is_equal, ALU.mult).then_inc(hot_ready, 1)

            def unpack(u, half):
                dve.wait_ge(copied, u * COPIES + COPIES)
                dve.wait_ge(added, u + 2)
                dve.tensor_scalar(high[:], packed[:, half], 12, None, ALU.arith_shift_right
                                  ).then_inc(unpack_step, 1)
                dve.wait_ge(unpack_step, u + 1)
                dve.tensor_scalar(packed[:, half], packed[:, half], FIELD - 1, None, ALU.bitwise_and
                                  ).then_inc(unpacked, 1)

            def groups(start, stop):
                with dve.Fori(start, stop) as n:
                    for s in range(SWEEPS):
                        hots(n, s, 0, 0)
                        hots(n, s, 0, 1)
                        unpack(n * SWEEPS + s, (s + 1) % 2)
                        with dve.Fori(1, PAIRS_OF_BLOCKS) as b:
                            hots(n, s, b, 0)
                            hots(n, s, b, 1)

            def table_rows(tiles, start):
                for i in range(start, start + len(tiles) + 1):
                    if i < start + len(tiles):
                        if i >= 2:
                            dve.wait_ge(logged, i - 1)
                        dve.tensor_scalar(at_least_1[:, i % 2, :], counts[:, tiles[i - start], :], 1.0, None, ALU.max
                                          ).then_inc(clamped, 1)
                    if i > start:
                        t = tiles[i - 1 - start]
                        dve.wait_ge(clamped, i)
                        dve.tensor_scalar(log_count[:, t, :], counts[:, t, :], 1.0, MASKED, ALU.is_lt, ALU.mult
                                          ).then_inc(table_step, 1)
                        dve.wait_ge(logged, i)
                        dve.wait_ge(table_step, 2 * i - 1 + (start > 0))
                        dve.scalar_tensor_tensor(log_count[:, t, :], logs[:, (i - 1) % 2, :], 1.0 / SCORE,
                                                 log_count[:, t, :], ALU.mult, ALU.add).then_inc(table_step, 1)

            dve.sem_inc(hot_free, 2)
            groups(0, SPLIT)
            dve.wait_ge(x_in, 32)
            for t in range(TILES):
                ins = dve.bn_stats(stats[:, t, :], g[:, t, :])
            ins.then_inc(stats_step, 1)
            dve.wait_ge(stats_step, 1)
            for t in range(TILES):
                ins = dve.bn_aggr(mv[:, t, :], stats[:, t, :])
            ins.then_inc(stats_step, 1)
            groups(SPLIT, NGROUPS)
            dve.wait_ge(added, ROUNDS + 2)
            dve.wait_ge(cond_pool, 5)
            table_rows(range(0, EARLY), 0)
            unpack(ROUNDS, (ROUNDS + 1) % 2)
            for i in range(SWEEP):
                last = counts[:, SWEEP + i, HALF:NODES]
                ins = dve.tensor_tensor(last, last, high[:, i, 0:NODES - HALF], ALU.add)
            ins.then_inc(table_step, 1)
            table_rows(range(EARLY, SWEEP), EARLY)
            dve.wait_ge(added, ROUNDS + 3)
            dve.wait_ge(table_step, 2 * SWEEP + 1)
            table_rows(range(SWEEP, TILES), SWEEP)

        @block.scalar
        def _(act):
            act.wait_ge(turned, 2)
            act.activation(bias_cols[:], bank[6][:, 0:3 * LAYERS * KT], ACT.Copy, scale=W_SCALE)
            act.activation(gu_cols[:, 0, :], bank[7][:, 0:P], ACT.Copy, scale=1.702)
            act.activation(gu_cols[:, 1, :], bank[7][:, 0:P], ACT.Copy, scale=W_SCALE).then_inc(cols_step, 1)
            act.sem_inc(copied, COPIES)

            def copy_out(r):
                half = r % 2
                for i in range(SWEEP):
                    act.wait_ge(counted, r * SWEEP + i + 1)
                    if i == 0:
                        act.wait_ge(added, r + 2)
                    act.activation(packed[:, half, i, 0:512], bank[i][:], ACT.Copy).then_inc(copied, 1)
                    if i == SWEEP - 2:
                        act.activation(packed[:, half, 0:4, 512:HALF],
                                       bank[5][:].rearrange("p (i n) -> p i n", i=4)[:, :, 0:HALF - 512], ACT.Copy
                                       ).then_inc(copied, 1)
                    if i == SWEEP - 1:
                        act.activation(packed[:, half, 4, 512:HALF], bank[7][:, 0:HALF - 512], ACT.Copy
                                       ).then_inc(copied, 1)

            def logarithms(start, stop):
                for i in range(start, stop):
                    act.wait_ge(clamped, i + 1)
                    if i >= 2:
                        act.wait_ge(table_step, 2 * (i - 1) + (i - 2 >= EARLY))
                    act.activation(logs[:, i % 2, :], at_least_1[:, i % 2, :], ACT.Ln).then_inc(logged, 1)

            for r in range(ROUNDS):
                if r == 2:
                    act.wait_ge(args_step, ARGS)
                    act.activation(noise, noise, ACT.Sin).then_inc(cond_act, 1)
                if r == 3:
                    act.wait_ge(norm_step, 6)
                    act.activation(norm_stack[:, 0:LAYERS * MATS, :], norm_raw[:], ACT.Copy).then_inc(norm_hi, 1)
                if r == ROUNDS - 1:
                    logarithms(0, EARLY)
                copy_out(r)
                if r == SPLIT * SWEEPS - 1:
                    for c, (c0, cn) in enumerate(CHUNKS):
                        act.wait_ge(cond_mm, 1 + c)
                        act.activation(linear[:, c0:c0 + cn], bank[6][0:COND, 0:cn], ACT.Identity,
                                       bias=f1b[:, 0:1]).then_inc(cond_act, 1)
                        act.activation(sig[:, c0:c0 + cn], bank[6][0:COND, 0:cn], ACT.Sigmoid,
                                       bias=f1b[:, 0:1]).then_inc(cond_act, 1)
                    for c, (c0, cn) in enumerate(CHUNKS):
                        act.wait_ge(cond_mm, NCH + 1 + c)
                        act.activation(cond_raw[:, c0:c0 + cn], bank[6][0:NROWS, 0:cn], ACT.Identity,
                                       bias=f2b[:, 0:1]).then_inc(cond_act, 1)
            logarithms(EARLY, TILES)

        @block.tensor
        def _(pe):
            pe.wait_ge(const_ready, 5)
            pe.wait_ge(small_in, 64)
            nb = 3 * LAYERS * KT
            pe.transpose(bank[6][:, 0:nb], bias_rows[:], ident[0:nb, 0:nb]).then_inc(turned, 1)
            pe.transpose(bank[7][:, 0:P], gu_rows[:], ident[:]).then_inc(turned, 1)
            pe.wait_ge(cols_step, 1)

            def count(n, s, b, half, first=False, last=False):
                rnd = n * SWEEPS + s
                blk = n * (SWEEPS * 2 * PAIRS_OF_BLOCKS) + (s * 2 * PAIRS_OF_BLOCKS + 2 * b + half)
                pe.wait_ge(hot_ready, blk * BLK + BLK)
                for i in range(SWEEP):
                    if first and i == 0:
                        pe.wait_ge(copied, rnd * COPIES + 5)
                    if first and i == SWEEP - 1:
                        pe.wait_ge(copied, rnd * COPIES + COPIES)
                    rest = bank[5][:, i * P:i * P + HALF - 512] if i < 4 else bank[7][:, 0:HALF - 512]
                    for u in range(BLK):
                        slot = half * BLK + u
                        start, stop = first and u == 0, last and u == BLK - 1
                        pe.matmul(bank[i][:], src_hot[:, slot, i * P:(i + 1) * P], dst_hot[:, slot, 0:512],
                                  start=start, stop=stop)
                        ins = pe.matmul(rest, src_hot[:, slot, i * P:(i + 1) * P], dst_hot[:, slot, 512:HALF],
                                        start=start and i in (0, 4), stop=stop and i in (3, 4))
                    if last:
                        ins.then_inc(counted, 1)
                if last:
                    pe.wait_ge(counted, rnd * SWEEP + SWEEP)
                    pe.sem_inc(hot_free, 1)
                else:
                    ins.then_inc(hot_free, 1)

            def groups(start, stop):
                with pe.Fori(start, stop) as n:
                    for s in range(SWEEPS):
                        count(n, s, 0, 0, first=True)
                        count(n, s, 0, 1)
                        with pe.Fori(1, PAIRS_OF_BLOCKS - 1) as b:
                            count(n, s, b, 0)
                            count(n, s, b, 1)
                        count(n, s, PAIRS_OF_BLOCKS - 1, 0)
                        count(n, s, PAIRS_OF_BLOCKS - 1, 1, last=True)

            groups(0, SPLIT)
            for c, (c0, cn) in enumerate(CHUNKS):
                pe.wait_ge(cond_act, 1 + 2 * c)
                pe.matmul(bank[6][0:COND, 0:cn], f1[:], noise[:, c0:c0 + cn], start=True, stop=True
                          ).then_inc(cond_mm, 1)
            pe.wait_ge(cond_pool, 1)
            for c, (c0, cn) in enumerate(CHUNKS):
                pe.wait_ge(cond_act, 1 + 2 * NCH + c)
                pe.matmul(bank[6][0:NROWS, 0:cn], f2[:], hidden[:, c0:c0 + cn], start=True, stop=True
                          ).then_inc(cond_mm, 1)
            groups(SPLIT, NGROUPS)


def attention_layers(nc, io, g, ident, bias_cols, log_count, cond_stack, norm_stack):
    LNG = TILES // 2
    QKV = 2 * NCH + 3
    V_SETS = [range(a, min(a + 4, TILES)) for a in range(0, TILES, 4)]
    FULL = 8
    LAG = 3
    NP = 3
    W_USES = 7
    with ExitStack() as ctx:
        def sb(name, shape, dt=F32):
            return ctx.enter_context(nc.sbuf_tensor("gnn_" + name, shape, dt))

        def sem(name):
            return ctx.enter_context(nc.semaphore(name))

        psum = ctx.enter_context(nc.psum_tensor("gnn_psum", [P, 8 * 512], F32))
        bank = [psum[:, i * 512:(i + 1) * 512] for i in range(8)]
        s_bank, t_bank, o_bank = bank[0:3], bank[3:6], bank[6:8]
        scores = psum[:, 0:NODES]
        v_out = psum[:, 3 * 512:3 * 512 + TILES * DH]
        turned = psum[:, 3 * 512:6 * 512].bitcast(F16)[:, 0:2 * TILES * P]
        h_bank = bank[6:8] + bank[0:2]
        yT = sb("yT", [P, 2, KT, PAD], F16)
        qk = sb("qk", [P, 2, 2, PAD], F16)
        v = sb("v", [P, 2, TILES, DH], F16)
        room = sb("room", [P, 3, 512])
        work = sb("work", [P, 2 * NP * PAD])
        pT = sb("pT", [P, 2, 2, TILES, P], F16)
        attended = sb("attended", [P, TILES, D])
        raw = sb("raw", [P, KT * D])
        ident_half = sb("ident_half", [P, P], F16)
        w_qkv = sb("w_qkv", [P, 2, 3, KT, DH], F16)
        w_o = sb("w_o", [P, 2, KT, D], F16)
        bv_rows = sb("bv_rows", [P, D])
        out_bias = sb("out_bias", [P, D])
        qk_bias = sb("qk_bias", [P, 2])
        hidden_bias = sb("hidden_bias", [P, KT])
        best = sb("best", [P, 2])
        shift = sb("shift", [P, 2])
        total = sb("total", [P, NP])
        inverse = sb("inverse", [P, 2 * NP])
        stats = sb("stats", [P, 2, 6])
        mv = sb("mv", [P, 2, 2])
        rstd = sb("rstd", [P, 2])
        minus_half = sb("minus_half", [P, 2])
        head_w = [w_qkv[:, a].rearrange("p w k c -> p (w k c)") for a in range(2)]

        def square_w(w):
            return [w[:, a].rearrange("p k d -> p (k d)") for a in range(2)]

        y = qk[:].rearrange("p a b n -> p (a b n)").bitcast(F32)[:, 0:4 * D].rearrange("p (s d) -> p s d", s=4)
        probs = work[:, 0:NP * PAD].rearrange("p (s n) -> p s n", s=NP)
        halves = work[:, NP * PAD:].bitcast(F16)
        parts = halves.rearrange("p (s a n) -> p s a n", s=NP, a=2)
        hT = work[:].bitcast(F16)[:, 0:2 * KT * PAD].rearrange("p (a t n) -> p a t n", a=2, t=KT)
        oT = halves[:, 0:4 * 2 * HEADS * P].rearrange("p (s a h n) -> p s a h n", s=4, a=2, h=HEADS)
        pT_flat = pT[:].rearrange("p s a b n -> p s (a b n)")
        w_m1 = pT[:].rearrange("p s a b n -> p (s a b n)")[:, 0:2 * KT * D].rearrange(
            "p (a k d) -> p a k d", a=2, k=KT)
        w_m2 = w_o

        names = ("start passed_pool passed_dve passed_pe raw_in w_scaled w_hi w_ready "
                 "bv_in bv_ready ob_in ob_free ob_added recip_ready qk_lo "
                 "stats_ready mv_ready var_eps rstd_ready norm_mm y_part y_ready y_turned y_hi y_lo "
                 "res_ready res_free bias_ready proj_ready qk_hi v_sum v_hi v_lo s_ready best_ready "
                 "shift_ready exp_ready inv_ready e_hi e_lo p_turned p_hi p_lo o_ready o_out o_turned o_hi o_lo "
                 "mlp_ready hidden h_zero h_hi h_ready")
        S = {n: sem("g_" + n) for n in names.split()}
        block = ctx.enter_context(nc.Block())

        @block.sync
        def _(sp):
            def load(L, use, dst, src):
                sp.wait_ge(S["w_ready"], L * W_USES + (use + 1))
                for a, b in zip(dst, src):
                    sp.dma_start(a, b).then_inc(S["raw_in"], 16)

            def square(name, L):
                return io["L0_gnn_" + name][bass.ds(L, 1), :, :].rearrange("a (k p) n -> p (a k) n", p=P)

            with sp.Fori(0, LAYERS) as L:
                for h in range(HEADS):
                    load(L, h, [raw[:, n * KT * DH:(n + 1) * KT * DH].rearrange("p (k c) -> p k c", k=KT)
                                          for n in range(3)],
                         [io["L0_gnn_" + w][bass.ds(L, 1), :, h * DH:(h + 1) * DH]
                          .rearrange("a (k p) c -> p (a k) c", p=P) for w in ("wq", "wk", "wv")])
                    if h == 0:
                        sp.wait_ge(S["res_free"], L * 2 * TILES + 1)
                        sp.dma_start(bv_rows[:], io["L0_gnn_bv"][bass.ds(L, 1), :].partition_broadcast(P)
                                     .rearrange("p a n -> p (a n)")).then_inc(S["bv_in"], 16)
                        sp.wait_ge(S["ob_free"], L * 2 + 1)
                        sp.dma_start(out_bias[:], io["L0_gnn_bo"][bass.ds(L, 1), :].partition_broadcast(P)
                                     .rearrange("p a n -> p (a n)")).then_inc(S["ob_in"], 16)
                load(L, 4, [raw[:].rearrange("p (k n) -> p k n", k=KT)], [square("wo", L)])
                sp.wait_ge(S["ob_free"], L * 2 + 2)
                sp.dma_start(out_bias[:], io["L0_gnn_m_b2"][bass.ds(L, 1), :].partition_broadcast(P)
                             .rearrange("p a n -> p (a n)")).then_inc(S["ob_in"], 16)
                load(L, 5, [raw[:].rearrange("p (k n) -> p k n", k=KT)], [square("m_w1", L)])
                load(L, 6, [raw[:].rearrange("p (k n) -> p k n", k=KT)], [square("m_w2", L)])
        RAW_IN = HEADS * 48 + 3 * 16

        @block.gpsimd
        def _(pool):
            pool.memset(minus_half[:], -0.5).then_inc(S["start"], 1)
            pool.sem_inc(S["w_ready"], 1)
            pool.sem_inc(S["ob_free"], 1)
            pool.wait_ge(S["start"], 1)

            def scale(L, use, raw_in, n):
                hold(pool, S["raw_in"], L * RAW_IN + raw_in, S["passed_pool"])
                pool.tensor_scalar(raw[:, 0:n], raw[:, 0:n], W_SCALE, None, ALU.mult).then_inc(S["w_scaled"], 1)

            def rest_part(L, use, n, hi, lo):
                pool.wait_ge(S["w_hi"], L * W_USES + (use + 1))
                pool.tensor_tensor(lo, raw[:, 0:n], hi, ALU.subtract).then_inc(S["w_ready"], 1)

            def rsqrt(L, first, group):
                n = L * 2 * LNG + (first + group + 1)
                hold(pool, S["mv_ready"], n, S["passed_pool"])
                pool.tensor_scalar(rstd[:], mv[:, :, 1], EPS, None, ALU.add).then_inc(S["var_eps"], 1)
                pool.wait_ge(S["var_eps"], n)
                pool.tensor_tensor(rstd[:], rstd[:], minus_half[:], ALU.pow).then_inc(S["rstd_ready"], 1)

            def head(L, h, use, n, hi, lo):
                for t in range(TILES):
                    if t == len(V_SETS) - 1:
                        pool.wait_ge(S["v_hi"], L * HEADS + (h + 1))
                        pool.tensor_tensor(v[:, 1].rearrange("p t d -> p (t d)"),
                                           room[:].rearrange("p c n -> p (c n)")[:, 0:TILES * DH],
                                           v[:, 0].rearrange("p t d -> p (t d)"), ALU.subtract
                                           ).then_inc(S["v_lo"], 1)
                    pool.wait_ge(S["e_hi"], L * HEADS * TILES + (h * TILES + t + 1))
                    pool.tensor_tensor(parts[:, t % NP, 1, 0:NODES], probs[:, t % NP, 0:NODES],
                                       parts[:, t % NP, 0, 0:NODES], ALU.subtract).then_inc(S["e_lo"], 1)
                    if t == 5:
                        rest_part(L, use, n, hi, lo)

            with pool.Fori(0, LAYERS) as L:
                rsqrt(L, 0, 0)
                scale(L, 0, 48, 3 * KT * DH)
                rsqrt(L, 0, 1)
                hold(pool, S["w_scaled"], L * W_USES + 1, S["passed_pool"])
                pool.tensor_copy(head_w[0], raw[:, 0:3 * KT * DH]).then_inc(S["w_hi"], 1)
                rsqrt(L, 0, 2)
                rest_part(L, 0, 3 * KT * DH, *head_w)
                for n in range(3, LNG):
                    rsqrt(L, 0, n)
                hold(pool, S["bv_in"], L * 16 + 16, S["passed_pool"])
                pool.tensor_scalar(bv_rows[:], bv_rows[:], W_SCALE, None, ALU.mult).then_inc(S["bv_ready"], 1)
                pool.wait_ge(S["ob_in"], L * 32 + 16)
                pool.wait_ge(S["y_ready"], L * 2 * TILES + TILES)
                for t in range(TILES):
                    ins = pool.tensor_tensor(g[:, t, :], g[:, t, :], out_bias[:], ALU.add)
                ins.then_inc(S["ob_added"], 1)
                pool.wait_ge(S["ob_added"], L * 2 + 1)
                pool.sem_inc(S["ob_free"], 1)
                with pool.Fori(0, HEADS - 1) as H:
                    head(L, H, H + 1, 3 * KT * DH, *head_w)
                head(L, HEADS - 1, HEADS, KT * D, *square_w(w_o))
                scale(L, 5, HEADS * 48 + 32, KT * D)
                for n in range(LNG):
                    rsqrt(L, LNG, n)
                    if n == 0:
                        rest_part(L, 5, KT * D, *square_w(w_m1))
                    if n == 2:
                        scale(L, 6, HEADS * 48 + 48, KT * D)
                hold(pool, S["res_ready"], L * 2 * TILES + TILES, S["passed_pool"])
                pool.memset(hT[:, :, :, NODES:PAD], 0.0).then_inc(S["h_zero"], 1)
                rest_part(L, 6, KT * D, *square_w(w_m2))
                pool.wait_ge(S["ob_in"], L * 32 + 32)
                pool.wait_ge(S["y_ready"], L * 2 * TILES + 2 * TILES)
                for t in range(TILES):
                    ins = pool.tensor_tensor(g[:, t, :], g[:, t, :], out_bias[:], ALU.add)
                ins.then_inc(S["ob_added"], 1)
                pool.wait_ge(S["ob_added"], L * 2 + 2)
                pool.sem_inc(S["ob_free"], 1)
            for n in range(LNG):
                rsqrt(LAYERS, 0, n)

        @block.vector
        def _(dve):
            dve.sem_inc(S["res_free"], 2)
            dve.sem_inc(S["o_out"], 2)
            dve.tensor_copy(ident_half[:], ident[:])

            def norm_stats(L, first, n):
                group = L * 2 * LNG + (first * LNG + n + 1)
                for j in range(2):
                    ins = dve.bn_stats(stats[:, j, :], g[:, 2 * n + j, :])
                ins.then_inc(S["stats_ready"], 1)
                hold(dve, S["stats_ready"], group, S["passed_dve"])
                for j in range(2):
                    ins = dve.bn_aggr(mv[:, j, :], stats[:, j, :])
                ins.then_inc(S["mv_ready"], 1)

            def norm_part(L, first, n):
                group = L * 2 * LNG + (first * LNG + n + 1)
                dve.wait_ge(S["mv_ready"], group)
                for j in range(2):
                    tile = L * 2 * TILES + (first * TILES + 2 * n + j + 1)
                    dve.wait_ge(S["norm_mm"], tile)
                    dve.scalar_tensor_tensor(y[:, 2 * (n % 2) + j, :], g[:, 2 * n + j, :], mv[:, j, 0:1],
                                             bank[j][:], ALU.subtract, ALU.mult).then_inc(S["y_part"], 1)

            def norm_finish(L, first, n):
                group = L * 2 * LNG + (first * LNG + n + 1)
                dve.wait_ge(S["rstd_ready"], group)
                for j in range(2):
                    tile = L * 2 * TILES + (first * TILES + 2 * n + j + 1)
                    dve.wait_ge(S["y_part"], tile)
                    slot = y[:, 2 * (n % 2) + j, :]
                    dve.scalar_tensor_tensor(slot, slot, rstd[:, j:j + 1], bank[2 + j][:], ALU.mult, ALU.add
                                             ).then_inc(S["y_ready"], 1)

            def norm_back(L, first, t, b):
                dve.wait_ge(S["y_hi"], L * 2 * TILES + (first * TILES + t + 1))
                dve.tensor_tensor(yT[:, 1, :, t * P:(t + 1) * P], bank[b][:].rearrange("p (k n) -> p k n", k=KT),
                                  yT[:, 0, :, t * P:(t + 1) * P], ALU.subtract).then_inc(S["y_lo"], 1)

            def residual(L, first, t):
                n = L * 2 * TILES + (first * TILES + t + 1)
                dve.wait_ge(S["res_ready"], n)
                dve.scalar_tensor_tensor(g[:, t, :], bank[6 + t % 2][:], BACK, g[:, t, :], ALU.mult, ALU.add
                                         ).then_inc(S["res_free"], 1)

            def head_bias(it):
                dve.tensor_copy(qk_bias[:, 0:1], bias_cols[:, bass.ds(it, 1)])
                dve.tensor_copy(qk_bias[:, 1:2], bias_cols[:, bass.ds(it + LAYERS * KT, 1)]
                                ).then_inc(S["bias_ready"], 1)

            def project_rest(it, w):
                for c, (c0, cn) in enumerate(CHUNKS):
                    dve.wait_ge(S["qk_hi"], it * 2 * NCH + ((1 - w) * NCH + c + 1))
                    dve.scalar_tensor_tensor(qk[:, w, 1, c0:c0 + cn], s_bank[c][:, 0:cn], qk_bias[:, w:w + 1],
                                             qk[:, w, 0, c0:c0 + cn], ALU.add, ALU.subtract
                                             ).then_inc(S["qk_lo"], 1)

            def project_v(L, H, it):
                dve.wait_ge(S["bv_ready"], L + 1)
                dve.wait_ge(S["proj_ready"], it * QKV + QKV)
                dve.tensor_tensor(room[:].rearrange("p c n -> p (c n)")[:, 0:TILES * DH]
                                  .rearrange("p (t d) -> p t d", d=DH), v_out.rearrange("p (t d) -> p t d", d=DH),
                                  bv_rows[:, bass.ds(H * DH, DH)].unsqueeze(1).to_broadcast([P, TILES, DH]),
                                  ALU.add).then_inc(S["v_sum"], 1)

            def turned_out_rest(L, t):
                dve.wait_ge(S["o_hi"], L * TILES + (t + 1))
                dve.tensor_tensor(oT[:, t % 4, 1], bank[5][:].rearrange("p (h n) -> p h n", h=HEADS),
                                  oT[:, t % 4, 0], ALU.subtract).then_inc(S["o_lo"], 1)

            def head(L, H, more, next_in, next_n):
                it = L * HEADS + H
                def scores_max(t):
                    if t >= NP:
                        hold(dve, S["e_lo"], it * TILES + (t - NP + 1), S["passed_dve"])
                    hold(dve, S["s_ready"], it * TILES + (t + 1), S["passed_dve"])
                    slot = best[:, t % 2:t % 2 + 1]
                    dve.tensor_tensor_reduce(probs[:, t % NP, 0:NODES], scores, log_count[:, t, :], 1.0, 2 * MASKED,
                                             ALU.add, ALU.max, slot).then_inc(S["best_ready"], 1)
                    dve.wait_ge(S["best_ready"], it * TILES + (t + 1))
                    dve.tensor_scalar(shift[:, t % 2:t % 2 + 1], slot, -SCORE, MAX_SHIFT, ALU.mult, ALU.min
                                      ).then_inc(S["shift_ready"], 1)

                def inverse_sum(t):
                    dve.wait_ge(S["exp_ready"], it * TILES + (t + 1))
                    slot = total[:, t % NP:t % NP + 1]
                    dve.tensor_scalar(slot, slot, LEAST_SUM, None, ALU.max).then_inc(S["recip_ready"], 1)
                    dve.wait_ge(S["recip_ready"], it * TILES + (t + 1))
                    dve.reciprocal(inverse[:, t % (2 * NP):t % (2 * NP) + 1], slot).then_inc(S["inv_ready"], 1)

                def turned_rest(t):
                    dve.wait_ge(S["p_turned"], it * 3 * TILES + (3 * t + 3))
                    dve.tensor_copy(pT_flat[:, t % 2, FULL * P:], turned[:, FULL * P:]).then_inc(S["p_lo"], 1)

                def out(t):
                    dve.wait_ge(S["inv_ready"], it * TILES + (t + 1))
                    dve.wait_ge(S["o_ready"], it * TILES + (t + 1))
                    dve.tensor_scalar(attended[:, t, bass.ds(H * DH, DH)], o_bank[t % 2][:, 0:DH],
                                      inverse[:, t % (2 * NP):t % (2 * NP) + 1], None, ALU.mult
                                      ).then_inc(S["o_out"], 1)

                for i in range(TILES + LAG):
                    if i < TILES:
                        scores_max(i)
                    if i == len(V_SETS) - 1:
                        project_v(L, H, it)
                    if i == 1:
                        dve.wait_ge(S["raw_in"], L * RAW_IN + next_in)
                        dve.tensor_scalar(raw[:, 0:next_n], raw[:, 0:next_n], W_SCALE, None, ALU.mult
                                          ).then_inc(S["w_scaled"], 1)
                    if 1 <= i <= TILES:
                        inverse_sum(i - 1)
                    if more and i == TILES:
                        head_bias(it + 1)
                        project_rest(it + 1, 1)
                    if more and i == TILES + 1:
                        project_rest(it + 1, 0)
                    t = i - LAG
                    if t >= 0:
                        turned_rest(t)
                    if t >= 1:
                        out(t - 1)
                if not more:
                    turned_out_rest(L, 0)
                out(TILES - 1)

            for n in range(LNG + 1):
                if n < LNG:
                    norm_stats(0, 0, n)
                    norm_part(0, 0, n)
                    norm_finish(0, 0, n)
                if n:
                    norm_back(0, 0, 2 * n - 2, 4)
                    norm_back(0, 0, 2 * n - 1, 5)
            with dve.Fori(0, LAYERS) as L:
                dve.tensor_copy(hidden_bias[:], bias_cols[:, bass.ds(L * KT + 2 * LAYERS * KT, KT)]
                                ).then_inc(S["bias_ready"], 1)
                dve.memset(qk[:, :, :, NODES:PAD], 0.0)
                dve.memset(parts[:, :, :, NODES:PAD], 0.0)
                head_bias(L * HEADS)
                dve.wait_ge(S["bias_ready"], L * (HEADS + 1) + 2)
                project_rest(L * HEADS, 1)
                project_rest(L * HEADS, 0)
                with dve.Fori(0, HEADS - 1) as H:
                    head(L, H, True, H * 48 + 96, 3 * KT * DH)
                head(L, HEADS - 1, False, HEADS * 48 + 16, KT * D)

                dve.wait_ge(S["ob_added"], L * 2 + 1)
                turned_out_rest(L, 1)
                for n in range(LNG + 1):
                    if n < LNG:
                        residual(L, 0, 2 * n)
                    if n > 1:
                        norm_back(L, 1, 2 * n - 3, 4)
                    if n < LNG:
                        residual(L, 0, 2 * n + 1)
                    if n < LNG - 1:
                        turned_out_rest(L, 2 * n + 2)
                    if n < LNG:
                        dve.wait_ge(S["res_free"], L * 2 * TILES + (2 * n + 4))
                        norm_stats(L, 1, n)
                    if n:
                        norm_back(L, 1, 2 * n - 2, 4)
                    if n < LNG - 1:
                        turned_out_rest(L, 2 * n + 3)
                    if n < LNG:
                        norm_part(L, 1, n)
                        norm_finish(L, 1, n)
                norm_back(L, 1, TILES - 1, 4)
                dve.wait_ge(S["h_zero"], L + 1)
                for n in range(KT * NCH + 1):
                    if n < KT * NCH:
                        f, (c0, cn) = n // NCH, CHUNKS[n % NCH]
                        if n >= 3:
                            dve.wait_ge(S["h_ready"], L * KT * NCH + (n - 2))
                        dve.wait_ge(S["mlp_ready"], L * KT * NCH + (n + 1))
                        dve.tensor_scalar(room[:, n % 3, 0:cn], h_bank[n % 4][:, 0:cn], hidden_bias[:, f:f + 1], 0.0,
                                          ALU.add, ALU.max).then_inc(S["hidden"], 1)
                    if n:
                        f, (c0, cn) = (n - 1) // NCH, CHUNKS[(n - 1) % NCH]
                        dve.wait_ge(S["h_hi"], L * KT * NCH + n)
                        dve.tensor_tensor(hT[:, 1, f, c0:c0 + cn], room[:, (n - 1) % 3, 0:cn],
                                          hT[:, 0, f, c0:c0 + cn], ALU.subtract).then_inc(S["h_ready"], 1)
                dve.wait_ge(S["ob_added"], L * 2 + 2)
                for n in range(LNG + 1):
                    if n < LNG:
                        residual(L, 1, 2 * n)
                        residual(L, 1, 2 * n + 1)
                        dve.wait_ge(S["res_free"], L * 2 * TILES + (TILES + 2 * n + 4))
                        norm_stats(L + 1, 0, n)
                        norm_part(L + 1, 0, n)
                        norm_finish(L + 1, 0, n)
                    if n:
                        norm_back(L + 1, 0, 2 * n - 2, 4)
                        norm_back(L + 1, 0, 2 * n - 1, 5)

        @block.scalar
        def _(act):
            def norm_hi(L, first, t, b):
                act.wait_ge(S["y_turned"], L * 2 * TILES + (first * TILES + t + 1))
                act.activation(yT[:, 0, :, t * P:(t + 1) * P], bank[b][:].rearrange("p (k n) -> p k n", k=KT),
                               ACT.Copy).then_inc(S["y_hi"], 1)

            def project_hi(it, w):
                for c, (c0, cn) in enumerate(CHUNKS):
                    act.wait_ge(S["proj_ready"], it * QKV + ((1 - w) * NCH + c + 1))
                    act.activation(qk[:, w, 0, c0:c0 + cn], s_bank[c][:, 0:cn], ACT.Identity,
                                   bias=qk_bias[:, w:w + 1]).then_inc(S["qk_hi"], 1)

            def project_v_hi(it):
                act.wait_ge(S["v_sum"], it + 1)
                act.activation(v[:, 0].rearrange("p t d -> p (t d)"),
                               room[:].rearrange("p c n -> p (c n)")[:, 0:TILES * DH], ACT.Copy
                               ).then_inc(S["v_hi"], 1)

            def weights_hi(L, use, n, hi):
                act.wait_ge(S["w_scaled"], L * W_USES + (use + 1))
                act.activation(hi, raw[:, 0:n], ACT.Copy).then_inc(S["w_hi"], 1)

            def head(L, H, more, next_w):
                it = L * HEADS + H

                def turned_hi(t):
                    act.wait_ge(S["p_turned"], it * 3 * TILES + (3 * t + 1))
                    act.activation(pT_flat[:, t % 2, 0:FULL * P], turned[:, 0:FULL * P], ACT.Copy
                                   ).then_inc(S["p_hi"], 1)

                for i in range(TILES + LAG):
                    t = i - LAG
                    if 0 <= t < TILES - LAG:
                        turned_hi(t)
                    if i < TILES:
                        act.wait_ge(S["shift_ready"], it * TILES + (i + 1))
                        act.activation(probs[:, i % NP, 0:NODES], probs[:, i % NP, 0:NODES], ACT.Exp,
                                       bias=shift[:, i % 2:i % 2 + 1], scale=SCORE,
                                       accum_out=total[:, i % NP:i % NP + 1]).then_inc(S["exp_ready"], 1)
                        if i >= NP:
                            act.wait_ge(S["p_turned"], it * 3 * TILES + 3 * (i - NP + 1))
                        if i == len(V_SETS) - 1:
                            project_v_hi(it)
                        act.wait_ge(S["exp_ready"], it * TILES + (i + 1))
                        act.activation(parts[:, i % NP, 0, 0:NODES], probs[:, i % NP, 0:NODES], ACT.Copy
                                       ).then_inc(S["e_hi"], 1)
                    if more and i == TILES:
                        act.wait_ge(S["bias_ready"], it + L + 3)
                        project_hi(it + 1, 1)
                    if more and i == TILES + 1:
                        project_hi(it + 1, 0)
                    if t >= TILES - LAG:
                        turned_hi(t)
                    if i == 3:
                        weights_hi(L, H + 1, *next_w)

            def turned_out_hi(L, t):
                act.wait_ge(S["o_turned"], L * TILES + (t + 1))
                act.activation(oT[:, t % 4, 0], bank[5][:].rearrange("p (h n) -> p h n", h=HEADS), ACT.Copy
                               ).then_inc(S["o_hi"], 1)

            for t in range(TILES):
                norm_hi(0, 0, t, 4 + t % 2)
            with act.Fori(0, LAYERS) as L:
                act.wait_ge(S["bias_ready"], L * (HEADS + 1) + 2)
                project_hi(L * HEADS, 1)
                project_hi(L * HEADS, 0)
                with act.Fori(0, HEADS - 1) as H:
                    head(L, H, True, (3 * KT * DH, head_w[0]))
                head(L, HEADS - 1, False, (KT * D, square_w(w_o)[0]))
                turned_out_hi(L, 0)
                turned_out_hi(L, 1)
                weights_hi(L, 5, KT * D, square_w(w_m1)[0])
                for n in range(LNG + 1):
                    if n > 1:
                        norm_hi(L, 1, 2 * n - 3, 4)
                    if n < LNG - 1:
                        turned_out_hi(L, 2 * n + 2)
                    if n:
                        norm_hi(L, 1, 2 * n - 2, 4)
                    if n < LNG - 1:
                        turned_out_hi(L, 2 * n + 3)
                norm_hi(L, 1, TILES - 1, 4)
                weights_hi(L, 6, KT * D, square_w(w_m2)[0])
                for n in range(KT * NCH):
                    f, (c0, cn) = n // NCH, CHUNKS[n % NCH]
                    act.wait_ge(S["hidden"], L * KT * NCH + (n + 1))
                    act.activation(hT[:, 0, f, c0:c0 + cn], room[:, n % 3, 0:cn], ACT.Copy
                                   ).then_inc(S["h_hi"], 1)
                for t in range(TILES):
                    norm_hi(L + 1, 0, t, 4 + t % 2)

        @block.tensor
        def _(pe):
            def norm_weights(L, first, t):
                if t >= 2:
                    hold(pe, S["y_ready"], L * 2 * TILES + (first * TILES + t - 1), S["passed_pe"])
                for m in range(2):
                    ins = pe.matmul(bank[2 * m + t % 2][:], cond_stack[:, t * P:(t + 1) * P],
                                    norm_stack[:, bass.ds(L * MATS + (2 * first + m), 1), :]
                                    .rearrange("c a d -> c (a d)"), start=True, stop=True)
                ins.then_inc(S["norm_mm"], 1)

            def norm_turn(L, first, t, start=False):
                n = L * 2 * TILES + (first * TILES + t)
                pe.wait_ge(S["y_ready"], n + 1)
                if first:
                    pe.wait_ge(S["y_lo"], n)
                elif not start or t >= 2:
                    pe.wait_ge(S["y_lo"], n - 1)
                out = bank[4 if first else 4 + t % 2]
                for k in range(KT):
                    ins = pe.transpose(out[:, k * P:(k + 1) * P], y[:, t % 4, k * P:(k + 1) * P], ident[:])
                ins.then_inc(S["y_turned"], 1)

            def project(L, H, it, w):
                if w:
                    pe.wait_ge(S["w_ready"], L * W_USES + (H + 2))
                for c, (c0, cn) in enumerate(CHUNKS):
                    if w and isinstance(H, int) and H == 0:
                        pe.wait_ge(S["y_lo"], L * 2 * TILES + min(4 * c + 4, TILES))
                    if not w:
                        pe.wait_ge(S["qk_lo"], it * 2 * NCH + (c + 1))
                    elif not (isinstance(H, int) and H == 0):
                        pe.wait_ge(S["best_ready"], it * TILES)
                    split_matmuls(pe, s_bank[c][:, 0:cn], lambda a, k: w_qkv[:, a, w, k, :],
                                  lambda b, k: yT[:, b, k, c0:c0 + cn], KT).then_inc(S["proj_ready"], 1)

            def project_v(c):
                for j, t in enumerate(V_SETS[c]):
                    ins = split_matmuls(pe, t_bank[c][:, j * DH:(j + 1) * DH],
                                        lambda a, k: yT[:, a, k, t * P:(t + 1) * P],
                                        lambda b, k: w_qkv[:, b, 2, k, :], KT)
                ins.then_inc(S["proj_ready"], 1)

            def turn_out(L, t):
                if t:
                    pe.wait_ge(S["o_lo"], L * TILES + t)
                else:
                    pe.wait_ge(S["p_lo"], L * HEADS * TILES + HEADS * TILES)
                for h in range(HEADS):
                    ins = pe.transpose(bank[5][:, h * P:(h + 1) * P], attended[:, t, h * DH:(h + 1) * DH],
                                       ident[:])
                ins.then_inc(S["o_turned"], 1)

            def head(L, H, more):
                it = L * HEADS + H

                def score(t):
                    if t:
                        pe.wait_ge(S["best_ready"], it * TILES + t)
                    else:
                        pe.wait_ge(S["qk_lo"], it * 2 * NCH + 2 * NCH)
                    for c, (c0, cn) in enumerate(CHUNKS):
                        ins = split_matmuls(pe, s_bank[c][:, 0:cn], lambda a, k: qk[:, 0, a, t * P:(t + 1) * P],
                                            lambda b, k: qk[:, 1, b, c0:c0 + cn], 1)
                    ins.then_inc(S["s_ready"], 1)

                def turn(t):
                    pe.wait_ge(S["e_lo"], it * TILES + (t + 1))
                    for c in range(3):
                        if t == 0:
                            pe.wait_ge(S["v_sum"], it + 1)
                        elif c == 0:
                            pe.wait_ge(S["p_hi"], it * TILES + t)
                        elif c == 1:
                            pe.wait_ge(S["p_lo"], it * TILES + t)
                        for j in range(c * FULL, min(c * FULL + FULL, 2 * TILES)):
                            b = j % TILES
                            ins = pe.transpose(turned[:, j * P:(j + 1) * P],
                                               parts[:, t % NP, j // TILES, b * P:(b + 1) * P], ident_half[:])
                        ins.then_inc(S["p_turned"], 1)

                def values(t):
                    pe.wait_ge(S["p_hi"], it * TILES + (t + 1))
                    pe.wait_ge(S["p_lo"], it * TILES + (t + 1))
                    if t == 0:
                        pe.wait_ge(S["v_lo"], it + 1)
                    pe.wait_ge(S["o_out"], it * TILES + (t + 1))
                    split_matmuls(pe, o_bank[t % 2][:, 0:DH], lambda a, k: pT[:, t % 2, a, k, :],
                                  lambda b, k: v[:, b, k, :], TILES).then_inc(S["o_ready"], 1)

                for i in range(TILES + LAG):
                    if i < TILES:
                        score(i)
                    if i < len(V_SETS):
                        project_v(i)
                    if more and i == TILES:
                        project(L, H + 1, it + 1, 1)
                    if more and i == TILES + 1:
                        project(L, H + 1, it + 1, 0)
                    t = i - LAG
                    if t >= 0:
                        turn(t)
                    if t >= 1:
                        values(t - 1)
                if not more:
                    turn_out(L, 0)
                values(TILES - 1)
                if not more:
                    pe.wait_ge(S["o_out"], it * TILES + (TILES + 2))

            def hidden_tile(L, n):
                f, (c0, cn) = n // NCH, CHUNKS[n % NCH]
                if n == 0:
                    pe.wait_ge(S["w_ready"], L * W_USES + 7)
                if n < NCH:
                    pe.wait_ge(S["y_lo"], L * 2 * TILES + (TILES + min(4 * n + 4, TILES)))
                if n < 2:
                    pe.wait_ge(S["res_free"], L * 2 * TILES + (TILES + n + 1))
                if n >= 4:
                    pe.wait_ge(S["hidden"], L * KT * NCH + (n - 3))
                split_matmuls(pe, h_bank[n % 4][:, 0:cn], lambda a, k: w_m1[:, a, k, f * P:(f + 1) * P],
                              lambda b, k: yT[:, b, k, c0:c0 + cn], KT).then_inc(S["mlp_ready"], 1)

            for n in range(LNG + 1):
                if n < LNG:
                    norm_weights(0, 0, 2 * n)
                    norm_weights(0, 0, 2 * n + 1)
                if n:
                    norm_turn(0, 0, 2 * n - 2, start=True)
                    norm_turn(0, 0, 2 * n - 1, start=True)
            with pe.Fori(0, LAYERS) as L:
                project(L, 0, L * HEADS, 1)
                project(L, 0, L * HEADS, 0)
                with pe.Fori(0, HEADS - 1) as H:
                    head(L, H, True)
                head(L, HEADS - 1, False)

                turn_out(L, 1)
                pe.wait_ge(S["w_ready"], L * W_USES + 6)
                def output(t):
                    pe.wait_ge(S["o_lo"], L * TILES + (t + 1))
                    pe.wait_ge(S["res_free"], L * 2 * TILES + (t + 1))
                    split_matmuls(pe, bank[6 + t % 2][:], lambda a, k: oT[:, t % 4, a, k, :],
                                  lambda b, k: w_o[:, b, k, :], HEADS).then_inc(S["res_ready"], 1)

                for n in range(LNG + 1):
                    if n < LNG:
                        output(2 * n)
                    else:
                        hidden_tile(L, 0)
                    if n > 1:
                        norm_turn(L, 1, 2 * n - 3)
                    if n < LNG:
                        output(2 * n + 1)
                    if n < LNG - 1:
                        turn_out(L, 2 * n + 2)
                    if n < LNG:
                        norm_weights(L, 1, 2 * n)
                        norm_weights(L, 1, 2 * n + 1)
                    if n:
                        norm_turn(L, 1, 2 * n - 2)
                    if n < LNG - 1:
                        turn_out(L, 2 * n + 3)
                hidden_tile(L, 1)
                norm_turn(L, 1, TILES - 1)
                for n in range(2, KT * NCH):
                    hidden_tile(L, n)
                pe.wait_ge(S["w_ready"], L * W_USES + 8)
                for n in range(LNG + 1):
                    if n < LNG:
                        for j in range(2):
                            t = 2 * n + j
                            pe.wait_ge(S["res_free"], L * 2 * TILES + (TILES + t + 1))
                            if t % 4 == 0:
                                pe.wait_ge(S["h_ready"], L * KT * NCH + (KT * NCH - NCH + 1 + t // 4))
                            split_matmuls(pe, bank[6 + j][:], lambda a, k: hT[:, a, k, t * P:(t + 1) * P],
                                          lambda b, k: w_m2[:, b, k, :], KT).then_inc(S["res_ready"], 1)
                        if n == 0:
                            hold(pe, S["hidden"], L * KT * NCH + KT * NCH, S["passed_pe"])
                        norm_weights(L + 1, 0, 2 * n)
                        norm_weights(L + 1, 0, 2 * n + 1)
                    if n:
                        norm_turn(L + 1, 0, 2 * n - 2)
                        norm_turn(L + 1, 0, 2 * n - 1)


def experts(nc, io, g, ident, gu_cols):
    I_T = FF // P
    LNG = TILES // 2
    ROUND = 2
    with ExitStack() as ctx:
        def sb(name, shape, dt=F32):
            return ctx.enter_context(nc.sbuf_tensor("moe_" + name, shape, dt))

        bank = [ctx.enter_context(nc.psum_tensor(f"moe_bank{i}", [P, 512], F32)) for i in range(8)]
        x_in = sb("x", [P, TILES, D])
        xT = sb("xT", [P, 2, KT, PAD], F16)
        actT = sb("actT", [P, 2, I_T, PAD], F16)
        y = sb("y", [P, 4, D])
        raw_gu = sb("raw_gu", [P, 2, 2, KT, P])
        w_gu = sb("w_gu", [P, ROUND, 2, 2, KT, P], F16)
        raw_down = sb("raw_down", [P, 2, D])
        w_down = sb("w_down", [P, 2, I_T, D], F16)
        sig = sb("sig", [P, 2, 512])
        gated = sb("gated", [P, 2, 512])
        raw_router = sb("raw_router", [P, KT, EXPERTS])
        w_router = sb("w_router", [P, 2, KT, EXPERTS], F16)
        router_b = sb("router_b", [P, EXPERTS])
        down_b = sb("down_b", [EXPERTS, D])
        logits = sb("logits", [P, TILES, EXPERTS])
        top = sb("top", [P, TILES])
        weight = sb("weight", [P, TILES, EXPERTS])
        share = sb("share", [P, TILES, EXPERTS])
        weightT = sb("weightT", [EXPERTS, PAD])
        greater = sb("greater", [P, TILES, EXPERTS, EXPERTS])
        equal = sb("equal", [P, TILES, EXPERTS, EXPERTS])
        before = sb("before", [P, EXPERTS, EXPERTS])
        rank = sb("rank", [P, TILES, EXPERTS])
        whole = sb("whole", [P, TILES])
        stats = sb("stats", [P, TILES, 6])
        mv = sb("mv", [P, TILES, 2])
        rstd = sb("rstd", [P, TILES])
        minus_half = sb("minus_half", [P, TILES])

        names = ("start small_in raw_in_0 raw_in_1 raw_scaled raw_hi w_ready down_in_0 down_in_1 down_scaled down_hi "
                 "down_ready x_step mv_ready rstd_step y_ready y_turned y_hi y_lo "
                 "router_step router_mm route route_exp "
                 "weight_turned bias_mm pair_ready sig_ready gated_ready act_ready act_hi act_lo "
                 "down_mm down_free turned_in out_done passed_pool passed_act")
        S = {n: ctx.enter_context(nc.semaphore("m_" + n)) for n in names.split()}
        x_in_sem = [ctx.enter_context(nc.semaphore(f"m_x_in_{n}")) for n in range(LNG)]
        block = ctx.enter_context(nc.Block())
        PAIRS = I_T * NCH

        @block.sync
        def _(sp):
            sp.wait_ge(S["start"], 1)
            for n in range(LNG):
                full = 2 if n < LNG - 1 else 1
                sp.dma_start(x_in[:, 2 * n:2 * n + full, :], io["x"][2 * n * P:(2 * n + full) * P, :]
                             .rearrange("(t p) d -> p t d", p=P)).then_inc(x_in_sem[n], 16)
            sp.dma_start(x_in[0:LAST, TILES - 1, :], io["x"][(TILES - 1) * P:NODES, :]).then_inc(x_in_sem[-1], 16)
            sp.dma_start(raw_router[:], io["L0_ffn_router_w"].rearrange("(k p) e -> p k e", p=P)
                         ).then_inc(S["small_in"], 16)
            sp.dma_start(router_b[:], io["L0_ffn_router_b"].rearrange("(a e) -> a e", a=1).partition_broadcast(P)
                         .rearrange("p a e -> p (a e)")).then_inc(S["small_in"], 16)
            sp.dma_start(down_b[:], io["L0_ffn_down_proj_bias"]).then_inc(S["small_in"], 16)
            with sp.Fori(0, EXPERTS) as e:
                gate_up = io["L0_ffn_gate_up_proj"][bass.ds(e, 1), :, :].rearrange("a (k p) n -> p (a k) n", p=P)
                down = io["L0_ffn_down_proj"][bass.ds(e, 1), :, :].rearrange("a (i p) n -> p (a i) n", p=P)
                for i in range(I_T + 1):
                    if i < I_T:
                        sp.wait_ge(S["w_ready"], e * I_T + (i + 1))
                        for u in range(2):
                            sp.dma_start(raw_gu[:, i % 2, u], gate_up[:, :, u * FF + i * P:u * FF + (i + 1) * P]
                                         ).then_inc(S[f"raw_in_{i % 2}"], 16)
                    if i:
                        sp.wait_ge(S["down_ready"], e * I_T + i)
                        sp.dma_start(raw_down[:, (i - 1) % 2, :], down[:, i - 1, :]
                                     ).then_inc(S[f"down_in_{(i - 1) % 2}"], 16)
            for n in range(LNG):
                full = 2 if n < LNG - 1 else 1
                sp.wait_ge(S["down_free"], (EXPERTS + 1) * TILES + 2 * n + full)
                sp.dma_start(io["out"][2 * n * P:(2 * n + full) * P, :].rearrange("(t p) d -> p t d", p=P),
                             g[:, 2 * n:2 * n + full, :]).then_inc(S["out_done"], 16)
            sp.wait_ge(S["down_free"], (EXPERTS + 2) * TILES)
            sp.dma_start(io["out"][(TILES - 1) * P:NODES, :], g[0:LAST, TILES - 1, :]).then_inc(S["out_done"], 16)
            sp.wait_ge(S["out_done"], 16 * (LNG + 1))

        @block.gpsimd
        def _(pool):
            pool.memset(x_in[96:P, TILES - 1, :], 0.0).then_inc(S["start"], 1)
            pool.wait_ge(S["start"], 1)
            pool.memset(minus_half[:], -0.5).then_inc(S["rstd_step"], 1)
            pool.memset(before[:], 1.0).then_inc(S["rstd_step"], 1)
            pool.sem_inc(S["w_ready"], 2)
            pool.sem_inc(S["down_ready"], 2)
            pool.wait_ge(S["rstd_step"], 2)
            pool.affine_select(out=before[:], in_=before[:], compare_op=ALU.is_gt, fill=0.0, base=0,
                               pattern=[[1, EXPERTS], [-1, EXPERTS]], channel_multiplier=0
                               ).then_inc(S["rstd_step"], 1)
            pool.wait_ge(S["rstd_step"], 3)
            for n in range(LNG):
                pool.wait_ge(S["mv_ready"], n + 1)
                slot = rstd[:, 2 * n:2 * n + 2]
                pool.tensor_scalar(slot, mv[:, 2 * n:2 * n + 2, 1], EPS, None, ALU.add).then_inc(S["rstd_step"], 1)
                pool.wait_ge(S["rstd_step"], 2 * n + 4)
                pool.tensor_tensor(slot, slot, minus_half[:, 0:2], ALU.pow).then_inc(S["rstd_step"], 1)

            def flat(x):
                return x.rearrange("p u k c -> p (u k c)")

            with pool.Fori(0, EXPERTS) as e:
                for i in range(I_T + 1):
                    if i < I_T:
                        n = e * I_T + (i + 1)
                        raw = flat(raw_gu[:, i % 2])
                        hold(pool, S[f"raw_in_{i % 2}"], (e * (I_T // 2) + (i // 2 + 1)) * 32, S["passed_pool"])
                        pool.tensor_scalar(raw, raw, W_SCALE, None, ALU.mult).then_inc(S["raw_scaled"], 1)
                        pool.wait_ge(S["raw_hi"], n)
                        pool.tensor_tensor(flat(w_gu[:, i % 2, 1]), raw, flat(w_gu[:, i % 2, 0]), ALU.subtract
                                           ).then_inc(S["w_ready"], 1)
                    if i:
                        j = i - 1
                        hold(pool, S[f"down_in_{j % 2}"], (e * (I_T // 2) + (j // 2 + 1)) * 16, S["passed_pool"])
                        pool.tensor_scalar(raw_down[:, j % 2], raw_down[:, j % 2], W_SCALE, None, ALU.mult
                                           ).then_inc(S["down_scaled"], 1)
                        pool.wait_ge(S["down_hi"], e * I_T + i)
                        pool.tensor_tensor(w_down[:, 1, j], raw_down[:, j % 2], w_down[:, 0, j], ALU.subtract
                                           ).then_inc(S["down_ready"], 1)

        @block.vector
        def _(dve):
            dve.sem_inc(S["down_free"], TILES)
            dve.memset(actT[:, :, :, NODES:PAD], 0.0)

            def normed_rest(t):
                dve.wait_ge(S["y_hi"], t + 1)
                dve.tensor_tensor(xT[:, 1, :, t * P:(t + 1) * P], bank[t % 2][:].rearrange("p (k n) -> p k n", k=KT),
                                  xT[:, 0, :, t * P:(t + 1) * P], ALU.subtract).then_inc(S["y_lo"], 1)

            for n in range(LNG + 1):
                if n < LNG:
                    dve.wait_ge(x_in_sem[n], 16 if n < LNG - 1 else 32)
                    for j in range(2):
                        t = 2 * n + j
                        ins = dve.tensor_tensor(g[:, t, :], g[:, t, :], x_in[:, t, :], ALU.add)
                    ins.then_inc(S["x_step"], 1)
                    dve.wait_ge(S["x_step"], 2 * n + 1)
                    for j in range(2):
                        ins = dve.bn_stats(stats[:, 2 * n + j, :], g[:, 2 * n + j, :])
                    ins.then_inc(S["x_step"], 1)
                    dve.wait_ge(S["x_step"], 2 * n + 2)
                    for j in range(2):
                        ins = dve.bn_aggr(mv[:, 2 * n + j, :], stats[:, 2 * n + j, :])
                    ins.then_inc(S["mv_ready"], 1)
                if n:
                    normed_rest(2 * n - 2)
                    normed_rest(2 * n - 1)
                if n < LNG:
                    dve.wait_ge(S["mv_ready"], n + 1)
                    dve.wait_ge(S["rstd_step"], 2 * n + 5)
                    for j in range(2):
                        t = 2 * n + j
                        dve.tensor_scalar(y[:, t % 4, :], g[:, t, :], mv[:, t, 0:1], rstd[:, t:t + 1], ALU.subtract,
                                          ALU.mult).then_inc(S["y_ready"], 1)
                if n == 0:
                    dve.wait_ge(S["small_in"], 48)
                    dve.tensor_scalar(raw_router[:], raw_router[:], W_SCALE, None, ALU.mult
                                      ).then_inc(S["router_step"], 1)
                    dve.wait_ge(S["router_step"], 1)
                    dve.tensor_copy(w_router[:, 0], raw_router[:]).then_inc(S["router_step"], 1)
                    dve.wait_ge(S["router_step"], 2)
                    dve.tensor_tensor(w_router[:, 1], raw_router[:], w_router[:, 0], ALU.subtract
                                      ).then_inc(S["router_step"], 1)

            def route(ins, at):
                ins.then_inc(S["route"], 1)
                dve.wait_ge(S["route"], at)

            dve.wait_ge(S["router_mm"], 1)
            route(dve.scalar_tensor_tensor(logits[:], bank[6][:, 0:TILES * EXPERTS]
                                           .rearrange("p (t e) -> p t e", t=TILES), 1.0 / W_SCALE,
                                           router_b[:].unsqueeze(1).to_broadcast([P, TILES, EXPERTS]),
                                           ALU.mult, ALU.add), 1)
            route(dve.tensor_reduce(top[:], logits[:], AX.X, ALU.max), 2)
            four = [P, TILES, EXPERTS, EXPERTS]
            other, own = logits[:].unsqueeze(2).to_broadcast(four), logits[:].unsqueeze(3).to_broadcast(four)
            dve.tensor_tensor(greater[:], other, own, ALU.is_gt)
            route(dve.tensor_tensor(equal[:], other, own, ALU.is_equal), 3)
            route(dve.tensor_tensor(equal[:], equal[:], before[:].unsqueeze(1).to_broadcast(four), ALU.mult), 4)
            route(dve.tensor_tensor(equal[:], equal[:], greater[:], ALU.add), 5)
            route(dve.tensor_reduce(rank[:], equal[:], AX.X, ALU.add), 6)
            flat = [P, TILES, EXPERTS]
            route(dve.tensor_tensor(weight[:], logits[:], top[:].unsqueeze(2).to_broadcast(flat), ALU.subtract), 7)
            dve.wait_ge(S["route_exp"], 1)
            route(dve.scalar_tensor_tensor(weight[:], rank[:], float(TOP_K), weight[:], ALU.is_lt, ALU.mult), 8)
            route(dve.tensor_reduce(whole[:], weight[:], AX.X, ALU.add), 9)
            route(dve.reciprocal(whole[:], whole[:]), 10)
            route(dve.tensor_tensor(weight[:], weight[:], whole[:].unsqueeze(2).to_broadcast(flat), ALU.mult), 11)
            dve.tensor_scalar(share[:], weight[:], BACK, None, ALU.mult).then_inc(S["route"], 1)
            dve.wait_ge(S["route"], 12)
            with dve.Fori(0, EXPERTS) as e:
                for m in range(PAIRS + 1):
                    if m < PAIRS:
                        i, (c0, cn) = m // NCH, CHUNKS[m % NCH]
                        n = e * PAIRS + (m + 1)
                        gate, up = bank[m % 3][:, 0:cn], bank[3 + m % 3][:, 0:cn]
                        col = e * (2 * I_T) + i
                        dve.wait_ge(S["sig_ready"], n)
                        if m >= 2:
                            dve.wait_ge(S["act_lo"], e * PAIRS + (m - 1))
                        dve.scalar_tensor_tensor(gated[:, m % 2, 0:cn], gate, gu_cols[:, 1, bass.ds(col, 1)],
                                                 sig[:, m % 2, 0:cn], ALU.add, ALU.mult
                                                 ).then_inc(S["gated_ready"], 1)
                        dve.wait_ge(S["gated_ready"], n)
                        dve.scalar_tensor_tensor(gated[:, m % 2, 0:cn], up,
                                                 gu_cols[:, 2, bass.ds(col + I_T, 1)],
                                                 gated[:, m % 2, 0:cn], ALU.add, ALU.mult
                                                 ).then_inc(S["act_ready"], 1)
                    if m:
                        i, (c0, cn) = (m - 1) // NCH, CHUNKS[(m - 1) % NCH]
                        dve.wait_ge(S["act_hi"], e * PAIRS + m)
                        dve.scalar_tensor_tensor(actT[:, 1, i, c0:c0 + cn], gated[:, (m - 1) % 2, 0:cn],
                                                 1.0 / W_SCALE, actT[:, 0, i, c0:c0 + cn], ALU.mult,
                                                 ALU.subtract).then_inc(S["act_lo"], 1)
                for t in range(TILES):
                    dve.wait_ge(S["down_mm"], e * TILES + (t + 1))
                    dve.scalar_tensor_tensor(g[:, t, :], bank[6 + t % 2][:], share[:, t, bass.ds(e, 1)],
                                             g[:, t, :], ALU.mult, ALU.add).then_inc(S["down_free"], 1)
                dve.wait_ge(S["down_free"], e * TILES + 2 * TILES)
            for c in range(NCH):
                dve.wait_ge(S["weight_turned"], c + 1)
                n = min(4, TILES - 4 * c) * P
                dve.tensor_copy(weightT[:, c * 512:c * 512 + n], bank[c][0:EXPERTS, 0:n]).then_inc(S["turned_in"], 1)
            for t in range(TILES):
                dve.wait_ge(S["bias_mm"], t + 1)
                dve.tensor_tensor(g[:, t, :], bank[6 + t % 2][:], g[:, t, :], ALU.add).then_inc(S["down_free"], 1)

        @block.scalar
        def _(act):
            for t in range(TILES):
                act.wait_ge(S["y_turned"], t + 1)
                act.activation(xT[:, 0, :, t * P:(t + 1) * P], bank[t % 2][:].rearrange("p (k n) -> p k n", k=KT),
                               ACT.Copy).then_inc(S["y_hi"], 1)
            act.wait_ge(S["route"], 7)
            act.activation(weight[:], weight[:], ACT.Exp).then_inc(S["route_exp"], 1)
            def gate_up_hi(e, i):
                act.wait_ge(S["raw_scaled"], e * I_T + (i + 1))
                act.activation(w_gu[:, i % 2, 0].rearrange("p u k c -> p (u k c)"),
                               raw_gu[:, i % 2].rearrange("p u k c -> p (u k c)"), ACT.Copy
                               ).then_inc(S["raw_hi"], 1)

            with act.Fori(0, EXPERTS) as e:
                gate_up_hi(e, 0)
                gate_up_hi(e, 1)
                for m in range(PAIRS + 1):
                    if m < PAIRS:
                        i, (c0, cn) = m // NCH, CHUNKS[m % NCH]
                        hold(act, S["pair_ready"], e * PAIRS + (m + 1), S["passed_act"])
                        act.activation(sig[:, m % 2, 0:cn], bank[m % 3][:, 0:cn], ACT.Sigmoid,
                                       bias=gu_cols[:, 0, bass.ds(e * (2 * I_T) + i, 1)], scale=1.702 / W_SCALE
                                       ).then_inc(S["sig_ready"], 1)
                        if i and i < I_T - 1 and m % NCH == 0:
                            gate_up_hi(e, i + 1)
                        if m % NCH == 1:
                            act.wait_ge(S["down_scaled"], e * I_T + (i + 1))
                            act.activation(w_down[:, 0, i], raw_down[:, i % 2], ACT.Copy).then_inc(S["down_hi"], 1)
                    if m:
                        i, (c0, cn) = (m - 1) // NCH, CHUNKS[(m - 1) % NCH]
                        act.wait_ge(S["act_ready"], e * PAIRS + m)
                        act.activation(actT[:, 0, i, c0:c0 + cn], gated[:, (m - 1) % 2, 0:cn], ACT.Copy,
                                       scale=1.0 / W_SCALE).then_inc(S["act_hi"], 1)

        @block.tensor
        def _(pe):
            for t in range(TILES):
                pe.wait_ge(S["y_ready"], t + 1)
                if t >= 2:
                    pe.wait_ge(S["y_lo"], t - 1)
                for k in range(KT):
                    ins = pe.transpose(bank[t % 2][:, k * P:(k + 1) * P], y[:, t % 4, k * P:(k + 1) * P], ident[:])
                ins.then_inc(S["y_turned"], 1)
            pe.wait_ge(S["y_lo"], TILES)
            pe.wait_ge(S["router_step"], 3)
            for t in range(TILES):
                ins = split_matmuls(pe, bank[6][:, t * EXPERTS:(t + 1) * EXPERTS],
                                    lambda a, k: xT[:, a, k, t * P:(t + 1) * P],
                                    lambda b, k: w_router[:, b, k, :], KT)
            ins.then_inc(S["router_mm"], 1)
            with pe.Fori(0, EXPERTS) as e:
                for m in range(PAIRS):
                    i, (c0, cn) = m // NCH, CHUNKS[m % NCH]
                    if m % NCH == 0:
                        pe.wait_ge(S["w_ready"], e * I_T + (i + 3))
                    if m >= 3:
                        pe.wait_ge(S["act_ready"], e * PAIRS + (m - 2))
                    for u in range(2):
                        ins = split_matmuls(pe, bank[3 * u + m % 3][:, 0:cn],
                                            lambda a, k: w_gu[:, i % 2, a, u, k, :],
                                            lambda b, k: xT[:, b, k, c0:c0 + cn], KT)
                    ins.then_inc(S["pair_ready"], 1)
                pe.wait_ge(S["down_ready"], e * I_T + (I_T + 2))
                for t in range(TILES):
                    if t % 4 == 0:
                        pe.wait_ge(S["act_lo"], e * PAIRS + (PAIRS - NCH + 1 + t // 4))
                    pe.wait_ge(S["down_free"], e * TILES + (TILES + t - 1))
                    split_matmuls(pe, bank[6 + t % 2][:], lambda a, i: actT[:, a, i, t * P:(t + 1) * P],
                                  lambda b, i: w_down[:, b, i, :], I_T).then_inc(S["down_mm"], 1)
            for c in range(NCH):
                for t in range(4 * c, min(4 * c + 4, TILES)):
                    ins = pe.transpose(bank[c][0:EXPERTS, (t % 4) * P:(t % 4 + 1) * P], weight[:, t, :], ident[:])
                ins.then_inc(S["weight_turned"], 1)
            for t in range(TILES):
                pe.wait_ge(S["turned_in"], t // 4 + 1)
                pe.wait_ge(S["down_free"], EXPERTS * TILES + TILES + t - 1)
                pe.matmul(bank[6 + t % 2][:], weightT[:, t * P:(t + 1) * P], down_b[:], start=True, stop=True
                          ).then_inc(S["bias_mm"], 1)




_INS = ["x", "src", "dst", "node_vec1"] + ["L0_gnn_" + n for n in (
    "f_w1", "f_b1", "f_w2", "f_b2", "s1_w", "s1_b", "b1_w", "b1_b", "wq", "bq", "wk", "bk", "wv", "bv", "wo", "bo",
    "s2_w", "s2_b", "b2_w", "b2_b", "m_w1", "m_b1", "m_w2", "m_b2")] + ["L0_ffn_" + n for n in (
        "router_w", "router_b", "gate_up_proj", "gate_up_proj_bias", "down_proj", "down_proj_bias")]


def kernel(**inputs):
    import concourse.bacc as _bacc
    from concourse.bass_utils import run_bass_kernel_spmd as _run

    nc = _bacc.Bacc("TRN2", target_bir_lowering=False, num_devices=1, dynamic_dma_scratch_size=1024)
    arrays, io = {}, {}
    for name in _INS:
        a = np.ascontiguousarray(inputs[name])
        arrays[f"in_{name}"] = a
        io[name] = nc.dram_tensor(f"in_{name}", a.shape, mybir.dt.from_np(a.dtype), kind="ExternalInput").ap()
    io["out"] = nc.dram_tensor("out_x", (NODES, D), F32, kind="ExternalOutput").ap()
    build(nc, io)
    r = _run(nc, [arrays], core_ids=[0])
    return r.results[0]["out_x"]
```
